# Optimizing a Trainium2 kernel written in Bass

```python
import numpy as np
import jax
import jax.numpy as jnp

def _softmax(x, axis=-1):
    return jax.nn.softmax(x, axis=axis)
def _gelu(x):
    return jax.nn.gelu(x, approximate=True)
def _silu(x):
    return jax.nn.silu(x)
def _sigmoid(x):
    return jax.nn.sigmoid(x)
def _layernorm(x, axis=-1, eps=1e-5):
    m = jnp.mean(x, axis=axis, keepdims=True)
    v = jnp.var(x, axis=axis, keepdims=True)
    return (x - m) / jnp.sqrt(v + eps)
def _scatter_add(tgt, idx, src, axis=0):
    return tgt.at[idx].add(src)
def _segment_sum(src, seg, n):
    return jax.ops.segment_sum(src, seg, n)

kernel_name = 'mk_metaformer_d1_conv_nchw128_b10ce7'

def setup_inputs(seed: int = 0):
    np.random.seed(seed)
    _w = jnp.asarray
    def _rec_inputs():
        import jax
        import jax.numpy as jnp
        _gk = jax.random.key(seed)
        x = -0.000929 + 1 * jax.random.normal(jax.random.fold_in(_gk, 1), (2, 128, 64, 64), jnp.float32)
        return x
    x = _rec_inputs()
    def _L0_conv_setup():
        import jax, jax.numpy as jnp
        import numpy as np
        GN_GROUPS = 16
        EPS = 1e-05

        def conv2d(x, w, b=None, padding=0):
            out = jax.lax.conv_general_dilated(x, w, (1, 1), [(padding, padding), (padding, padding)], dimension_numbers=('NCHW', 'OIHW', 'NCHW'))
            if b is not None:
                out = out + b[None, :, None, None]
            return out

        def group_norm(x, gamma, beta):
            B, C, H, W = x.shape
            xg = x.reshape(B, GN_GROUPS, C // GN_GROUPS, H, W)
            m = xg.mean(axis=(2, 3, 4), keepdims=True)
            v = xg.var(axis=(2, 3, 4), keepdims=True)
            xg = (xg - m) * jax.lax.rsqrt(v + EPS)
            return xg.reshape(B, C, H, W) * gamma[None, :, None, None] + beta[None, :, None, None]

        def bilinear_sample(x, py, px):
            B, C, H, W = x.shape
            y0 = jnp.floor(py)
            x0 = jnp.floor(px)
            xf = x.reshape(B, C, H * W)

            def gather(yi, xi):
                valid = (yi >= 0) & (yi <= H - 1) & (xi >= 0) & (xi <= W - 1)
                yc = jnp.clip(yi, 0, H - 1).astype(jnp.int32)
                xc = jnp.clip(xi, 0, W - 1).astype(jnp.int32)
                idx = (yc * W + xc).reshape(B, -1)
                g = jnp.take_along_axis(xf, idx[:, None, :], axis=2)
                g = g.reshape(B, C, *yi.shape[1:])
                return g * valid[:, None].astype(x.dtype)
            wy = (py - y0)[:, None]
            wx = (px - x0)[:, None]
            v00 = gather(y0, x0)
            v01 = gather(y0, x0 + 1)
            v10 = gather(y0 + 1, x0)
            v11 = gather(y0 + 1, x0 + 1)
            return v00 * (1 - wy) * (1 - wx) + v01 * (1 - wy) * wx + v10 * wy * (1 - wx) + v11 * wy * wx

        def deform_conv(x, off_w, off_b, mod_w, mod_b, reg_w, k, pad):
            B, C, H, W = x.shape
            offset = conv2d(x, off_w, off_b, pad)
            mask = 2.0 * jax.nn.sigmoid(conv2d(x, mod_w, mod_b, pad))
            off = offset.reshape(B, k * k, 2, H, W)
            ky, kx = jnp.meshgrid(jnp.arange(k), jnp.arange(k), indexing='ij')
            base_y = (jnp.arange(H) - pad).astype(x.dtype)[None, None, :, None] + ky.reshape(1, -1, 1, 1).astype(x.dtype)
            base_x = (jnp.arange(W) - pad).astype(x.dtype)[None, None, None, :] + kx.reshape(1, -1, 1, 1).astype(x.dtype)
            py = base_y + off[:, :, 0]
            px = base_x + off[:, :, 1]
            sampled = bilinear_sample(x, py, px) * mask[:, None]
            O = reg_w.shape[0]
            return jnp.einsum('bckhw,ock->bohw', sampled, reg_w.reshape(O, C, k * k))

        def branch(x, off_w, off_b, mod_w, mod_b, reg_w, gng, gnb, k, pad):
            y = deform_conv(x, off_w, off_b, mod_w, mod_b, reg_w, k, pad)
            return jax.nn.relu(group_norm(y, gng, gnb))

        def _forward(x, b1_offw, b1_offb, b1_modw, b1_modb, b1_regw, b1_gng, b1_gnb, b2_offw, b2_offb, b2_modw, b2_modb, b2_regw, b2_gng, b2_gnb, b3_offw, b3_offb, b3_modw, b3_modb, b3_regw, b3_gng, b3_gnb, b4_offw, b4_offb, b4_modw, b4_modb, b4_regw, b4_gng, b4_gnb, pool_w, pool_gng, pool_gnb, fuse_w, fuse_gng, fuse_gnb):
            x1 = branch(x, b1_offw, b1_offb, b1_modw, b1_modb, b1_regw, b1_gng, b1_gnb, 1, 0)
            x2 = branch(x, b2_offw, b2_offb, b2_modw, b2_modb, b2_regw, b2_gng, b2_gnb, 1, 0)
            x3 = branch(x, b3_offw, b3_offb, b3_modw, b3_modb, b3_regw, b3_gng, b3_gnb, 3, 1)
            x4 = branch(x, b4_offw, b4_offb, b4_modw, b4_modb, b4_regw, b4_gng, b4_gnb, 7, 3)
            xm = x.mean(axis=(2, 3), keepdims=True)
            x5 = jax.nn.relu(group_norm(conv2d(xm, pool_w), pool_gng, pool_gnb))
            x5 = jnp.broadcast_to(x5, x1.shape)
            cat = jnp.concatenate([x1, x2, x3, x4, x5], axis=1)
            out = jax.nn.relu(group_norm(conv2d(cat, fuse_w), fuse_gng, fuse_gnb))
            return out
        key = jax.random.key(seed)
        keys = iter(jax.random.split(key, 64))
        C, O = (128, 256)
        inp = {}
        inp['x'] = jax.random.normal(next(keys), (2, C, 64, 64), jnp.float32)
        for name, k in [('b1', 1), ('b2', 1), ('b3', 3), ('b4', 7)]:
            inp[f'{name}_offw'] = 0.01 * jax.random.normal(next(keys), (2 * k * k, C, k, k), jnp.float32)
            inp[f'{name}_offb'] = jnp.zeros((2 * k * k,), jnp.float32)
            inp[f'{name}_modw'] = 0.01 * jax.random.normal(next(keys), (k * k, C, k, k), jnp.float32)
            inp[f'{name}_modb'] = jnp.zeros((k * k,), jnp.float32)
            inp[f'{name}_regw'] = jax.random.normal(next(keys), (O, C, k, k), jnp.float32) / np.sqrt(C * k * k)
            inp[f'{name}_gng'] = jnp.ones((O,), jnp.float32)
            inp[f'{name}_gnb'] = jnp.zeros((O,), jnp.float32)
        inp['pool_w'] = jax.random.normal(next(keys), (O, C, 1, 1), jnp.float32) / np.sqrt(C)
        inp['pool_gng'] = jnp.ones((O,), jnp.float32)
        inp['pool_gnb'] = jnp.zeros((O,), jnp.float32)
        inp['fuse_w'] = jax.random.normal(next(keys), (C, 5 * O, 1, 1), jnp.float32) / np.sqrt(5 * O)
        inp['fuse_gng'] = jnp.ones((C,), jnp.float32)
        inp['fuse_gnb'] = jnp.zeros((C,), jnp.float32)
        return inp
    _L0_conv_all = _L0_conv_setup()
    _L0_conv_in = {k: v for k, v in _L0_conv_all.items() if k in ('b1_offw', 'b1_offb', 'b1_modw', 'b1_modb', 'b1_regw', 'b1_gng', 'b1_gnb', 'b2_offw', 'b2_offb', 'b2_modw', 'b2_modb', 'b2_regw', 'b2_gng', 'b2_gnb', 'b3_offw', 'b3_offb', 'b3_modw', 'b3_modb', 'b3_regw', 'b3_gng', 'b3_gnb', 'b4_offw', 'b4_offb', 'b4_modw', 'b4_modb', 'b4_regw', 'b4_gng', 'b4_gnb', 'pool_w', 'pool_gng', 'pool_gnb', 'fuse_w', 'fuse_gng', 'fuse_gnb', )}
    del _L0_conv_all

    def _L0_ffn_setup():
        import jax, jax.numpy as jnp
        import numpy as np
        PADDED_SL = 8192
        TEMPERATURE = 1.0
        SIGMA_POW = 0.25

        def _stu_conv(phi, u, n):
            b, sl, d = u.shape
            sgn = jnp.where(jnp.arange(sl) % 2 == 0, 1.0, -1.0).astype(u.dtype)
            sgn3 = sgn[None, :, None]
            Vf = jnp.fft.rfft(phi, n=n, axis=0)
            Uf_p = jnp.fft.rfft(u, n=n, axis=1)
            Uf_m = jnp.fft.rfft(u * sgn3, n=n, axis=1)
            U_plus = jnp.fft.irfft(Vf[None, :, :, None] * Uf_p[:, :, None, :], n=n, axis=1)[:, :sl]
            U_minus = jnp.fft.irfft(Vf[None, :, :, None] * Uf_m[:, :, None, :], n=n, axis=1)[:, :sl]
            U_minus = U_minus * sgn[None, :, None, None]
            return (U_plus, U_minus)

        def _compute_spectral(u, sigma, phi, Mpp, Mpm):
            U_plus, U_minus = _stu_conv(phi, u, PADDED_SL)
            s = sigma ** SIGMA_POW
            out = jnp.einsum('btkd,k,kde->bte', U_plus, s, Mpp)
            out = out + jnp.einsum('btkd,k,kde->bte', U_minus, s, Mpm)
            return out

        def _compute_ar_u(Mu, u):
            sl = u.shape[1]
            out = jnp.zeros(u.shape[:2] + (Mu.shape[-1],), dtype=u.dtype)
            for i in range(Mu.shape[0]):
                ui = jnp.pad(u, ((0, 0), (i, 0), (0, 0)))[:, :sl]
                out = out + jnp.einsum('btd,de->bte', ui, Mu[i])
            return out

        def _stu(u, sigma, phi, Mu, Mpp, Mpm):
            return _compute_spectral(u, sigma, phi, Mpp, Mpm) + _compute_ar_u(Mu, u)
        key = jax.random.key(seed)
        ks = jax.random.split(key, 8)
        b, sl, d, K, k_u = (2, 4096, 128, 16, 3)
        x = jax.random.normal(ks[0], (b, sl, d), dtype=jnp.float32)
        sigma = jax.random.uniform(ks[1], (K,), dtype=jnp.float32, minval=0.001, maxval=1.0)
        phi = jax.random.normal(ks[2], (sl, K), dtype=jnp.float32) / np.sqrt(sl)
        M_u = jax.random.normal(ks[3], (4, k_u, d, d), dtype=jnp.float32) * 0.02
        M_phi_plus = jax.random.normal(ks[4], (4, K, d, d), dtype=jnp.float32) * 0.02
        M_phi_minus = jax.random.normal(ks[5], (4, K, d, d), dtype=jnp.float32) * 0.02
        log_weights = jnp.ones((4,), dtype=jnp.float32)
        u01 = jax.random.uniform(ks[6], (4,), dtype=jnp.float32, minval=1e-06, maxval=1.0 - 1e-06)
        gumbel = -jnp.log(-jnp.log(u01))
        return {'x': x, 'sigma': sigma, 'phi': phi, 'M_u': M_u, 'M_phi_plus': M_phi_plus, 'M_phi_minus': M_phi_minus, 'log_weights': log_weights, 'gumbel': gumbel}
    _L0_ffn_all = _L0_ffn_setup()
    _L0_ffn_in = {k: v for k, v in _L0_ffn_all.items() if k in ('sigma', 'phi', 'M_u', 'M_phi_plus', 'M_phi_minus', 'log_weights', 'gumbel', )}
    del _L0_ffn_all

    return {
        "x": x,
        "L0_conv_b1_offw": _L0_conv_in["b1_offw"],
        "L0_conv_b1_offb": _L0_conv_in["b1_offb"],
        "L0_conv_b1_modw": _L0_conv_in["b1_modw"],
        "L0_conv_b1_modb": _L0_conv_in["b1_modb"],
        "L0_conv_b1_regw": _L0_conv_in["b1_regw"],
        "L0_conv_b1_gng": _L0_conv_in["b1_gng"],
        "L0_conv_b1_gnb": _L0_conv_in["b1_gnb"],
        "L0_conv_b2_offw": _L0_conv_in["b2_offw"],
        "L0_conv_b2_offb": _L0_conv_in["b2_offb"],
        "L0_conv_b2_modw": _L0_conv_in["b2_modw"],
        "L0_conv_b2_modb": _L0_conv_in["b2_modb"],
        "L0_conv_b2_regw": _L0_conv_in["b2_regw"],
        "L0_conv_b2_gng": _L0_conv_in["b2_gng"],
        "L0_conv_b2_gnb": _L0_conv_in["b2_gnb"],
        "L0_conv_b3_offw": _L0_conv_in["b3_offw"],
        "L0_conv_b3_offb": _L0_conv_in["b3_offb"],
        "L0_conv_b3_modw": _L0_conv_in["b3_modw"],
        "L0_conv_b3_modb": _L0_conv_in["b3_modb"],
        "L0_conv_b3_regw": _L0_conv_in["b3_regw"],
        "L0_conv_b3_gng": _L0_conv_in["b3_gng"],
        "L0_conv_b3_gnb": _L0_conv_in["b3_gnb"],
        "L0_conv_b4_offw": _L0_conv_in["b4_offw"],
        "L0_conv_b4_offb": _L0_conv_in["b4_offb"],
        "L0_conv_b4_modw": _L0_conv_in["b4_modw"],
        "L0_conv_b4_modb": _L0_conv_in["b4_modb"],
        "L0_conv_b4_regw": _L0_conv_in["b4_regw"],
        "L0_conv_b4_gng": _L0_conv_in["b4_gng"],
        "L0_conv_b4_gnb": _L0_conv_in["b4_gnb"],
        "L0_conv_pool_w": _L0_conv_in["pool_w"],
        "L0_conv_pool_gng": _L0_conv_in["pool_gng"],
        "L0_conv_pool_gnb": _L0_conv_in["pool_gnb"],
        "L0_conv_fuse_w": _L0_conv_in["fuse_w"],
        "L0_conv_fuse_gng": _L0_conv_in["fuse_gng"],
        "L0_conv_fuse_gnb": _L0_conv_in["fuse_gnb"],
        "L0_ffn_sigma": _L0_ffn_in["sigma"],
        "L0_ffn_phi": _L0_ffn_in["phi"],
        "L0_ffn_M_u": _L0_ffn_in["M_u"],
        "L0_ffn_M_phi_plus": _L0_ffn_in["M_phi_plus"],
        "L0_ffn_M_phi_minus": _L0_ffn_in["M_phi_minus"],
        "L0_ffn_log_weights": _L0_ffn_in["log_weights"],
        "L0_ffn_gumbel": _L0_ffn_in["gumbel"],
    }

def reference(x, L0_conv_b1_offw, L0_conv_b1_offb, L0_conv_b1_modw, L0_conv_b1_modb, L0_conv_b1_regw, L0_conv_b1_gng, L0_conv_b1_gnb, L0_conv_b2_offw, L0_conv_b2_offb, L0_conv_b2_modw, L0_conv_b2_modb, L0_conv_b2_regw, L0_conv_b2_gng, L0_conv_b2_gnb, L0_conv_b3_offw, L0_conv_b3_offb, L0_conv_b3_modw, L0_conv_b3_modb, L0_conv_b3_regw, L0_conv_b3_gng, L0_conv_b3_gnb, L0_conv_b4_offw, L0_conv_b4_offb, L0_conv_b4_modw, L0_conv_b4_modb, L0_conv_b4_regw, L0_conv_b4_gng, L0_conv_b4_gnb, L0_conv_pool_w, L0_conv_pool_gng, L0_conv_pool_gnb, L0_conv_fuse_w, L0_conv_fuse_gng, L0_conv_fuse_gnb, L0_ffn_sigma, L0_ffn_phi, L0_ffn_M_u, L0_ffn_M_phi_plus, L0_ffn_M_phi_minus, L0_ffn_log_weights, L0_ffn_gumbel):
    import jax
    import jax.numpy as jnp
    def _L0_conv_ref(x, b1_offw, b1_offb, b1_modw, b1_modb, b1_regw, b1_gng, b1_gnb, b2_offw, b2_offb, b2_modw, b2_modb, b2_regw, b2_gng, b2_gnb, b3_offw, b3_offb, b3_modw, b3_modb, b3_regw, b3_gng, b3_gnb, b4_offw, b4_offb, b4_modw, b4_modb, b4_regw, b4_gng, b4_gnb, pool_w, pool_gng, pool_gnb, fuse_w, fuse_gng, fuse_gnb):
        import jax, jax.numpy as jnp
        import numpy as np
        GN_GROUPS = 16
        EPS = 1e-05

        def conv2d(x, w, b=None, padding=0):
            out = jax.lax.conv_general_dilated(x, w, (1, 1), [(padding, padding), (padding, padding)], dimension_numbers=('NCHW', 'OIHW', 'NCHW'))
            if b is not None:
                out = out + b[None, :, None, None]
            return out

        def group_norm(x, gamma, beta):
            B, C, H, W = x.shape
            xg = x.reshape(B, GN_GROUPS, C // GN_GROUPS, H, W)
            m = xg.mean(axis=(2, 3, 4), keepdims=True)
            v = xg.var(axis=(2, 3, 4), keepdims=True)
            xg = (xg - m) * jax.lax.rsqrt(v + EPS)
            return xg.reshape(B, C, H, W) * gamma[None, :, None, None] + beta[None, :, None, None]

        def bilinear_sample(x, py, px):
            B, C, H, W = x.shape
            y0 = jnp.floor(py)
            x0 = jnp.floor(px)
            xf = x.reshape(B, C, H * W)

            def gather(yi, xi):
                valid = (yi >= 0) & (yi <= H - 1) & (xi >= 0) & (xi <= W - 1)
                yc = jnp.clip(yi, 0, H - 1).astype(jnp.int32)
                xc = jnp.clip(xi, 0, W - 1).astype(jnp.int32)
                idx = (yc * W + xc).reshape(B, -1)
                g = jnp.take_along_axis(xf, idx[:, None, :], axis=2)
                g = g.reshape(B, C, *yi.shape[1:])
                return g * valid[:, None].astype(x.dtype)
            wy = (py - y0)[:, None]
            wx = (px - x0)[:, None]
            v00 = gather(y0, x0)
            v01 = gather(y0, x0 + 1)
            v10 = gather(y0 + 1, x0)
            v11 = gather(y0 + 1, x0 + 1)
            return v00 * (1 - wy) * (1 - wx) + v01 * (1 - wy) * wx + v10 * wy * (1 - wx) + v11 * wy * wx

        def deform_conv(x, off_w, off_b, mod_w, mod_b, reg_w, k, pad):
            B, C, H, W = x.shape
            offset = conv2d(x, off_w, off_b, pad)
            mask = 2.0 * jax.nn.sigmoid(conv2d(x, mod_w, mod_b, pad))
            off = offset.reshape(B, k * k, 2, H, W)
            ky, kx = jnp.meshgrid(jnp.arange(k), jnp.arange(k), indexing='ij')
            base_y = (jnp.arange(H) - pad).astype(x.dtype)[None, None, :, None] + ky.reshape(1, -1, 1, 1).astype(x.dtype)
            base_x = (jnp.arange(W) - pad).astype(x.dtype)[None, None, None, :] + kx.reshape(1, -1, 1, 1).astype(x.dtype)
            py = base_y + off[:, :, 0]
            px = base_x + off[:, :, 1]
            sampled = bilinear_sample(x, py, px) * mask[:, None]
            O = reg_w.shape[0]
            return jnp.einsum('bckhw,ock->bohw', sampled, reg_w.reshape(O, C, k * k))

        def branch(x, off_w, off_b, mod_w, mod_b, reg_w, gng, gnb, k, pad):
            y = deform_conv(x, off_w, off_b, mod_w, mod_b, reg_w, k, pad)
            return jax.nn.relu(group_norm(y, gng, gnb))

        def _forward(x, b1_offw, b1_offb, b1_modw, b1_modb, b1_regw, b1_gng, b1_gnb, b2_offw, b2_offb, b2_modw, b2_modb, b2_regw, b2_gng, b2_gnb, b3_offw, b3_offb, b3_modw, b3_modb, b3_regw, b3_gng, b3_gnb, b4_offw, b4_offb, b4_modw, b4_modb, b4_regw, b4_gng, b4_gnb, pool_w, pool_gng, pool_gnb, fuse_w, fuse_gng, fuse_gnb):
            x1 = branch(x, b1_offw, b1_offb, b1_modw, b1_modb, b1_regw, b1_gng, b1_gnb, 1, 0)
            x2 = branch(x, b2_offw, b2_offb, b2_modw, b2_modb, b2_regw, b2_gng, b2_gnb, 1, 0)
            x3 = branch(x, b3_offw, b3_offb, b3_modw, b3_modb, b3_regw, b3_gng, b3_gnb, 3, 1)
            x4 = branch(x, b4_offw, b4_offb, b4_modw, b4_modb, b4_regw, b4_gng, b4_gnb, 7, 3)
            xm = x.mean(axis=(2, 3), keepdims=True)
            x5 = jax.nn.relu(group_norm(conv2d(xm, pool_w), pool_gng, pool_gnb))
            x5 = jnp.broadcast_to(x5, x1.shape)
            cat = jnp.concatenate([x1, x2, x3, x4, x5], axis=1)
            out = jax.nn.relu(group_norm(conv2d(cat, fuse_w), fuse_gng, fuse_gnb))
            return out
        return _forward(x, b1_offw, b1_offb, b1_modw, b1_modb, b1_regw, b1_gng, b1_gnb, b2_offw, b2_offb, b2_modw, b2_modb, b2_regw, b2_gng, b2_gnb, b3_offw, b3_offb, b3_modw, b3_modb, b3_regw, b3_gng, b3_gnb, b4_offw, b4_offb, b4_modw, b4_modb, b4_regw, b4_gng, b4_gnb, pool_w, pool_gng, pool_gnb, fuse_w, fuse_gng, fuse_gnb)

    def _L0_ffn_ref(x, sigma, phi, M_u, M_phi_plus, M_phi_minus, log_weights, gumbel):
        import jax, jax.numpy as jnp
        import numpy as np
        PADDED_SL = 8192
        TEMPERATURE = 1.0
        SIGMA_POW = 0.25

        def _stu_conv(phi, u, n):
            b, sl, d = u.shape
            sgn = jnp.where(jnp.arange(sl) % 2 == 0, 1.0, -1.0).astype(u.dtype)
            sgn3 = sgn[None, :, None]
            Vf = jnp.fft.rfft(phi, n=n, axis=0)
            Uf_p = jnp.fft.rfft(u, n=n, axis=1)
            Uf_m = jnp.fft.rfft(u * sgn3, n=n, axis=1)
            U_plus = jnp.fft.irfft(Vf[None, :, :, None] * Uf_p[:, :, None, :], n=n, axis=1)[:, :sl]
            U_minus = jnp.fft.irfft(Vf[None, :, :, None] * Uf_m[:, :, None, :], n=n, axis=1)[:, :sl]
            U_minus = U_minus * sgn[None, :, None, None]
            return (U_plus, U_minus)

        def _compute_spectral(u, sigma, phi, Mpp, Mpm):
            U_plus, U_minus = _stu_conv(phi, u, PADDED_SL)
            s = sigma ** SIGMA_POW
            out = jnp.einsum('btkd,k,kde->bte', U_plus, s, Mpp)
            out = out + jnp.einsum('btkd,k,kde->bte', U_minus, s, Mpm)
            return out

        def _compute_ar_u(Mu, u):
            sl = u.shape[1]
            out = jnp.zeros(u.shape[:2] + (Mu.shape[-1],), dtype=u.dtype)
            for i in range(Mu.shape[0]):
                ui = jnp.pad(u, ((0, 0), (i, 0), (0, 0)))[:, :sl]
                out = out + jnp.einsum('btd,de->bte', ui, Mu[i])
            return out

        def _stu(u, sigma, phi, Mu, Mpp, Mpm):
            return _compute_spectral(u, sigma, phi, Mpp, Mpm) + _compute_ar_u(Mu, u)
        T = x.shape[1]
        outs = []
        for i, frac in enumerate((1, 2, 4, 8)):
            xi = x[:, :T // frac]
            si = _stu(xi, sigma, phi, M_u[i], M_phi_plus[i], M_phi_minus[i])
            si = jnp.pad(si, ((0, 0), (0, T - si.shape[1]), (0, 0)))
            outs.append(si)
        y_soft = jax.nn.softmax((log_weights + gumbel) / TEMPERATURE)
        y_hard = jax.nn.one_hot(jnp.argmax(y_soft), 4, dtype=y_soft.dtype)
        weights = y_hard - jax.lax.stop_gradient(y_soft) + y_soft
        stacked = jnp.stack(outs, axis=-1)
        return jnp.sum(stacked * weights, axis=-1)

    def _gn(v, G=32, eps=1e-5):
        B_, C_, H_, W_ = v.shape
        g = v.reshape(B_, G, C_ // G, H_, W_)
        m = jnp.mean(g, axis=(2, 3, 4), keepdims=True)
        s = jnp.var(g, axis=(2, 3, 4), keepdims=True)
        return ((g - m) / jnp.sqrt(s + eps)).reshape(v.shape)

    def _ln_c(v, eps=1e-6):
        m = jnp.mean(v, axis=1, keepdims=True)
        s = jnp.var(v, axis=1, keepdims=True)
        return (v - m) / jnp.sqrt(s + eps)

    def _ln_t(v, eps=1e-5):
        m = jnp.mean(v, axis=-1, keepdims=True)
        s = jnp.var(v, axis=-1, keepdims=True)
        return (v - m) / jnp.sqrt(s + eps)

    def _to_tokens(v):
        B_, C_, H_, W_ = v.shape
        return v.reshape(B_, C_, H_ * W_).transpose(0, 2, 1)
    def _from_tokens(t, like):
        B_, C_, H_, W_ = like.shape
        return t.transpose(0, 2, 1).reshape(B_, C_, H_, W_)

    x = x + _L0_conv_ref(_ln_c(x), L0_conv_b1_offw, L0_conv_b1_offb, L0_conv_b1_modw, L0_conv_b1_modb, L0_conv_b1_regw, L0_conv_b1_gng, L0_conv_b1_gnb, L0_conv_b2_offw, L0_conv_b2_offb, L0_conv_b2_modw, L0_conv_b2_modb, L0_conv_b2_regw, L0_conv_b2_gng, L0_conv_b2_gnb, L0_conv_b3_offw, L0_conv_b3_offb, L0_conv_b3_modw, L0_conv_b3_modb, L0_conv_b3_regw, L0_conv_b3_gng, L0_conv_b3_gnb, L0_conv_b4_offw, L0_conv_b4_offb, L0_conv_b4_modw, L0_conv_b4_modb, L0_conv_b4_regw, L0_conv_b4_gng, L0_conv_b4_gnb, L0_conv_pool_w, L0_conv_pool_gng, L0_conv_pool_gnb, L0_conv_fuse_w, L0_conv_fuse_gng, L0_conv_fuse_gnb)
    t = _to_tokens(x)
    t = t + _L0_ffn_ref(_ln_t(t), L0_ffn_sigma, L0_ffn_phi, L0_ffn_M_u, L0_ffn_M_phi_plus, L0_ffn_M_phi_minus, L0_ffn_log_weights, L0_ffn_gumbel)
    x = _from_tokens(t, x)
    return x


_drawn_inputs = setup_inputs


def setup_inputs(seed=0):
    import zlib

    import numpy as np

    out = dict(_drawn_inputs(seed))
    spreads = {'L0_conv_b1_offb': (0.0, 0.464),
     'L0_conv_b1_gng': (1.0, 0.2),
     'L0_conv_b1_gnb': (0.0, 0.297),
     'L0_conv_b2_offb': (0.0, 0.1),
     'L0_conv_b2_gng': (1.0, 0.2),
     'L0_conv_b2_gnb': (0.0, 0.315),
     'L0_conv_b3_offb': (0.0, 0.1),
     'L0_conv_b3_modb': (0.0, 0.8),
     'L0_conv_b3_gng': (1.0, 0.2),
     'L0_conv_b3_gnb': (0.0, 0.325),
     'L0_conv_b4_offb': (0.0, 0.1),
     'L0_conv_b4_modb': (0.0, 0.697),
     'L0_conv_b4_gng': (1.0, 0.2),
     'L0_conv_b4_gnb': (0.0, 0.302),
     'L0_conv_pool_gng': (1.0, 0.2),
     'L0_conv_pool_gnb': (0.0, 0.308),
     'L0_conv_fuse_gng': (1.0, 0.2),
     'L0_conv_fuse_gnb': (0.0, 0.1),
     'L0_ffn_log_weights': (1.0, 0.2)}
    factors = {'L0_conv_b1_modw': 3.646, 'L0_conv_b2_modw': 3.135}
    for name, (base, spread) in spreads.items():
        noise = np.random.default_rng([zlib.crc32(name.encode()), seed]).standard_normal(out[name].shape)
        drawn = base * np.exp(spread * noise) if base else spread * noise
        out[name] = jnp.asarray(drawn.astype(out[name].dtype))
    for name, factor in factors.items():
        out[name] = (out[name] * factor).astype(out[name].dtype)
    return out
```

```python
import concourse.bass as bass
from concourse import mybir
from contextlib import ExitStack

B, C, H, W = 2, 128, 64, 64
HW = H * W
O = 256
TAPS = 49 + 9 + 1 + 1
BRANCHES = ((0, 49), (49, 9), (58, 1), (59, 1))
NBR = len(BRANCHES)
PAD = 3
HP = H + 2 * PAD
TS = H + 3
TROWS = TS * TS
CH = 512
GI = HW // CH
NG = B * GI
RING = 4
KF = 16
HALF = HW // 2
SEG = 4
NFC = 2 * (NBR + 1)
F32 = mybir.dt.float32
I32 = mybir.dt.int32
ALU = mybir.AluOpType
ACT = mybir.ActivationFunctionType
AX = mybir.AxisListType


class Steps:

    def __init__(self, eng, sem, base=0):
        self.eng, self.sem, self.base, self.n = eng, sem, base, 0

    def then(self, ins):
        self.n += 1
        ins.then_inc(self.sem, 1)
        self.eng.wait_ge(self.sem, self.base + self.n)


def flat(ap):
    n = len(ap.shape) - 1
    names = " ".join("abcdef"[:n])
    return ap.rearrange(f"p {names} -> p ({names})")


def stage_normalise(nc, mem, x, table, ident, eps6, xnpad, xsum):
    ctx = ExitStack()
    with ctx:
        sb = lambda name, shape, dt=F32: ctx.enter_context(nc.sbuf_tensor(name, shape, dt))
        sem = lambda name: ctx.enter_context(nc.semaphore(name))
        xg = [sb(f"xg{h}", [C, CH]) for h in range(2)]
        xn = [sb(f"xn{h}", [128, 4, C]) for h in range(2)]
        stats = [sb(f"ln_stats{h}", [128, 4, 6]) for h in range(2)]
        mv = [sb(f"ln_mv{h}", [128, 4, 2]) for h in range(2)]
        sd = [sb(f"ln_sd{h}", [128, 4]) for h in range(2)]
        rs = [sb(f"ln_rs{h}", [128, 4]) for h in range(2)]
        zero = sb("zero", [TS, 2 * 4 * C])
        ps_x = [ctx.enter_context(nc.psum_tensor(f"ps_x{h}", [128, 4, C], F32)) for h in range(2)]
        ps_n = [ctx.enter_context(nc.psum_tensor(f"ps_n{h}", [128, CH], F32)) for h in range(2)]

        zero_set = sem("zero_set")
        border_written = sem("border_written")
        pad_zeroed = sem("pad_zeroed")
        x_loaded = [sem(f"x_loaded{h}") for h in range(2)]
        x_turned = [sem(f"x_turned{h}") for h in range(2)]
        var_ready = [sem(f"var_ready{h}") for h in range(2)]
        sd_ready = [sem(f"sd_ready{h}") for h in range(2)]
        dve_step = sem("ln_dve_step")
        xn_ready = [sem(f"xn_ready{h}") for h in range(2)]
        xn_turned = [sem(f"xn_turned{h}") for h in range(2)]
        xn_copied = [sem(f"xn_copied{h}") for h in range(2)]
        table_written = [sem(f"table_written{h}") for h in range(2)]
        gate = sem("ln_gate")
        WR = 8 * 16
        tab = table.rearrange("(b y x) s -> b y x s", b=B, y=TS)
        tab2 = table.rearrange("(y x) s -> y x s", x=TS)
        block = ctx.enter_context(nc.Block())

        @block.gpsimd
        def _(pool):
            pool.memset(zero[:], 0.0).then_inc(zero_set, 1)
            pool.memset(xnpad[:], 0.0).then_inc(pad_zeroed, 1)

        @block.sync
        def _(sp):
            sp.wait_ge(zero_set, 1)
            for b in range(B):
                for y in (0, TS - 2):
                    sp.dma_start(tab[b, y:y + 2, :, :].rearrange("y x s -> (y x s)").rearrange("(p n) -> p n", p=TS),
                                 zero[:, :]).then_inc(border_written, 16)
                for c in (0, TS - 2):
                    sp.dma_start(tab[b, 2:TS - 2, c:c + 2, :].rearrange("y x s -> y (x s)"), zero[0:TS - 4, :])\
                        .then_inc(border_written, 16)
            for h in range(2):
                sp.sem_inc(table_written[h], WR)
            sp.wait_ge(border_written, 16 * 4 * B)
            with sp.Fori(0, B) as b:
                with sp.Fori(0, GI // 2) as i:
                    k = b * (GI // 2) + i
                    for h in range(2):
                        sp.wait_ge(x_turned[h], k + 1)
                        sp.dma_start(xg[h][:, :], x[bass.ds(b, 1), :, bass.ds(i * (2 * CH) + h * CH, CH)]
                                     .rearrange("b c n -> (b c) n")).then_inc(x_loaded[h], 16)
                    for h in range(2):
                        sp.wait_ge(xn_ready[h], k + 2)
                        for half in range(2):
                            src = xn[h][64 * half:64 * half + 64, :, :]
                            for slot, (dy, dx) in enumerate(((0, 0), (0, 1), (1, 0), (1, 1))):
                                y0 = b * TS + i * 16 + (h * 8 + half + 2 - dy)
                                dst = tab2[bass.ds(y0, 4, step=2), 2 - dx:2 - dx + W, slot * C:(slot + 1) * C]
                                sp.dma_start(dst.rearrange("t x c -> x t c"), src).then_inc(table_written[h], 16)
            for h in range(2):
                sp.wait_ge(table_written[h], WR * (NG // 2 + 1))

        @block.tensor
        def _(pe):
            for h in range(2):
                pe.sem_inc(x_turned[h], 1)
                pe.sem_inc(xn_turned[h], 1)
            with pe.Fori(0, NG // 2) as k:
                for h in range(2):
                    pe.wait_ge(x_loaded[h], 16 * k + 16)
                    pe.wait_ge(xn_ready[h], k + 1)
                    for j in range(4):
                        last = nc.tensor.transpose(ps_x[h][:, j, :], xg[h][:, 128 * j:128 * j + 128], ident[:, :])
                    last.then_inc(x_turned[h], 1)
                for h in range(2):
                    pe.wait_ge(xn_ready[h], k + 2)
                    pe.wait_ge(xn_copied[h], k + 1)
                    for j in range(4):
                        last = nc.tensor.transpose(ps_n[h][:, 128 * j:128 * j + 128], xn[h][:, j, :], ident[:, :])
                    last.then_inc(xn_turned[h], 1)

        @block.vector
        def _(dve):
            for h in range(2):
                dve.sem_inc(xn_ready[h], 1)
            with dve.Fori(0, NG // 2) as k:
                st = Steps(dve, dve_step, k * 4)
                for h in range(2):
                    dve.wait_ge(x_turned[h], k + 2)
                    for j in range(4):
                        last = nc.vector.bn_stats(stats[h][:, j, :], ps_x[h][:, j, :])
                    st.then(last)
                    dve.sem_inc(gate, 1)
                    for j in range(4):
                        last = nc.vector.bn_aggr(mv[h][:, j, :], stats[h][:, j, :])
                    last.then_inc(var_ready[h], 1)
                for h in range(2):
                    dve.wait_ge(sd_ready[h], k + 1)
                    st.then(nc.vector.reciprocal(rs[h][:, :], sd[h][:, :]))
                    dve.wait_ge(table_written[h], k * WR + WR)
                    dve.wait_ge(xn_turned[h], k + 1)
                    for j in range(4):
                        last = nc.vector.tensor_scalar(xn[h][:, j, :], ps_x[h][:, j, :], mv[h][:, j, 0:1],
                                                       rs[h][:, j:j + 1], ALU.subtract, ALU.mult)
                    last.then_inc(xn_ready[h], 1)

        @block.scalar
        def _(act):
            for h in range(2):
                act.sem_inc(xn_copied[h], 1)
            act.wait_ge(pad_zeroed, 1)
            with act.Fori(0, B) as b:
                with act.Fori(0, GI // 2) as i:
                    k = b * (GI // 2) + i
                    for h in range(2):
                        act.wait_ge(var_ready[h], k + 1)
                        nc.scalar.activation(sd[h][:, :], mv[h][:, :, 1], ACT.Sqrt, bias=eps6[:, 0:1])\
                            .then_inc(sd_ready[h], 1)
                    for h in range(2):
                        act.wait_ge(xn_turned[h], k + 2)
                        act.sem_inc(gate, 1)
                        nc.scalar.activation(
                            xnpad[:, bass.ds(b * HP + i * 16 + h * 8 + PAD, 8), PAD:PAD + W],
                            ps_n[h][:, :].rearrange("p (y x) -> p y x", x=W), ACT.Copy).then_inc(xn_copied[h], 1)
            for h in range(2):
                act.wait_ge(xn_copied[h], NG // 2 + 1)

    with ExitStack() as ctx:
        block = ctx.enter_context(nc.Block())

        @block.vector
        def _(dve):
            for b in range(B):
                nc.vector.tensor_reduce(xsum[:, b:b + 1], xnpad[:, b * HP + PAD:b * HP + PAD + H, PAD:PAD + W],
                                        AX.XY, ALU.add)


def stage_offsets(nc, mem, xnpad, w_om, base_om, bias_om, row_off, idx_dram, wts_dram):
    ctx = ExitStack()
    with ctx:
        sb = lambda name, shape, dt=F32: ctx.enter_context(nc.sbuf_tensor(name, shape, dt))
        sem = lambda name: ctx.enter_context(nc.semaphore(name))
        wom = sb("wom", [C, 49, 3, TAPS])
        base = sb("base", [128, 3, TAPS])
        biasb = sb("biasb", [128, 3, TAPS])
        rowt = sb("rowt", [128, HW // 128])
        imgo = sb("imgo", [128, B])
        win = [sb(f"win{h}", [C, 7, 8, W]) for h in range(2)]
        P = sb("P", [128, 3, TAPS])
        sg = sb("sg", [128, TAPS])
        pi = sb("pi", [128, 2, TAPS], I32)
        fl = sb("fl", [128, 2, TAPS])
        gt = sb("gt", [128, 2, TAPS])
        fr = sb("fr", [128, 2, TAPS])
        rowf = sb("rowf", [128, TAPS])
        a = sb("a", [128, 2, TAPS])
        idx = sb("idx", [128, TAPS, 4], I32)
        wts = sb("wts", [128, TAPS, 4, 2, 2])
        ps = [ctx.enter_context(nc.psum_tensor(f"ps_om{h}", [128, 3, 128], F32)) for h in range(2)]

        params = sem("om_params")
        base_ready = sem("base_ready")
        copied = [sem(f"win_copied{h}") for h in range(2)]
        copied_a = [sem(f"win_copied_a{h}") for h in range(2)]
        conv_done = [sem(f"om_done{h}") for h in range(2)]
        om_read = [sem(f"om_read{h}") for h in range(2)]
        mod_ready = sem("mod_ready")
        sig_ready = sem("sig_ready")
        sig_used = sem("sig_used")
        step = sem("om_step")
        imgset = sem("imgset")
        group_ready = sem("om_group_ready")
        stored = sem("om_stored")
        gate = sem("om_gate")
        block = ctx.enter_context(nc.Block())
        taps = sorted(range(49), key=lambda t: (t != 24, t))

        def columns(t):
            ky, kx = divmod(t, 7)
            if t == 24:
                return TAPS
            return 58 if 2 <= ky <= 4 and 2 <= kx <= 4 else 49

        @block.sync
        def _(sp):
            sp.dma_start(wom[:], w_om).then_inc(params, 16)
            sp.dma_start(base[:], base_om).then_inc(params, 16)
            sp.dma_start(biasb[:], bias_om.rearrange("(a k) t -> a k t", a=1).to_broadcast([128, 3, TAPS])).then_inc(params, 16)
            sp.dma_start(rowt[:], row_off).then_inc(params, 16)
            sp.sem_inc(stored, 32)
            with sp.Fori(0, NG) as g:
                sp.wait_ge(group_ready, g + 1)
                sp.dma_start(idx_dram[bass.ds(g, 1), :, :].rearrange("g p n -> (g p) n"),
                             flat(idx[:])).then_inc(stored, 16)
                sp.dma_start(wts_dram[bass.ds(g, 1), :, :].rearrange("g p n -> (g p) n"),
                             flat(wts[:])).then_inc(stored, 16)
            sp.wait_ge(stored, 32 * (NG + 1))

        @block.gpsimd
        def _(pool):
            for b in range(B):
                pool.memset(imgo[:, b:b + 1], float(b * TROWS)).then_inc(imgset, 1)
            with pool.Fori(0, B) as b:
                with pool.Fori(0, GI) as g:
                    for j in range(4):
                        h = j % 2
                        pool.wait_ge(conv_done[h], (b * GI + g) * 2 + (j // 2 + 1))
                        pool.sem_inc(gate, 1)
                        for kx in range(0, 3):
                            last = nc.gpsimd.tensor_copy(
                                win[h][:, kx, :, :], xnpad[:, bass.ds(b * HP + g * 8 + 2 * j, 8), kx:kx + W])
                        last.then_inc(copied[h], 1)

        @block.scalar
        def _(act):
            with act.Fori(0, B) as b:
                with act.Fori(0, GI) as g:
                    for j in range(4):
                        h = j % 2
                        m = (b * GI + g) * 4 + j
                        act.wait_ge(conv_done[h], (b * GI + g) * 2 + (j // 2 + 1))
                        act.sem_inc(gate, 1)
                        for kx in range(3, 7):
                            last = nc.scalar.activation(
                                win[h][:, kx, :, :], xnpad[:, bass.ds(b * HP + g * 8 + 2 * j, 8), kx:kx + W], ACT.Copy)
                        last.then_inc(copied_a[h], 1)
                        act.wait_ge(mod_ready, m + 1)
                        act.wait_ge(sig_used, m + 1)
                        nc.scalar.activation(sg[:, :], P[:, 2, :], ACT.Sigmoid).then_inc(sig_ready, 1)

        @block.tensor
        def _(pe):
            for h in range(2):
                pe.sem_inc(conv_done[h], 1)
            pe.wait_ge(params, 64)
            with pe.Fori(0, NG) as g:
                for j in range(4):
                    h = j % 2
                    n = g * 2 + j // 2
                    pe.wait_ge(copied[h], n + 1)
                    pe.wait_ge(copied_a[h], n + 1)
                    pe.wait_ge(om_read[h], n + 1)
                    for t in taps:
                        ky, kx = divmod(t, 7)
                        m = columns(t)
                        last = nc.tensor.matmul(ps[h][:, :, 0:m], win[h][:, kx, ky:ky + 2, :].rearrange("c y x -> c (y x)"), wom[:, t, :, 0:m],
                                                start=(t == 24), stop=(t == 48), skip_group_check=True)
                    last.then_inc(conv_done[h], 1)

        @block.vector
        def _(dve):
            for h in range(2):
                dve.sem_inc(om_read[h], 1)
            dve.sem_inc(sig_used, 1)
            dve.wait_ge(params, 64)
            dve.wait_ge(imgset, B)
            nc.vector.tensor_tensor(base[:], base[:], biasb[:], ALU.add).then_inc(base_ready, 1)
            dve.wait_ge(base_ready, 1)
            PER = 14
            with dve.Fori(0, B) as b:
                with dve.Fori(0, GI) as g:
                    grp = b * GI + g
                    for j in range(4):
                        h = j % 2
                        st = Steps(dve, step, (grp * 4 + j) * PER)
                        dve.wait_ge(conv_done[h], grp * 2 + (j // 2 + 2))
                        st.then(nc.vector.tensor_tensor(P[:], ps[h][:, :, 0:TAPS], base[:], ALU.add))
                        dve.sem_inc(om_read[h], 1)
                        dve.sem_inc(mod_ready, 1)
                        st.then(nc.vector.tensor_scalar(P[:, 0, :], P[:, 0, :], rowt[:, bass.ds(g * 4 + j, 1)], 0.0,
                                                        ALU.add, ALU.max))
                        st.then(nc.vector.tensor_scalar(P[:, 0:2, :], P[:, 0:2, :], 0.0, float(H + 2), ALU.max, ALU.min))
                        st.then(nc.vector.tensor_copy(pi[:], P[:, 0:2, :]))
                        st.then(nc.vector.tensor_copy(fl[:], pi[:]))
                        st.then(nc.vector.tensor_tensor(gt[:], fl[:], P[:, 0:2, :], ALU.is_gt))
                        st.then(nc.vector.tensor_tensor(fl[:], fl[:], gt[:], ALU.subtract))
                        st.then(nc.vector.tensor_tensor(fr[:], P[:, 0:2, :], fl[:], ALU.subtract))
                        st.then(nc.vector.scalar_tensor_tensor(rowf[:], fl[:, 0, :], float(TS), fl[:, 1, :],
                                                               ALU.mult, ALU.add))
                        if j == 0:
                            dve.wait_ge(stored, grp * 32 + 32)
                        st.then(nc.vector.tensor_scalar(idx[:, :, j], rowf[:], imgo[:, bass.ds(b, 1)], None, ALU.add))
                        dve.wait_ge(sig_ready, grp * 4 + j + 1)
                        st.then(nc.vector.scalar_tensor_tensor(a[:, 1, :], sg[:], 2.0, fr[:, 0, :], ALU.mult, ALU.mult))
                        st.then(nc.vector.scalar_tensor_tensor(a[:, 0, :], sg[:], 2.0, a[:, 1, :], ALU.mult, ALU.subtract))
                        dve.sem_inc(sig_used, 1)
                        for r in range(2):
                            last = nc.vector.tensor_tensor(wts[:, :, j, r, 1], a[:, r, :], fr[:, 1, :], ALU.mult)
                        st.then(last)
                        for r in range(2):
                            last = nc.vector.tensor_tensor(wts[:, :, j, r, 0], a[:, r, :], wts[:, :, j, r, 1], ALU.subtract)
                        st.then(last)
                        assert st.n == PER
                    dve.sem_inc(group_ready, 1)


def stage_branches(nc, mem, table, idx_dram, wts_dram, regw, ident, y_dram, ystats):
    ctx = ExitStack()
    with ctx:
        sb = lambda name, shape, dt=F32: ctx.enter_context(nc.sbuf_tensor(name, shape, dt))
        sem = lambda name: ctx.enter_context(nc.semaphore(name))
        R = sb("R", [C, TAPS, O])
        idx = sb("idx_c", [128, TAPS, 4], I32)
        wts = sb("wts_c", [128, TAPS * 16])
        G = [sb(f"G{s}", [128, 4, 4 * C]) for s in range(RING)]
        acc = [sb(f"acc{h}", [128, 4, C]) for h in range(2)]
        sT = [sb(f"sT{h}", [C, CH]) for h in range(2)]
        yb = [sb(f"yb{h}", [128, 2, CH]) for h in range(2)]
        ps_y = [ctx.enter_context(nc.psum_tensor(f"ps_y{h}", [128, 2, CH], F32)) for h in range(2)]
        ps_t = [ctx.enter_context(nc.psum_tensor(f"ps_t{h}", [C, CH], F32)) for h in range(2)]

        r_loaded = sem("r_loaded")
        part_loaded = [sem(f"part_loaded{u}") for u in range(2)]
        gathered = [sem(f"gathered{s}") for s in range(RING)]
        first_corner = sem("first_corner")
        corner = sem("corner")
        blended = sem("blended")
        turned = sem("turned")
        copied = sem("copied")
        summed = sem("summed")
        evacuated = sem("evacuated")
        measured = sem("measured")
        stored = [sem(f"y_stored{h}") for h in range(2)]
        gate = sem("c_gate")
        SPLIT = 32
        parts = ((0, SPLIT), (SPLIT, TAPS))
        block = ctx.enter_context(nc.Block())
        ends = [t0 + n for t0, n in BRANCHES]

        @block.sync
        def _(sp):
            sp.dma_start(R[:], regw).then_inc(r_loaded, 16)
            for h in range(2):
                sp.sem_inc(stored[h], 16)

            def load(g, u):
                lo, hi = parts[u]
                sp.dma_start(idx[:, lo:hi, :].rearrange("p t j -> p (t j)"),
                             idx_dram[bass.ds(g, 1), :, 4 * lo:4 * hi].rearrange("g p n -> (g p) n")).then_inc(part_loaded[u], 16)
                sp.dma_start(wts[:, 16 * lo:16 * hi],
                             wts_dram[bass.ds(g, 1), :, 16 * lo:16 * hi].rearrange("g p n -> (g p) n")).then_inc(part_loaded[u], 16)

            def store(g, br):
                sp.wait_ge(evacuated, g * NBR + (br + 3))
                sp.dma_start(y_dram[bass.ds(g, 1), br, :, :, :].rearrange("g h p n -> (g p) h n"),
                             yb[br % 2][:, :, :]).then_inc(stored[br % 2], 16)

            for u in range(2):
                load(0, u)
            with sp.Fori(0, NG - 1) as g:
                for u in range(2):
                    sp.wait_ge(blended, g * TAPS + parts[u][1] + RING)
                    load(g + 1, u)
                    if u == 0:
                        store(g, 0)
                for br in range(1, NBR):
                    store(g, br)
            for br in range(NBR):
                store(NG - 1, br)
            for h in range(2):
                sp.wait_ge(stored[h], 16 + 32 * NG)

        @block.gpsimd
        def _(pool):
            with pool.Fori(0, NG) as g:
                for k in range(TAPS):
                    if k in (0, SPLIT):
                        pool.wait_ge(part_loaded[k // SPLIT], g * 32 + 32)
                        pool.sem_inc(gate, 1)
                    pool.wait_ge(blended, g * TAPS + k + 1)
                    pool.sem_inc(gate, 1)
                    for j in range(4):
                        pool.indirect_dma_start(G[k % RING][:, j, :], None, table,
                                                bass.IndirectOffsetOnAxis(ap=idx[:, k, j:j + 1], axis=0))\
                            .then_inc(gathered[k % RING], 16)

        def rounds(eng, body, after):
            with eng.Fori(0, NG) as g:
                eng.wait_ge(part_loaded[0], g * 32 + 32)
                eng.sem_inc(gate, 1)
                with eng.Fori(0, 8) as q:
                    body(g, q)
                eng.wait_ge(part_loaded[1], g * 32 + 32)
                eng.sem_inc(gate, 1)
                with eng.Fori(8, 13) as q:
                    body(g, q)
                after(g, (0,))
                with eng.Fori(13, 15) as q:
                    body(g, q)
                after(g, (1, 2, 3))

        @block.scalar
        def _(act):
            act.sem_inc(evacuated, 2)

            def corner0(g, q, i):
                n = g * TAPS + q * 4 + i
                act.wait_ge(gathered[i], (g * 15 + q) * 64 + 64)
                act.wait_ge(turned, n + 1)
                act.sem_inc(gate, 1)
                for j in range(4):
                    last = nc.scalar.activation(acc[i % 2][:, j, :], G[i][:, j, 0:C], ACT.Copy,
                                                scale=wts[:, bass.ds(q * 64 + (i * 16 + j * 4), 1)])
                last.then_inc(first_corner, 1)

            def copy_out(g, q, i):
                n = g * TAPS + q * 4 + i
                act.wait_ge(turned, n + 3)
                act.wait_ge(summed, n + 1)
                nc.scalar.activation(sT[i % 2][:, :], ps_t[i % 2][:, :], ACT.Copy).then_inc(copied, 1)

            def body(g, q):
                corner0(g, q, 0)
                for i in range(1, 4):
                    corner0(g, q, i)
                    copy_out(g, q, i - 1)
                copy_out(g, q, 3)

            def after(g, brs):
                for br in brs:
                    act.wait_ge(summed, g * TAPS + ends[br] + 2)
                    act.wait_ge(stored[br % 2], g * 32 + (br // 2 * 16 + 16))
                    act.wait_ge(measured, g * NBR + br + 1)
                    for half in range(2):
                        last = nc.scalar.activation(yb[br % 2][:, half, :], ps_y[br % 2][:, half, :], ACT.Copy)
                    last.then_inc(evacuated, 1)

            rounds(act, body, after)

        @block.vector
        def _(dve):
            dve.sem_inc(blended, RING)
            dve.sem_inc(measured, 2)

            def body(g, q):
                for i in range(4):
                    n = g * TAPS + q * 4 + i
                    dve.wait_ge(first_corner, n + 1)
                    for c in range(1, 4):
                        if c > 1:
                            dve.wait_ge(corner, n * 2 + c - 1)
                        for j in range(4):
                            last = nc.vector.scalar_tensor_tensor(
                                acc[i % 2][:, j, :], G[i][:, j, c * C:(c + 1) * C],
                                wts[:, bass.ds(q * 64 + (i * 16 + j * 4 + c), 1)], acc[i % 2][:, j, :],
                                ALU.mult, ALU.add)
                        last.then_inc(corner if c < 3 else blended, 1)

            def after(g, brs):
                for br in brs:
                    dve.wait_ge(evacuated, g * NBR + br + 3)
                    dve.sem_inc(gate, 1)
                    for half in range(2):
                        last = nc.vector.bn_stats(ystats[:, 2 * br + half, bass.ds(g * 6, 6)],
                                                  yb[br % 2][:, half, :])
                    last.then_inc(measured, 1)

            rounds(dve, body, after)
            dve.wait_ge(measured, NBR * NG + 2)

        @block.tensor
        def _(pe):
            pe.sem_inc(turned, 2)
            pe.sem_inc(summed, 2)
            pe.wait_ge(r_loaded, 16)
            with pe.Fori(0, NG) as g:

                def turn(k):
                    pe.wait_ge(blended, g * TAPS + k + 1 + RING)
                    for j in range(4):
                        last = nc.tensor.transpose(ps_t[k % 2][:, 128 * j:128 * j + 128], acc[k % 2][:, j, :], ident[:, :])
                    last.then_inc(turned, 1)

                def contract(k):
                    br = [k < e for e in ends].index(True)
                    t0, n = BRANCHES[br]
                    pe.wait_ge(copied, g * TAPS + k + 1)
                    if k == t0:
                        pe.wait_ge(evacuated, g * NBR + br + 1)
                    for half in range(2):
                        last = nc.tensor.matmul(ps_y[br % 2][:, half, :], R[:, k, 128 * half:128 * half + 128],
                                                sT[k % 2][:, :], start=(k == t0), stop=(k == ends[br] - 1))
                    last.then_inc(summed, 1)

                for k in range(TAPS):
                    turn(k)
                    if k:
                        contract(k - 1)
                contract(TAPS - 1)


def group_affine(dve, act_sem, st, sq, var, sd, a, b, gm, gamma, beta, ready, nc):
    st.then(nc.vector.tensor_tensor(sq, gm[:, 0, :], gm[:, 0, :], ALU.mult))
    st.then(nc.vector.tensor_tensor(var, gm[:, 1, :], sq, ALU.subtract))
    st.then(nc.vector.tensor_scalar(var, var, 0.0, None, ALU.max))
    dve.sem_inc(ready, 1)
    dve.wait_ge(act_sem, 1)
    st.then(nc.vector.reciprocal(sd, sd))
    st.then(nc.vector.tensor_tensor(a, gamma, sd, ALU.mult))
    st.then(nc.vector.tensor_tensor(b, gm[:, 0, :], a, ALU.mult))
    st.then(nc.vector.tensor_tensor(b, beta, b, ALU.subtract))


def stage_fuse(nc, mem, y_dram, ystats, xsum, pool_w, fuse_w, gnp, gnf, blk16, blk8, eps5, fu, fa, fb):
    ctx = ExitStack()
    with ctx:
        sb = lambda name, shape, dt=F32: ctx.enter_context(nc.sbuf_tensor(name, shape, dt))
        sem = lambda name: ctx.enter_context(nc.semaphore(name))
        pw = sb("pw", [C, O])
        fw = sb("fw", [128, NFC, C])
        gp = sb("gp", [128, 2, B, NFC])
        gf = sb("gf", [C, 2, B])
        mv = sb("mv", [128, B, 2 * NBR, 2])
        me = sb("me", [128, 2, B * NFC])
        gm = sb("gm", [128, 2, B * NFC])
        sq = sb("sq", [128, B * NFC])
        var = sb("var", [128, B * NFC])
        sd = sb("sd", [128, B * NFC])
        ya = sb("ya", [128, B * NFC])
        ybb = sb("ybb", [128, B * NFC])
        xmean = sb("xmean", [C, B])
        y5 = sb("y5", [128, B, 2])
        z5 = sb("z5", [128, 2, B])
        bias5 = sb("bias5", [C, B])
        yin = [sb(f"yin{h}", [128, 2 * NBR, CH]) for h in range(2)]
        fstats = sb("fstats", [C, NG * 6])
        fmv = sb("fmv", [C, B, 2])
        fme = sb("fme", [C, 2, B])
        fgm = sb("fgm", [C, 2, B])
        fsq = sb("fsq", [C, B])
        fvar = sb("fvar", [C, B])
        fsd = sb("fsd", [C, B])
        ps_s = ctx.enter_context(nc.psum_tensor("ps_s", [128, 2, 64], F32))
        ps_f = [ctx.enter_context(nc.psum_tensor(f"ps_f{h}", [C, CH], F32)) for h in range(2)]
        params = sem("f_params")
        step = sem("f_step")
        xm_ready = sem("xm_ready")
        y5_ready = sem("y5_ready")
        me_ready = sem("me_ready")
        gm_ready = sem("gm_ready")
        var_ready = sem("f_var_ready")
        sd_ready = sem("f_sd_ready")
        ab_ready = sem("ab_ready")
        z5_ready = sem("z5_ready")
        b5_summed = sem("b5_summed")
        b5_ready = sem("b5_ready")
        y_loaded = [sem(f"y_loaded{h}") for h in range(2)]
        z_ready = [sem(f"z_ready{h}") for h in range(2)]
        fused = [sem(f"fused{h}") for h in range(2)]
        fu_ready = [sem(f"fu_ready{h}") for h in range(2)]
        fu_measured = sem("fu_measured")
        fme_ready = sem("fme_ready")
        fgm_ready = sem("fgm_ready")
        fvar_ready = sem("fvar_ready")
        fsd_ready = sem("fsd_ready")
        gate = sem("f_gate")
        block = ctx.enter_context(nc.Block())
        view = lambda t: t.rearrange("p (b n) -> p b n", b=B)

        @block.sync
        def _(sp):
            sp.dma_start(pw[:], pool_w).then_inc(params, 16)
            sp.dma_start(fw[:], fuse_w).then_inc(params, 16)
            sp.dma_start(gp[:], gnp).then_inc(params, 16)
            sp.dma_start(gf[:], gnf).then_inc(params, 16)
            with sp.Fori(0, NG // 2) as i:
                for h in range(2):
                    sp.wait_ge(fused[h], i + 1)
                    sp.dma_start(yin[h][:], y_dram[bass.ds(i * 2 + h, 1), :, :, :, :]
                                 .rearrange("g b h p n -> (g p) (b h) n")).then_inc(y_loaded[h], 16)

        @block.tensor
        def _(pe):
            for h in range(2):
                pe.sem_inc(fused[h], 1)
            pe.wait_ge(params, 64)
            pe.wait_ge(xm_ready, 1)
            for half in range(2):
                last = nc.tensor.matmul(ps_s[:, half, 0:B], pw[:, 128 * half:128 * half + 128], xmean[:, :],
                                        start=True, stop=True)
            last.then_inc(y5_ready, 1)
            pe.wait_ge(me_ready, 1)
            nc.tensor.matmul(ps_s[:, 0, 0:2 * B * NFC], blk16[:, :], flat(me[:]), start=True, stop=True)\
                .then_inc(gm_ready, 1)
            pe.wait_ge(z5_ready, 1)
            for half in range(2):
                last = nc.tensor.matmul(ps_s[:, 1, 0:B], fw[:, 2 * NBR + half, :], z5[:, half, :],
                                        start=(half == 0), stop=(half == 1))
            last.then_inc(b5_summed, 1)
            with pe.Fori(0, NG // 2) as i:
                for h in range(2):
                    pe.wait_ge(z_ready[h], i + 1)
                    pe.wait_ge(fu_ready[h], i + 1)
                    for n in range(2 * NBR):
                        last = nc.tensor.matmul(ps_f[h][:, :], fw[:, n, :], yin[h][:, n, :],
                                                start=(n == 0), stop=(n == 2 * NBR - 1))
                    last.then_inc(fused[h], 1)
            pe.wait_ge(fme_ready, 1)
            nc.tensor.matmul(ps_s[:, 0, 0:2 * B], blk8[:, :], flat(fme[:]), start=True, stop=True).then_inc(fgm_ready, 1)

        @block.scalar
        def _(act):
            for h in range(2):
                act.sem_inc(fu_ready[h], 1)
            act.wait_ge(var_ready, 1)
            nc.scalar.activation(sd[:], var[:], ACT.Sqrt, bias=eps5[:, 0:1]).then_inc(sd_ready, 1)
            act.wait_ge(ab_ready, 1)
            act.wait_ge(b5_ready, 1)
            act.sem_inc(gate, 1)
            with act.Fori(0, B) as b:
                with act.Fori(0, GI // 2) as i:
                    k = b * (GI // 2) + i
                    for h in range(2):
                        act.wait_ge(y_loaded[h], k * 16 + 16)
                        act.sem_inc(gate, 1)
                        for n in range(2 * NBR):
                            last = nc.scalar.activation(yin[h][:, n, :], yin[h][:, n, :], ACT.Relu,
                                                        bias=ybb[:, bass.ds(b * NFC + n, 1)],
                                                        scale=ya[:, bass.ds(b * NFC + n, 1)])
                        last.then_inc(z_ready[h], 1)
                    for h in range(2):
                        act.wait_ge(fused[h], k + 2)
                        act.sem_inc(gate, 1)
                        nc.scalar.activation(fu[:, bass.ds(b * HW + i * (2 * CH) + h * CH, CH)], ps_f[h][:, :],
                                             ACT.Identity, bias=bias5[:, bass.ds(b, 1)]).then_inc(fu_ready[h], 1)
            act.wait_ge(fvar_ready, 1)
            nc.scalar.activation(fsd[:], fvar[:], ACT.Sqrt, bias=eps5[:, 0:1]).then_inc(fsd_ready, 1)

        @block.vector
        def _(dve):
            st = Steps(dve, step)
            nc.vector.tensor_scalar(xmean[:], xsum[:], 1.0 / HW, None, ALU.mult).then_inc(xm_ready, 1)
            for b in range(B):
                for n in range(2 * NBR):
                    last = nc.vector.bn_aggr(mv[:, b, n, :], ystats[:, n, b * GI * 6:(b + 1) * GI * 6])
            st.then(last)
            m0, m1 = view(me[:, 0, :])[:, :, 0:2 * NBR], view(me[:, 1, :])[:, :, 0:2 * NBR]
            nc.vector.tensor_copy(m0, mv[:, :, :, 0])
            st.then(nc.vector.tensor_tensor(m1, mv[:, :, :, 0], mv[:, :, :, 0], ALU.mult))
            nc.vector.tensor_tensor(m1, m1, mv[:, :, :, 1], ALU.add)
            dve.wait_ge(y5_ready, 1)
            st.then(nc.vector.tensor_copy(y5[:], ps_s[:, :, 0:B].rearrange("p h b -> p b h")))
            nc.vector.tensor_copy(view(me[:, 0, :])[:, :, 2 * NBR:], y5[:])
            nc.vector.tensor_tensor(view(me[:, 1, :])[:, :, 2 * NBR:], y5[:], y5[:], ALU.mult).then_inc(me_ready, 1)
            dve.wait_ge(gm_ready, 1)
            st.then(nc.vector.tensor_copy(flat(gm[:]), ps_s[:, 0, 0:2 * B * NFC]))
            dve.wait_ge(params, 64)
            group_affine(dve, sd_ready, st, sq[:], var[:], sd[:], ya[:], ybb[:], gm, flat(gp[:, 0, :, :]),
                         flat(gp[:, 1, :, :]), var_ready, nc)
            dve.sem_inc(ab_ready, 1)
            z5v = z5[:].rearrange("p h b -> p b h")
            st.then(nc.vector.tensor_tensor(z5v, y5[:], view(ya[:])[:, :, 2 * NBR:], ALU.mult))
            st.then(nc.vector.tensor_tensor(z5v, z5v, view(ybb[:])[:, :, 2 * NBR:], ALU.add))
            nc.vector.tensor_scalar(z5[:], z5[:], 0.0, None, ALU.max).then_inc(z5_ready, 1)
            dve.wait_ge(b5_summed, 1)
            nc.vector.tensor_copy(bias5[:], ps_s[:, 1, 0:B]).then_inc(b5_ready, 1)
            with dve.Fori(0, NG // 2) as i:
                for h in range(2):
                    dve.wait_ge(fu_ready[h], i + 2)
                    dve.sem_inc(gate, 1)
                    nc.vector.bn_stats(fstats[:, bass.ds(i * 12 + h * 6, 6)],
                                       fu[:, bass.ds(i * (2 * CH) + h * CH, CH)]).then_inc(fu_measured, 1)
            dve.wait_ge(fu_measured, NG)
            for b in range(B):
                last = nc.vector.bn_aggr(fmv[:, b, :], fstats[:, b * GI * 6:(b + 1) * GI * 6])
            st.then(last)
            nc.vector.tensor_copy(fme[:, 0, :], fmv[:, :, 0])
            st.then(nc.vector.tensor_tensor(fme[:, 1, :], fmv[:, :, 0], fmv[:, :, 0], ALU.mult))
            nc.vector.tensor_tensor(fme[:, 1, :], fme[:, 1, :], fmv[:, :, 1], ALU.add).then_inc(fme_ready, 1)
            dve.wait_ge(fgm_ready, 1)
            st.then(nc.vector.tensor_copy(flat(fgm[:]), ps_s[:, 0, 0:2 * B]))
            group_affine(dve, fsd_ready, st, fsq[:], fvar[:], fsd[:], fa[:], fb[:], fgm, gf[:, 0, :], gf[:, 1, :],
                         fvar_ready, nc)


def stage_tokens(nc, mem, x, ident, flip, eps5, fu, fa, fb, accum, u_all, uT):
    ctx = ExitStack()
    with ctx:
        sb = lambda name, shape, dt=F32: ctx.enter_context(nc.sbuf_tensor(name, shape, dt))
        sem = lambda name: ctx.enter_context(nc.semaphore(name))
        xg = [sb(f"t_xg{h}", [C, CH]) for h in range(2)]
        rb = [sb(f"t_rb{h}", [C, CH]) for h in range(2)]
        tch = [sb(f"tch{h}", [C, 2, CH // 2]) for h in range(2)]
        un = [sb(f"un{h}", [128, 4, C]) for h in range(2)]
        stats = [sb(f"t_stats{h}", [128, 4, 6]) for h in range(2)]
        mv = [sb(f"t_mv{h}", [128, 4, 2]) for h in range(2)]
        sd = [sb(f"t_sd{h}", [128, 4]) for h in range(2)]
        rs = [sb(f"t_rs{h}", [128, 4]) for h in range(2)]
        ps_x = [ctx.enter_context(nc.psum_tensor(f"ps_tx{h}", [128, 4, C], F32)) for h in range(2)]
        ps_n = [ctx.enter_context(nc.psum_tensor(f"ps_tn{h}", [128, CH], F32)) for h in range(2)]
        ps_r = [ctx.enter_context(nc.psum_tensor(f"ps_tr{h}", [128, CH], F32)) for h in range(2)]
        pair = lambda name: [sem(f"{name}{h}") for h in range(2)]
        x_loaded = pair("tx_loaded")
        relu_ready = pair("relu_ready")
        t_ready = pair("t_ready")
        t_turned = pair("t_turned")
        t_kept = pair("t_kept")
        var_ready = pair("tvar_ready")
        sd_ready = pair("tsd_ready")
        u_ready = pair("u_ready")
        u_kept = pair("u_kept")
        u_turned = pair("u_turned")
        uT_ready = pair("uT_ready")
        edge_zeroed = sem("edge_zeroed")
        step = sem("t_step")
        gate = sem("t_gate")
        block = ctx.enter_context(nc.Block())
        NH = GI // 2

        def loops(eng):
            ctx = ExitStack()
            b = ctx.enter_context(eng.Fori(0, B))
            i = ctx.enter_context(eng.Fori(0, NH))
            return ctx, b, i, b * NH + i

        @block.sync
        def _(sp):
            loop, b, i, k = loops(sp)
            with loop:
                for h in range(2):
                    sp.wait_ge(t_ready[h], k + 1)
                    sp.dma_start(xg[h][:, :], x[bass.ds(b, 1), :, bass.ds(i * (2 * CH) + h * CH, CH)]
                                 .rearrange("b c n -> (b c) n")).then_inc(x_loaded[h], 16)

        @block.scalar
        def _(act):
            for h in range(2):
                act.sem_inc(uT_ready[h], 1)
                act.sem_inc(u_kept[h], 1)
            act.wait_ge(edge_zeroed, 1)
            loop, b, i, k = loops(act)
            with loop:
                for h in range(2):
                    act.wait_ge(t_ready[h], k + 1)
                    act.sem_inc(gate, 1)
                    nc.scalar.activation(rb[h][:, :], fu[:, bass.ds(b * HW + i * (2 * CH) + h * CH, CH)], ACT.Relu,
                                         bias=fb[:, bass.ds(b, 1)], scale=fa[:, bass.ds(b, 1)]).then_inc(relu_ready[h], 1)
                for h in range(2):
                    act.wait_ge(var_ready[h], k + 1)
                    nc.scalar.activation(sd[h][:, :], mv[h][:, :, 1], ACT.Sqrt, bias=eps5[:, 0:1]).then_inc(sd_ready[h], 1)
                for h in range(2):
                    act.wait_ge(u_turned[h], k + 2)
                    act.sem_inc(gate, 1)
                    nc.scalar.activation(uT[:, bass.ds(b * 2, 2), bass.ds(i * CH + (h * (CH // 2) + 1), CH // 2)],
                                         ps_n[h][:, :].rearrange("p (a n) -> p a n", a=2), ACT.Copy).then_inc(uT_ready[h], 1)
                    nc.scalar.activation(u_all[:, bass.ds(b * 2, 2), bass.ds(i * 4 + h * 2, 2), :],
                                         ps_r[h][:, :].rearrange("p (a j c) -> p a j c", a=2, j=2), ACT.Copy)\
                        .then_inc(u_kept[h], 1)
            for h in range(2):
                act.wait_ge(u_kept[h], NG // 2 + 1)
                act.wait_ge(uT_ready[h], NG // 2 + 1)

        @block.gpsimd
        def _(pool):
            for h in range(2):
                pool.sem_inc(t_kept[h], 1)
            pool.memset(uT[:, :, 0:1], 0.0).then_inc(edge_zeroed, 1)
            loop, b, i, k = loops(pool)
            with loop:
                for h in range(2):
                    pool.wait_ge(t_ready[h], k + 2)
                    pool.sem_inc(gate, 1)
                    nc.gpsimd.tensor_copy(accum[:, bass.ds(b * 2, 2), bass.ds(i * CH + h * (CH // 2), CH // 2)],
                                          tch[h][:, :, :]).then_inc(t_kept[h], 1)
            for h in range(2):
                pool.wait_ge(t_kept[h], NG // 2 + 1)

        @block.tensor
        def _(pe):
            for h in range(2):
                pe.sem_inc(t_turned[h], 1)
                pe.sem_inc(u_turned[h], 1)
            with pe.Fori(0, NG // 2) as k:
                for h in range(2):
                    pe.wait_ge(t_ready[h], k + 2)
                    pe.wait_ge(u_ready[h], k + 1)
                    for j in range(4):
                        last = nc.tensor.transpose(ps_x[h][:, j, :], tch[h][:, j // 2, 128 * (j % 2):128 * (j % 2) + 128],
                                                   ident[:, :])
                    last.then_inc(t_turned[h], 1)
                for h in range(2):
                    pe.wait_ge(u_ready[h], k + 2)
                    pe.wait_ge(uT_ready[h], k + 1)
                    pe.wait_ge(u_kept[h], k + 1)
                    nc.tensor.matmul(ps_r[h][:, :], flip[:, :], flat(un[h][:]), start=True, stop=True)
                    for j in range(4):
                        last = nc.tensor.transpose(ps_n[h][:, 128 * j:128 * j + 128], un[h][:, j, :], ident[:, :])
                    last.then_inc(u_turned[h], 1)

        @block.vector
        def _(dve):
            for h in range(2):
                dve.sem_inc(t_ready[h], 1)
                dve.sem_inc(u_ready[h], 1)
            with dve.Fori(0, NG // 2) as k:
                st = Steps(dve, step, k * 4)
                for h in range(2):
                    dve.wait_ge(x_loaded[h], k * 16 + 16)
                    dve.wait_ge(relu_ready[h], k + 1)
                    dve.wait_ge(t_turned[h], k + 1)
                    dve.wait_ge(t_kept[h], k + 1)
                    parity = lambda t: t[:, :].rearrange("p (n a) -> p a n", a=2)
                    nc.vector.tensor_tensor(tch[h][:, :, :], parity(rb[h]), parity(xg[h]), ALU.add).then_inc(t_ready[h], 1)
                for h in range(2):
                    dve.wait_ge(t_turned[h], k + 2)
                    for j in range(4):
                        last = nc.vector.bn_stats(stats[h][:, j, :], ps_x[h][:, j, :])
                    st.then(last)
                    dve.sem_inc(gate, 1)
                    for j in range(4):
                        last = nc.vector.bn_aggr(mv[h][:, j, :], stats[h][:, j, :])
                    last.then_inc(var_ready[h], 1)
                for h in range(2):
                    dve.wait_ge(sd_ready[h], k + 1)
                    st.then(nc.vector.reciprocal(rs[h][:, :], sd[h][:, :]))
                    dve.wait_ge(u_turned[h], k + 1)
                    for j in range(4):
                        last = nc.vector.tensor_scalar(un[h][:, j, :], ps_x[h][:, j, :], mv[h][:, j, 0:1],
                                                       rs[h][:, j:j + 1], ALU.subtract, ALU.mult)
                    last.then_inc(u_ready[h], 1)


def segments(r):
    return ((0, 256, 0), (256, 512, 1)) if r == 0 else ((0, 512, min(r + 1, SEG - 1)),)


def stage_spectral(nc, mem, phi, m_phi, m_u, sigma, logw, gumbel, accum, u_all, uT, out):
    ctx = ExitStack()
    with ctx:
        sb = lambda name, shape, dt=F32: ctx.enter_context(nc.sbuf_tensor(name, shape, dt))
        sem = lambda name: ctx.enter_context(nc.semaphore(name))
        lw = sb("lw", [128, SEG])
        gb = sb("gb", [128, SEG])
        sm = sb("sm", [128, 4])
        ys = sb("ys", [128, SEG])
        hot = sb("hot", [128, SEG])
        wi = sb("wi", [128, SEG])
        sg = sb("sigma_b", [128, KF])
        ws = sb("ws", [128, KF, SEG])
        mu = sb("mu", [C, SEG, 3, C])
        mus = sb("mus", [C, 3, SEG, C])
        ml = [sb(f"ml{h}", [C, 2, SEG, C]) for h in range(2)]
        mt = sb("mt", [C, 2, SEG, C])
        ms = [sb(f"ms{h}", [C, 2, SEG, C]) for h in range(2)]
        se = [sb(f"se{h}", [128, HALF]) for h in range(2)]
        so = [sb(f"so{h}", [128, HALF + 1]) for h in range(2)]
        ub = [sb(f"ub{h}", [C, 2, CH]) for h in range(2)]
        ob = [sb(f"ob{h}", [C, CH]) for h in range(2)]
        ps_c = [ctx.enter_context(nc.psum_tensor(f"ps_c{q}", [C, 2, CH], F32)) for q in range(2)]
        ps_m = [ctx.enter_context(nc.psum_tensor(f"ps_m{q}", [C, CH], F32)) for q in range(2)]
        pair = lambda name: [sem(f"{name}{h}") for h in range(2)]
        params = sem("s_params")
        step = sem("s_step")
        z_ready = sem("s_z_ready")
        e_ready = sem("s_e_ready")
        sig_rooted = sem("sig_rooted")
        mus_ready = sem("mus_ready")
        m_loaded = pair("m_loaded")
        strips_loaded = pair("strips_loaded")
        ms_ready = pair("ms_ready")
        filter_done = pair("filter_done")
        mt_used = sem("mt_used")
        convolved = sem("convolved")
        u_copied = sem("u_copied")
        mixed = sem("mixed")
        added = sem("added")
        o_ready = pair("o_ready")
        o_stored = pair("o_stored")
        gate = sem("s_gate")
        block = ctx.enter_context(nc.Block())
        regions = [(b, p, r) for b in range(B) for p in range(2) for r in range(4)]
        NR = len(regions)
        PADC = HALF + 128
        strip_e = bass.AP(tensor=phi.tensor, offset=1, ap=[[2 * PADC, KF], [1, 128], [1, HALF]])
        strip_o = bass.AP(tensor=phi.tensor, offset=PADC, ap=[[2 * PADC, KF], [1, 128], [1, HALF + 1]])

        @block.sync
        def _(sp):
            one = lambda t, n: t.rearrange("(a k) -> a k", a=1).to_broadcast([128, n])
            sp.dma_start(lw[:], one(logw, SEG)).then_inc(params, 16)
            sp.dma_start(gb[:], one(gumbel, SEG)).then_inc(params, 16)
            sp.dma_start(sg[:], one(sigma, KF)).then_inc(params, 16)
            sp.dma_start(mu[:], m_u).then_inc(params, 16)
            for h in range(2):
                sp.sem_inc(o_stored[h], 16)
            with sp.Fori(0, KF // 2) as i:
                for h in range(2):
                    sp.wait_ge(filter_done[h], i + 1)
                    sp.dma_start(ml[h][:], m_phi[bass.ds(i * 2 + h, 1), :, :, :, :].rearrange("k d s i e -> (k d) s i e"))\
                        .then_inc(m_loaded[h], 16)
                    sp.dma_start(se[h][:], strip_e[bass.ds(i * 2 + h, 1), :, :].rearrange("k p n -> (k p) n"))\
                        .then_inc(strips_loaded[h], 16)
                    sp.dma_start(so[h][:], strip_o[bass.ds(i * 2 + h, 1), :, :].rearrange("k p n -> (k p) n"))\
                        .then_inc(strips_loaded[h], 16)
            for n in range(NG):
                b, g = divmod(n, GI)
                sp.wait_ge(o_ready[n % 2], n // 2 + 1)
                sp.dma_start(out[b, :, g * CH:(g + 1) * CH], ob[n % 2][:, :]).then_inc(o_stored[n % 2], 16)
            for h in range(2):
                sp.wait_ge(o_stored[h], 16 * (NG // 2 + 1))

        @block.scalar
        def _(act):
            act.wait_ge(params, 64)
            act.wait_ge(z_ready, 1)
            nc.scalar.activation(ys[:], lw[:], ACT.Exp, bias=sm[:, 1:2]).then_inc(e_ready, 1)
            nc.scalar.activation(sg[:], sg[:], ACT.Sqrt).then_inc(sig_rooted, 1)
            act.wait_ge(sig_rooted, 1)
            nc.scalar.activation(sg[:], sg[:], ACT.Sqrt).then_inc(sig_rooted, 1)
            with act.Fori(0, KF) as k:
                for n in range(NR):
                    act.wait_ge(convolved, k * NR + n + 1)
                    act.wait_ge(mixed, k * NR + n + 1)
                    nc.scalar.activation(ub[n % 2][:, :, :], ps_c[n % 2][:, :, :], ACT.Copy).then_inc(u_copied, 1)

        @block.vector
        def _(dve):
            dve.sem_inc(added, 2)
            st = Steps(dve, step)
            dve.wait_ge(params, 64)
            st.then(nc.vector.tensor_tensor(lw[:], lw[:], gb[:], ALU.add))
            st.then(nc.vector.tensor_reduce(sm[:, 0:1], lw[:], AX.X, ALU.max))
            nc.vector.tensor_scalar(sm[:, 1:2], sm[:, 0:1], -1.0, None, ALU.mult).then_inc(z_ready, 1)
            dve.wait_ge(e_ready, 1)
            st.then(nc.vector.tensor_reduce(sm[:, 2:3], ys[:], AX.X, ALU.add))
            st.then(nc.vector.reciprocal(sm[:, 3:4], sm[:, 2:3]))
            st.then(nc.vector.tensor_scalar(ys[:], ys[:], sm[:, 3:4], None, ALU.mult))
            st.then(nc.vector.tensor_reduce(sm[:, 0:1], ys[:], AX.X, ALU.max))
            st.then(nc.vector.tensor_scalar(hot[:], ys[:], sm[:, 0:1], None, ALU.is_ge))
            st.then(nc.vector.tensor_scalar(sm[:, 2:3], sm[:, 3:4], 0.0, 1.0, ALU.mult, ALU.add))
            for i in range(SEG):
                st.then(nc.vector.tensor_tensor(hot[:, i:i + 1], hot[:, i:i + 1], sm[:, 2:3], ALU.mult))
                st.then(nc.vector.tensor_tensor(sm[:, 2:3], sm[:, 2:3], hot[:, i:i + 1], ALU.subtract))
            st.then(nc.vector.tensor_tensor(wi[:], hot[:], ys[:], ALU.subtract))
            st.then(nc.vector.tensor_tensor(wi[:], wi[:], ys[:], ALU.add))
            dve.wait_ge(sig_rooted, 2)
            for i in range(SEG):
                last = nc.vector.tensor_scalar(ws[:, :, i], sg[:, :], wi[:, i:i + 1], None, ALU.mult)
            st.then(last)
            st.then(nc.vector.tensor_scalar(mus[:, :, SEG - 1, :], mu[:, 0, :, :], wi[:, 0:1], None, ALU.mult))
            for i in range(1, SEG):
                ins = nc.vector.scalar_tensor_tensor(mus[:, :, SEG - 1 - i, :], mu[:, i, :, :], wi[:, i:i + 1],
                                                     mus[:, :, SEG - i, :], ALU.mult, ALU.add)
                if i < SEG - 1:
                    st.then(ins)
                else:
                    ins.then_inc(mus_ready, 1)

            def add(count, n):
                b, p, r = regions[n]
                dve.wait_ge(mixed, count + 3)
                acc = accum[:, 2 * b + p, CH * r:CH * r + CH]
                nc.vector.tensor_tensor(acc, acc, ps_m[n % 2][:, :], ALU.add).then_inc(added, 1)

            for n in range(NR):
                add(n, n)
            base = st.n
            PER = 2 * (2 + SEG - 1)
            with dve.Fori(0, KF // 2) as i:
                st = Steps(dve, step, i * PER + base)
                for h in range(2):
                    dve.wait_ge(m_loaded[h], i * 16 + 16)
                    dve.wait_ge(filter_done[h], i + 1)
                    nc.vector.tensor_tensor(mt[:, 0, :, :], ml[h][:, 0, :, :], ml[h][:, 1, :, :], ALU.add)
                    st.then(nc.vector.tensor_tensor(mt[:, 1, :, :], ml[h][:, 0, :, :], ml[h][:, 1, :, :], ALU.subtract))
                    for s in range(SEG):
                        w = ws[:].rearrange("p k s -> p (k s)")[:, bass.ds(i * (2 * SEG) + (h * SEG + s), 1)]
                        if s == 0:
                            ins = nc.vector.tensor_scalar(ms[h][:, :, SEG - 1, :], mt[:, :, 0, :], w, None, ALU.mult)
                        else:
                            ins = nc.vector.scalar_tensor_tensor(ms[h][:, :, SEG - 1 - s, :], mt[:, :, s, :], w,
                                                                 ms[h][:, :, SEG - s, :], ALU.mult, ALU.add)
                        st.then(ins)
                    dve.sem_inc(ms_ready[h], 1)
                    for n in range(NR):
                        add(i * (2 * NR) + (h * NR + n + NR), n)
                assert st.n == PER
            dve.wait_ge(added, NR * (KF + 1) + 2)
            for n in range(NG):
                b, g = divmod(n, GI)
                dve.wait_ge(o_stored[n % 2], 16 * (n // 2 + 1))
                nc.vector.tensor_copy(ob[n % 2][:, :].rearrange("p (n a) -> p a n", a=2),
                                      accum[:, 2 * b:2 * b + 2, g * (CH // 2):(g + 1) * (CH // 2)]).then_inc(o_ready[n % 2], 1)

        @block.tensor
        def _(pe):
            for h in range(2):
                pe.sem_inc(filter_done[h], 1)
            pe.sem_inc(mixed, 2)
            pe.wait_ge(mus_ready, 1)
            for n, (b, p, r) in enumerate(regions):
                pe.wait_ge(added, n + 1)
                for s, (lo, hi, seg) in enumerate(segments(r)):
                    for lag in range(3):
                        q, shift = (p - lag) % 2, (p - lag) // 2
                        c0 = 1 + CH * r + lo + shift
                        last = nc.tensor.matmul(ps_m[n % 2][:, lo:hi], mus[:, lag, seg, :], uT[:, 2 * b + q, c0:c0 + hi - lo],
                                                start=(s == 0 and lag == 0), stop=(lag == 2), skip_group_check=True)
                last.then_inc(mixed, 1)

            def convolve(h, n):
                b, p, r = regions[n]
                for par in range(2):
                    q = p if par == 0 else 1 - p
                    last_j = 4 * r + 3
                    for j in range(last_j + 1):
                        m0 = CH * r - 128 * j
                        lo = max(0, -m0)
                        m0 = max(m0, 0)
                        strip, s0 = (se[h], m0) if par == 0 else (so[h], m0 + p)
                        last = nc.tensor.matmul(ps_c[n % 2][:, par, lo:CH], u_all[:, 2 * b + q, j, :],
                                                strip[:, s0:s0 + CH - lo], start=(j == 0), stop=(j == last_j),
                                                skip_group_check=True)
                last.then_inc(convolved, 1)

            def mix(h, n, count):
                b, p, r = regions[n]
                pe.wait_ge(u_copied, count + 1)
                pe.wait_ge(added, count + NR + 1)
                for s, (lo, hi, seg) in enumerate(segments(r)):
                    for par in range(2):
                        last = nc.tensor.matmul(ps_m[n % 2][:, lo:hi], ms[h][:, par, seg, :], ub[n % 2][:, par, lo:hi],
                                                start=(s == 0 and par == 0), stop=(par == 1), skip_group_check=True)
                last.then_inc(mixed, 1)

            with pe.Fori(0, KF // 2) as i:
                for h in range(2):
                    pe.wait_ge(strips_loaded[h], i * 32 + 32)
                    pe.wait_ge(ms_ready[h], i + 1)
                    for n in range(NR):
                        count = i * (2 * NR) + (h * NR + n)
                        convolve(h, n)
                        if n:
                            mix(h, n - 1, count - 1)
                    mix(h, NR - 1, count)
                    pe.sem_inc(filter_done[h], 1)


def program(nc, d):
    ctx = ExitStack()
    with ctx:
        sb = lambda name, shape, dt=F32: ctx.enter_context(nc.sbuf_tensor(name, shape, dt))
        table = nc.dram_tensor("table", (B * TROWS, 4 * C), F32, kind="Internal").ap()
        idx_dram = nc.dram_tensor("idx_dram", (NG, 128, TAPS * 4), I32, kind="Internal").ap()
        wts_dram = nc.dram_tensor("wts_dram", (NG, 128, TAPS * 16), F32, kind="Internal").ap()
        y_dram = nc.dram_tensor("y_dram", (NG, NBR, 2, 128, CH), F32, kind="Internal").ap()
        ident = sb("ident", [128, 128])
        flip = sb("flip", [128, 128])
        blk16 = sb("blk16", [128, 128])
        blk8 = sb("blk8", [128, 128])
        eps6 = sb("eps6", [128, 1])
        eps5 = sb("eps5", [128, 1])
        xsum = sb("xsum", [C, B])
        ystats = sb("ystats", [128, 2 * NBR, NG * 6])
        fa = sb("fa", [C, B])
        fb = sb("fb", [C, B])
        const_loaded = ctx.enter_context(nc.semaphore("const_loaded"))
        with nc.Block() as block:
            @block.sync
            def _(sp):
                for t, name in ((ident, "ident"), (flip, "flip"), (blk16, "blk16"), (blk8, "blk8")):
                    sp.dma_start(t[:], d[name]).then_inc(const_loaded, 16)
                sp.wait_ge(const_loaded, 64)

            @block.gpsimd
            def _(pool):
                pool.memset(eps6[:], 1e-6)
                pool.memset(eps5[:], 1e-5)

        with nc.sbuf_tensor("xnpad", [C, B * HP, HP], F32) as xnpad:
            stage_normalise(nc, None, d["x"], table, ident, eps6, xnpad, xsum)
            stage_offsets(nc, None, xnpad, d["w_om"], d["base_om"], d["bias_om"], d["row_off"], idx_dram, wts_dram)
        stage_branches(nc, None, table, idx_dram, wts_dram, d["regw"], ident, y_dram, ystats)
        accum = sb("accum", [C, 2 * B, HALF])
        u_all = sb("u_all", [128, 2 * B, HALF // 128, C])
        uT = sb("uT", [C, 2 * B, HALF + 1])
        with nc.sbuf_tensor("fu", [C, B * HW], F32) as fu:
            stage_fuse(nc, None, y_dram, ystats, xsum, d["pool_w"], d["fuse_w"], d["gnp"], d["gnf"], blk16, blk8, eps5,
                       fu, fa, fb)
            stage_tokens(nc, None, d["x"], ident, flip, eps5, fu, fa, fb, accum, u_all, uT)
        stage_spectral(nc, None, d["phi"], d["m_phi"], d["m_u"], d["sigma"], d["logw"], d["gumbel"], accum, u_all, uT,
                       d["out"])


def kernel(**inputs):
    import numpy as np
    import concourse.bacc as bacc
    from concourse.bass_utils import run_bass_kernel_spmd as run

    g = {n: np.asarray(v) for n, v in inputs.items()}
    P = "L0_conv_"
    f = np.float32
    a = {}
    a["x"] = g["x"].reshape(B, C, HW)
    w_om = np.zeros((C, 7, 7, 3, TAPS), f)
    bias_om = np.zeros((3, TAPS), f)
    base = np.zeros((128, 3, TAPS), f)
    regw = np.zeros((C, TAPS, O), f)
    p = np.arange(128)
    t0 = 0
    for name, k in (("b4", 7), ("b3", 3), ("b1", 1), ("b2", 1)):
        n, lo = k * k, (7 - k) // 2
        offw = g[P + name + "_offw"].reshape(n, 2, C, k, k)
        w_om[:, lo:lo + k, lo:lo + k, 0:2, t0:t0 + n] = offw.transpose(2, 3, 4, 1, 0)
        w_om[:, lo:lo + k, lo:lo + k, 2, t0:t0 + n] = g[P + name + "_modw"].transpose(1, 2, 3, 0)
        bias_om[0:2, t0:t0 + n] = g[P + name + "_offb"].reshape(n, 2).T
        bias_om[2, t0:t0 + n] = g[P + name + "_modb"]
        ky, kx = np.divmod(np.arange(n), k)
        base[:, 0, t0:t0 + n] = (p[:, None] // W) + ky - k // 2 + 2
        base[:, 1, t0:t0 + n] = (p[:, None] % W) + kx - k // 2 + 2
        regw[:, t0:t0 + n, :] = g[P + name + "_regw"].reshape(O, C, n).transpose(1, 2, 0)
        t0 += n
    a["w_om"] = w_om.reshape(C, 49, 3, TAPS)
    a["bias_om"], a["base_om"], a["regw"] = bias_om, base, regw
    a["row_off"] = np.broadcast_to((2 * np.arange(HW // 128)).astype(f), (128, HW // 128)).copy()
    order = ("b4", "b3", "b1", "b2", "pool")
    gnp = np.stack([np.concatenate([g[P + n + s].reshape(2, 128) for n in order]) for s in ("_gng", "_gnb")])
    a["gnp"] = np.repeat(gnp.transpose(2, 0, 1)[:, :, None, :], B, axis=2)
    a["gnf"] = np.repeat(np.stack([g[P + "fuse_gng"], g[P + "fuse_gnb"]], 1)[:, :, None], B, axis=2)
    fw = g[P + "fuse_w"].reshape(C, 5, 2, 128)[:, [3, 2, 0, 1, 4]]
    a["fuse_w"] = fw.reshape(C, NFC, 128).transpose(2, 1, 0)
    a["pool_w"] = g[P + "pool_w"].reshape(O, C).T
    a["ident"] = np.eye(128, dtype=f)
    a["flip"] = a["ident"][::-1]
    grp = lambda n: (p[:, None] // n == p[None, :] // n).astype(f) / f(n)
    a["blk16"], a["blk8"] = grp(O // 16), grp(C // 16)
    Q = "L0_ffn_"
    phi = np.zeros((KF, 2, 128 + HALF), f)
    phi[:, :, 128:] = g[Q + "phi"].reshape(HALF, 2, KF).transpose(2, 1, 0)
    a["phi"] = phi
    a["m_phi"] = np.stack([g[Q + "M_phi_plus"], g[Q + "M_phi_minus"]]).transpose(2, 3, 0, 1, 4)
    a["m_u"] = g[Q + "M_u"].transpose(2, 0, 1, 3)
    a["sigma"], a["logw"], a["gumbel"] = g[Q + "sigma"], g[Q + "log_weights"], g[Q + "gumbel"]
    a = {n: np.ascontiguousarray(v) for n, v in a.items()}

    nc = bacc.Bacc("TRN2", target_bir_lowering=False, num_devices=1)
    d = {n: nc.dram_tensor(f"in_{n}", v.shape, mybir.dt.from_np(v.dtype), kind="ExternalInput").ap() for n, v in a.items()}
    d["out"] = nc.dram_tensor("out", (B, C, HW), F32, kind="ExternalOutput").ap()
    program(nc, d)
    r = run(nc, [{f"in_{n}": v for n, v in a.items()}], core_ids=[0])
    return r.results[0]["out"].reshape(B, C, H, W)
```

```python
import concourse.bass as bass
from concourse import mybir
from contextlib import ExitStack

B, C, H, W = 2, 128, 64, 64
HW = H * W
O = 256
TAPS = 49 + 9 + 1 + 1
BRANCHES = ((0, 49), (49, 9), (58, 1), (59, 1))
NBR = len(BRANCHES)
PAD = 3
HP = H + 2 * PAD
TS = H + 3
TROWS = TS * TS
CH = 512
GI = HW // CH
XR = 2 * HP + 28
HR = CH // W + 2 * PAD
NG = B * GI
RING = 6
KF = 16
HALF = HW // 2
SEG = 4
BS = 64
NB = HALF // BS
NF = NB
EX = BS + 1
KC = 4
NFC = 2 * (NBR + 1)
F32 = mybir.dt.float32
F32R = mybir.dt.float32r
I32 = mybir.dt.int32
ALU = mybir.AluOpType
ACT = mybir.ActivationFunctionType
AX = mybir.AxisListType


class Steps:

    def __init__(self, eng, sem, base=0):
        self.eng, self.sem, self.base, self.n = eng, sem, base, 0

    def then(self, ins):
        self.n += 1
        ins.then_inc(self.sem, 1)
        self.eng.wait_ge(self.sem, self.base + self.n)


def flat(ap):
    n = len(ap.shape) - 1
    names = " ".join("abcdef"[:n])
    return ap.rearrange(f"p {names} -> p ({names})")


def stage_normalise(nc, x, table, ident, eps6, xsum, xn_dram):
    ctx = ExitStack()
    with ctx:
        sb = lambda name, shape, dt=F32: ctx.enter_context(nc.sbuf_tensor(name, shape, dt))
        sem = lambda name: ctx.enter_context(nc.semaphore(name))
        xg = [sb(f"xg{h}", [C, CH]) for h in range(2)]
        xn = [sb(f"xn{h}", [128, 4, C]) for h in range(2)]
        stats = [sb(f"ln_stats{h}", [128, 4, 6]) for h in range(2)]
        mv = [sb(f"ln_mv{h}", [128, 4, 2]) for h in range(2)]
        sd = [sb(f"ln_sd{h}", [128, 4]) for h in range(2)]
        rs = [sb(f"ln_rs{h}", [128, 4]) for h in range(2)]
        zero = sb("zero", [TS, 2 * 4 * C])
        xnpad = sb("xnpad", [C, XR, HP])
        ps_x = [ctx.enter_context(nc.psum_tensor(f"ps_x{h}", [128, 4, C], F32)) for h in range(2)]
        ps_n = [ctx.enter_context(nc.psum_tensor(f"ps_n{h}", [128, CH], F32)) for h in range(2)]

        zero_set = sem("zero_set")
        border_written = sem("border_written")
        pad_zeroed = sem("pad_zeroed")
        x_loaded = [sem(f"x_loaded{h}") for h in range(2)]
        x_turned = [sem(f"x_turned{h}") for h in range(2)]
        var_ready = [sem(f"var_ready{h}") for h in range(2)]
        sd_ready = [sem(f"sd_ready{h}") for h in range(2)]
        dve_step = sem("ln_dve_step")
        xn_ready = [sem(f"xn_ready{h}") for h in range(2)]
        xn_turned = [sem(f"xn_turned{h}") for h in range(2)]
        xn_copied = [sem(f"xn_copied{h}") for h in range(2)]
        table_written = [sem(f"table_written{h}") for h in range(2)]
        xn_stored = sem("xn_stored")
        gate = sem("ln_gate")
        WR = 8 * 16
        tab = table.rearrange("(b y x) s -> b y x s", b=B, y=TS)
        tab2 = table.rearrange("(y x) s -> y x s", x=TS)
        block = ctx.enter_context(nc.Block())

        @block.gpsimd
        def _(pool):
            pool.memset(zero[:], 0.0).then_inc(zero_set, 1)
            pool.memset(xnpad[:], 0.0).then_inc(pad_zeroed, 1)

        @block.sync
        def _(sp):
            sp.wait_ge(zero_set, 1)
            for b in range(B):
                for y in (0, TS - 2):
                    sp.dma_start(tab[b, y:y + 2, :, :].rearrange("y x s -> (y x s)").rearrange("(p n) -> p n", p=TS),
                                 zero[:, :]).then_inc(border_written, 16)
                for c in (0, TS - 2):
                    sp.dma_start(tab[b, 2:TS - 2, c:c + 2, :].rearrange("y x s -> y (x s)"), zero[0:TS - 4, :])\
                        .then_inc(border_written, 16)
            for h in range(2):
                sp.sem_inc(table_written[h], WR)
            sp.wait_ge(border_written, 16 * 4 * B)
            with sp.Fori(0, B) as b:
                with sp.Fori(0, GI // 2) as i:
                    k = b * (GI // 2) + i
                    for h in range(2):
                        sp.wait_ge(x_turned[h], k + 1)
                        sp.dma_start(xg[h][:, :], x[bass.ds(b, 1), :, bass.ds(i * (2 * CH) + h * CH, CH)]
                                     .rearrange("b c n -> (b c) n")).then_inc(x_loaded[h], 16)
                    for h in range(2):
                        sp.wait_ge(xn_ready[h], k + 2)
                        for half in range(2):
                            src = xn[h][64 * half:64 * half + 64, :, :]
                            for slot, (dy, dx) in enumerate(((0, 0), (0, 1), (1, 0), (1, 1))):
                                y0 = b * TS + i * 16 + (h * 8 + half + 2 - dy)
                                dst = tab2[bass.ds(y0, 4, step=2), 2 - dx:2 - dx + W, slot * C:(slot + 1) * C]
                                sp.dma_start(dst.rearrange("t x c -> x t c"), src).then_inc(table_written[h], 16)
            for h in range(2):
                sp.wait_ge(table_written[h], WR * (NG // 2 + 1))

        @block.tensor
        def _(pe):
            for h in range(2):
                pe.sem_inc(x_turned[h], 1)
                pe.sem_inc(xn_turned[h], 1)
            with pe.Fori(0, NG // 2) as k:
                for h in range(2):
                    pe.wait_ge(x_loaded[h], 16 * k + 16)
                    pe.wait_ge(xn_ready[h], k + 1)
                    for j in range(4):
                        last = nc.tensor.transpose(ps_x[h][:, j, :], xg[h][:, 128 * j:128 * j + 128], ident[:, :])
                    last.then_inc(x_turned[h], 1)
                for h in range(2):
                    pe.wait_ge(xn_ready[h], k + 2)
                    pe.wait_ge(xn_copied[h], k + 1)
                    for j in range(4):
                        last = nc.tensor.transpose(ps_n[h][:, 128 * j:128 * j + 128], xn[h][:, j, :], ident[:, :])
                    last.then_inc(xn_turned[h], 1)

        @block.vector
        def _(dve):
            for h in range(2):
                dve.sem_inc(xn_ready[h], 1)
            with dve.Fori(0, NG // 2) as k:
                st = Steps(dve, dve_step, k * 4)
                for h in range(2):
                    dve.wait_ge(x_turned[h], k + 2)
                    for j in range(4):
                        last = nc.vector.bn_stats(stats[h][:, j, :], ps_x[h][:, j, :])
                    st.then(last)
                    dve.sem_inc(gate, 1)
                    for j in range(4):
                        last = nc.vector.bn_aggr(mv[h][:, j, :], stats[h][:, j, :])
                    last.then_inc(var_ready[h], 1)
                for h in range(2):
                    dve.wait_ge(sd_ready[h], k + 1)
                    st.then(nc.vector.reciprocal(rs[h][:, :], sd[h][:, :]))
                    dve.wait_ge(table_written[h], k * WR + WR)
                    dve.wait_ge(xn_turned[h], k + 1)
                    for j in range(4):
                        last = nc.vector.tensor_scalar(xn[h][:, j, :], ps_x[h][:, j, :], mv[h][:, j, 0:1],
                                                       rs[h][:, j:j + 1], ALU.subtract, ALU.mult)
                    last.then_inc(xn_ready[h], 1)
            for h in range(2):
                dve.wait_ge(xn_copied[h], NG // 2 + 1)
            for b in range(B):
                nc.vector.tensor_reduce(xsum[:, b:b + 1], xnpad[:, b * HP + PAD:b * HP + PAD + H, PAD:PAD + W],
                                        AX.XY, ALU.add)

        @block.scalar
        def _(act):
            for h in range(2):
                act.sem_inc(xn_copied[h], 1)
            act.wait_ge(pad_zeroed, 1)
            with act.Fori(0, B) as b:
                with act.Fori(0, GI // 2) as i:
                    k = b * (GI // 2) + i
                    for h in range(2):
                        act.wait_ge(var_ready[h], k + 1)
                        nc.scalar.activation(sd[h][:, :], mv[h][:, :, 1], ACT.Sqrt, bias=eps6[:, 0:1])\
                            .then_inc(sd_ready[h], 1)
                    for h in range(2):
                        act.wait_ge(xn_turned[h], k + 2)
                        act.sem_inc(gate, 1)
                        nc.scalar.activation(
                            xnpad[:, bass.ds(b * HP + i * 16 + h * 8 + PAD, 8), PAD:PAD + W],
                            ps_n[h][:, :].rearrange("p (y x) -> p y x", x=W), ACT.Copy).then_inc(xn_copied[h], 1)
            for h in range(2):
                act.wait_ge(xn_copied[h], NG // 2 + 1)
            act.dma_start(xn_dram, xnpad[:]).then_inc(xn_stored, 16)
            act.wait_ge(xn_stored, 16)


def stage_branches(nc, xn_dram, table, w_om, base_om, bias_om, row_off, img_off, regw, ident, y_dram, ystats):
    ctx = ExitStack()
    with ctx:
        sb = lambda name, shape, dt=F32: ctx.enter_context(nc.sbuf_tensor(name, shape, dt))
        sem = lambda name: ctx.enter_context(nc.semaphore(name))
        pair = lambda name: [sem(f"{name}{h}") for h in range(2)]
        wom = sb("wom", [C, 49, 3, TAPS])
        base = sb("base", [128, 3, TAPS])
        rowt = sb("rowt", [128, (NG + 1) * 4])
        imgt = sb("imgt", [128, (NG + 1) * 4])
        win = sb("win", [C, 7, HR, W])
        P = sb("P", [128, 3, TAPS])
        sg = sb("sg", [128, TAPS])
        pi = sb("pi", [128, 2, TAPS], I32)
        fl = sb("fl", [128, 2, TAPS])
        gt = sb("gt", [128, 2, TAPS])
        fr = sb("fr", [128, 2, TAPS])
        a = sb("a", [128, 2, TAPS])
        rowf = a[:, 0, :]
        idx_next = sb("idx_next", [128, TAPS, 4], I32)
        wts_next = sb("wts_next", [128, TAPS, 4, 2, 2])
        R = sb("R", [C, TAPS, O])
        idx = sb("idx", [128, TAPS, 4], I32)
        wts = sb("wts", [128, TAPS * 16])
        G = [sb(f"G{s}", [128, 4, 4 * C]) for s in range(RING)]
        acc = [sb(f"acc{h}", [128, 4, C]) for h in range(3)]
        sT = [sb(f"sT{h}", [C, CH]) for h in range(2)]
        yb = [sb(f"yb{h}", [128, 2, CH]) for h in range(3)]
        YB = (0, 1, 0, 2)
        ps_y = [ctx.enter_context(nc.psum_tensor(f"ps_y{h}", [128, 2, CH], F32)) for h in range(2)]
        ps_t = [ctx.enter_context(nc.psum_tensor(f"ps_t{h}", [C, CH], F32)) for h in range(2)]
        ps_o = [ctx.enter_context(nc.psum_tensor(f"ps_o{h}", [128, 3, 128], F32)) for h in range(2)]

        params = sem("om_params")
        base_ready = sem("base_ready")
        win_loaded = sem("win_loaded")
        om_done = sem("om_done")
        om_read = sem("om_read")
        mod_ready = sem("mod_ready")
        sig_ready = sem("sig_ready")
        sig_used = sem("sig_used")
        step = sem("om_step")
        offsets_ready = sem("offsets_ready")
        handed = pair("handed")
        r_loaded = sem("r_loaded")
        gathered = [sem(f"gathered{s}") for s in range(RING)]
        first_corner = sem("first_corner")
        corner = sem("corner")
        blended = sem("blended")
        turned = sem("turned")
        copied = sem("copied")
        summed = sem("summed")
        evacuated = sem("evacuated")
        measured = sem("measured")
        stored = [sem(f"y_stored{h}") for h in range(3)]
        gate = sem("c_gate")
        SPLIT = TAPS // 2
        parts = ((0, SPLIT), (SPLIT, TAPS))
        TILE_STEPS = 11
        WINDOW_STEP = 4 * TILE_STEPS + 4
        block = ctx.enter_context(nc.Block())
        ends = [t0 + n for t0, n in BRANCHES]
        centre = 24
        conv_taps = sorted(range(49), key=lambda t: (t != centre, t))

        def columns(t):
            ky, kx = divmod(t, 7)
            if t == centre:
                return TAPS
            return 58 if 2 <= ky <= 4 and 2 <= kx <= 4 else 49

        @block.sync
        def _(sp):
            sp.dma_start(wom[:], w_om).then_inc(params, 16)
            sp.dma_start(base[:], base_om).then_inc(params, 16)
            sp.dma_start(P[:], bias_om.rearrange("(a k) t -> a k t", a=1).to_broadcast([128, 3, TAPS]))\
                .then_inc(params, 16)
            sp.dma_start(rowt[:], row_off).then_inc(params, 16)
            sp.dma_start(imgt[:], img_off).then_inc(params, 16)
            for h in range(3):
                sp.sem_inc(stored[h], 16)

            def load_window(n, kx):
                row = n * (CH // W) + (n >> 3) * (2 * PAD)
                rows = xn_dram[:, 0:HR, kx:kx + W] if isinstance(n, int) and n == 0 else \
                    xn_dram[:, bass.ds(row, HR), kx:kx + W]
                sp.dma_start(win[:, kx, :, :], rows).then_inc(win_loaded, 16)

            def hand(u):
                lo, hi = parts[u]
                sp.dma_start(idx[:, lo:hi, :], idx_next[:, lo:hi, :]).then_inc(handed[u], 16)
                sp.dma_start(wts[:, 16 * lo:16 * hi], flat(wts_next[:])[:, 16 * lo:16 * hi]).then_inc(handed[u], 16)

            def store(g, br):
                sp.wait_ge(evacuated, g * NBR + (br + 3))
                sp.dma_start(y_dram[bass.ds(g, 1), br, :, :, :].rearrange("g h p n -> (g p) h n"),
                             yb[YB[br]][:, :, :]).then_inc(stored[YB[br]], 16)

            for kx in range(7):
                load_window(0, kx)
            sp.dma_start(R[:], regw).then_inc(r_loaded, 16)
            sp.wait_ge(offsets_ready, 1)
            for u in range(2):
                hand(u)
            for kx in range(7):
                load_window(1, kx)
            with sp.Fori(0, NG) as g:
                sp.wait_ge(offsets_ready, g + 2)
                for u in range(2):
                    sp.wait_ge(blended, g * TAPS + parts[u][1] + RING)
                    hand(u)
                    for kx in range(6) if u == 0 else (6,):
                        if u == 0:
                            sp.wait_ge(blended, g * TAPS + (WINDOW_STEP + 2 * kx + RING))
                        load_window(g + 2, kx)
                        if kx == 3:
                            store(g, 0)
                for br in range(1, NBR):
                    store(g, br)
            for h in range(3):
                sp.wait_ge(stored[h], 16 + 16 * YB.count(h) * NG)
            for h in range(2):
                sp.wait_ge(handed[h], 32 * (NG + 1))
            sp.wait_ge(win_loaded, 7 * 16 * (NG + 2))

        @block.gpsimd
        def _(pool):
            with pool.Fori(0, NG) as g:
                for k in range(TAPS):
                    if k in (0, SPLIT):
                        pool.wait_ge(handed[k // SPLIT], g * 32 + 32)
                        pool.sem_inc(gate, 1)
                    pool.wait_ge(blended, g * TAPS + k + 1)
                    pool.sem_inc(gate, 1)
                    for j in range(4):
                        pool.indirect_dma_start(G[k % RING][:, j, :], None, table,
                                                bass.IndirectOffsetOnAxis(ap=idx[:, k, j:j + 1], axis=0))\
                            .then_inc(gathered[k % RING], 16)

        def groups(eng, body, offsets, after):
            for j in range(4):
                offsets(0, j)
            eng.sem_inc(gate, 1)
            with eng.Fori(0, NG) as g:
                eng.wait_ge(handed[0], g * 32 + 32)
                eng.sem_inc(gate, 1)
                for lo, hi, j in ((0, 2, 0), (2, 4, 1), (4, 5, None), (5, 6, 2), (6, 8, 3), (8, 9, None)):
                    if lo == 5:
                        eng.wait_ge(handed[1], g * 32 + 32)
                        eng.sem_inc(gate, 1)
                    with eng.Fori(lo, hi) as q:
                        body(g, q)
                    if j is not None:
                        offsets(g + 1, j)
                        eng.sem_inc(gate, 1)
                after(g, (0,))
                with eng.Fori(9, 10) as q:
                    body(g, q)
                after(g, (1, 2, 3))

        @block.scalar
        def _(act):
            act.sem_inc(evacuated, 2)

            def offsets(n, j):
                m = n * 4 + j
                act.wait_ge(mod_ready, m + 1)
                act.wait_ge(sig_used, m + 1)
                nc.scalar.activation(sg[:, :], P[:, 2, :], ACT.Sigmoid).then_inc(sig_ready, 1)

            def corner0(g, q, i):
                n = g * TAPS + q * RING + i
                act.wait_ge(gathered[i], (g * (TAPS // RING) + q) * 64 + 64)
                act.wait_ge(turned, n + 1)
                act.sem_inc(gate, 1)
                for j in range(4):
                    last = nc.scalar.activation(acc[i % 3][:, j, :], G[i][:, j, 0:C], ACT.Copy,
                                                scale=wts[:, bass.ds(q * (16 * RING) + (i * 16 + j * 4), 1)])
                last.then_inc(first_corner, 1)

            def copy_out(g, q, i):
                n = g * TAPS + q * RING + i
                act.wait_ge(turned, n + 4)
                act.wait_ge(summed, n + 1)
                nc.scalar.activation(sT[i % 2][:, :], ps_t[i % 2][:, :], ACT.Copy).then_inc(copied, 1)

            def body(g, q):
                corner0(g, q, 0)
                for i in range(1, RING):
                    corner0(g, q, i)
                    copy_out(g, q, i - 1)
                copy_out(g, q, RING - 1)

            def after(g, brs):
                for br in brs:
                    act.wait_ge(summed, g * TAPS + ends[br] + 2)
                    n = YB.count(YB[br])
                    act.wait_ge(stored[YB[br]], g * (16 * n) + 16 * (YB[:br].count(YB[br]) + 1))
                    act.wait_ge(measured, g * NBR + br + 1)
                    for half in range(2):
                        last = nc.scalar.activation(yb[YB[br]][:, half, :], ps_y[br % 2][:, half, :], ACT.Copy)
                    last.then_inc(evacuated, 1)

            groups(act, body, offsets, after)

        @block.vector
        def _(dve):
            dve.sem_inc(blended, RING)
            dve.sem_inc(measured, 2)
            dve.sem_inc(sig_used, 1)
            dve.wait_ge(params, 80)
            nc.vector.tensor_tensor(base[:], base[:], P[:], ALU.add).then_inc(base_ready, 1)
            dve.wait_ge(base_ready, 1)
            PER = 14

            def offsets(n, j):
                m = n * 4 + j
                st = Steps(dve, step, m * PER)
                dve.wait_ge(om_done, m + 1)
                st.then(nc.vector.tensor_tensor(P[:], ps_o[j % 2][:, :, 0:TAPS], base[:], ALU.add))
                dve.sem_inc(om_read, 1)
                dve.sem_inc(mod_ready, 1)
                col = lambda t: t[:, m:m + 1] if isinstance(m, int) else t[:, bass.ds(m, 1)]
                st.then(nc.vector.tensor_scalar(P[:, 0, :], P[:, 0, :], col(rowt), 0.0, ALU.add, ALU.max))
                st.then(nc.vector.tensor_scalar(P[:, 0:2, :], P[:, 0:2, :], 0.0, float(H + 2), ALU.max, ALU.min))
                st.then(nc.vector.tensor_copy(pi[:], P[:, 0:2, :]))
                st.then(nc.vector.tensor_copy(fl[:], pi[:]))
                st.then(nc.vector.tensor_tensor(gt[:], fl[:], P[:, 0:2, :], ALU.is_gt))
                st.then(nc.vector.tensor_tensor(fl[:], fl[:], gt[:], ALU.subtract))
                st.then(nc.vector.tensor_tensor(fr[:], P[:, 0:2, :], fl[:], ALU.subtract))
                st.then(nc.vector.scalar_tensor_tensor(rowf, fl[:, 0, :], float(TS), fl[:, 1, :], ALU.mult, ALU.add))
                if j == 0 and not isinstance(n, int):
                    for u in range(2):
                        dve.wait_ge(handed[u], n * 32)
                st.then(nc.vector.tensor_scalar(idx_next[:, :, j], rowf, col(imgt), None, ALU.add))
                dve.wait_ge(sig_ready, m + 1)
                st.then(nc.vector.scalar_tensor_tensor(a[:, 1, :], sg[:], 2.0, fr[:, 0, :], ALU.mult, ALU.mult))
                st.then(nc.vector.scalar_tensor_tensor(a[:, 0, :], sg[:], 2.0, a[:, 1, :], ALU.mult, ALU.subtract))
                dve.sem_inc(sig_used, 1)
                for r in range(2):
                    last = nc.vector.tensor_tensor(wts_next[:, :, j, r, 1], a[:, r, :], fr[:, 1, :], ALU.mult)
                st.then(last)
                for r in range(2):
                    last = nc.vector.tensor_tensor(wts_next[:, :, j, r, 0], a[:, r, :], wts_next[:, :, j, r, 1],
                                                   ALU.subtract)
                st.then(last)
                assert st.n == PER
                if j == 3:
                    dve.sem_inc(offsets_ready, 1)

            def body(g, q):
                for i in range(RING):
                    n = g * TAPS + q * RING + i
                    dve.wait_ge(first_corner, n + 1)
                    for c in range(1, 4):
                        if c > 1:
                            dve.wait_ge(corner, n * 2 + c - 1)
                        for j in range(4):
                            last = nc.vector.scalar_tensor_tensor(
                                acc[i % 3][:, j, :], G[i][:, j, c * C:(c + 1) * C],
                                wts[:, bass.ds(q * (16 * RING) + (i * 16 + j * 4 + c), 1)], acc[i % 3][:, j, :],
                                ALU.mult, ALU.add)
                        last.then_inc(corner if c < 3 else blended, 1)

            def after(g, brs):
                for br in brs:
                    dve.wait_ge(evacuated, g * NBR + br + 3)
                    dve.sem_inc(gate, 1)
                    for half in range(2):
                        last = nc.vector.bn_stats(ystats[:, 2 * br + half, bass.ds(g * 6, 6)],
                                                  yb[YB[br]][:, half, :])
                    last.then_inc(measured, 1)

            groups(dve, body, offsets, after)
            dve.wait_ge(measured, NBR * NG + 2)

        @block.tensor
        def _(pe):
            pe.sem_inc(turned, 3)
            pe.sem_inc(summed, 2)
            pe.sem_inc(om_read, 2)
            pe.wait_ge(params, 80)

            def convolve(n, j, lo, hi):
                m = n * 4 + j
                if lo == 0:
                    if j == 0:
                        pe.wait_ge(win_loaded, n * 112 + 112)
                    pe.wait_ge(om_read, m + 1)
                for t in conv_taps[lo:hi]:
                    ky, kx = divmod(t, 7)
                    last = nc.tensor.matmul(ps_o[j % 2][:, :, 0:columns(t)],
                                            win[:, kx, 2 * j + ky:2 * j + ky + 2, :].rearrange("c y x -> c (y x)"),
                                            wom[:, t, :, 0:columns(t)], start=(t == centre), stop=(t == conv_taps[-1]),
                                            skip_group_check=True)
                if hi == 49:
                    last.then_inc(om_done, 1)

            for j in range(4):
                convolve(0, j, 0, 49)
            pe.wait_ge(r_loaded, 16)
            with pe.Fori(0, NG) as g:

                def turn(k):
                    pe.wait_ge(blended, g * TAPS + k + 1 + RING)
                    for j in range(4):
                        last = nc.tensor.transpose(ps_t[k % 2][:, 128 * j:128 * j + 128], acc[k % 3][:, j, :], ident[:, :])
                    last.then_inc(turned, 1)

                def contract(k):
                    br = [k < e for e in ends].index(True)
                    t0, n = BRANCHES[br]
                    pe.wait_ge(copied, g * TAPS + k + 1)
                    if k == t0:
                        pe.wait_ge(evacuated, g * NBR + br + 1)
                    for half in range(2):
                        last = nc.tensor.matmul(ps_y[br % 2][:, half, :], R[:, k, 128 * half:128 * half + 128],
                                                sT[k % 2][:, :], start=(k == t0), stop=(k == ends[br] - 1))
                    last.then_inc(summed, 1)

                for k in range(TAPS):
                    turn(k)
                    if k:
                        contract(k - 1)
                    j, i = divmod(k, TILE_STEPS)
                    if j < 4 and i:
                        share = lambda i: 49 * i // (TILE_STEPS - 1)
                        convolve(g + 1, j, share(i - 1), share(i))
                contract(TAPS - 1)


def group_affine(dve, act_sem, st, sq, var, sd, a, b, gm, gamma, beta, ready, nc):
    st.then(nc.vector.tensor_tensor(sq, gm[:, 0, :], gm[:, 0, :], ALU.mult))
    st.then(nc.vector.tensor_tensor(var, gm[:, 1, :], sq, ALU.subtract))
    st.then(nc.vector.tensor_scalar(var, var, 0.0, None, ALU.max))
    dve.sem_inc(ready, 1)
    dve.wait_ge(act_sem, 1)
    st.then(nc.vector.reciprocal(sd, sd))
    st.then(nc.vector.tensor_tensor(a, gamma, sd, ALU.mult))
    st.then(nc.vector.tensor_tensor(b, gm[:, 0, :], a, ALU.mult))
    st.then(nc.vector.tensor_tensor(b, beta, b, ALU.subtract))


def stage_fuse(nc, y_dram, ystats, xsum, pool_w, fuse_w, gnp, gnf, blk16, blk8, eps5, fu, fa, fb):
    ctx = ExitStack()
    with ctx:
        sb = lambda name, shape, dt=F32: ctx.enter_context(nc.sbuf_tensor(name, shape, dt))
        sem = lambda name: ctx.enter_context(nc.semaphore(name))
        pw = sb("pw", [C, O])
        fw = sb("fw", [128, NFC, C])
        gp = sb("gp", [128, 2, B, NFC])
        gf = sb("gf", [C, 2, B])
        mv = sb("mv", [128, B, 2 * NBR, 2])
        me = sb("me", [128, 2, B * NFC])
        gm = sb("gm", [128, 2, B * NFC])
        sq = sb("sq", [128, B * NFC])
        var = sb("var", [128, B * NFC])
        sd = sb("sd", [128, B * NFC])
        ya = sb("ya", [128, B * NFC])
        ybb = sb("ybb", [128, B * NFC])
        xmean = sb("xmean", [C, B])
        y5 = sb("y5", [128, B, 2])
        z5 = sb("z5", [128, 2, B])
        bias5 = sb("bias5", [C, B])
        yin = [sb(f"yin{h}", [128, 2 * NBR, CH]) for h in range(2)]
        fstats = sb("fstats", [C, NG * 6])
        fmv = sb("fmv", [C, B, 2])
        fme = sb("fme", [C, 2, B])
        fgm = sb("fgm", [C, 2, B])
        fsq = sb("fsq", [C, B])
        fvar = sb("fvar", [C, B])
        fsd = sb("fsd", [C, B])
        ps_s = ctx.enter_context(nc.psum_tensor("ps_s", [128, 2, 64], F32))
        ps_f = [ctx.enter_context(nc.psum_tensor(f"ps_f{h}", [C, CH], F32)) for h in range(2)]
        params = sem("f_params")
        step = sem("f_step")
        xm_ready = sem("xm_ready")
        y5_ready = sem("y5_ready")
        me_ready = sem("me_ready")
        gm_ready = sem("gm_ready")
        var_ready = sem("f_var_ready")
        sd_ready = sem("f_sd_ready")
        ab_ready = sem("ab_ready")
        z5_ready = sem("z5_ready")
        b5_summed = sem("b5_summed")
        b5_ready = sem("b5_ready")
        y_loaded = [sem(f"y_loaded{h}") for h in range(2)]
        z_ready = [sem(f"z_ready{h}") for h in range(2)]
        fused = [sem(f"fused{h}") for h in range(2)]
        fu_ready = [sem(f"fu_ready{h}") for h in range(2)]
        fu_measured = sem("fu_measured")
        fme_ready = sem("fme_ready")
        fgm_ready = sem("fgm_ready")
        fvar_ready = sem("fvar_ready")
        fsd_ready = sem("fsd_ready")
        gate = sem("f_gate")
        block = ctx.enter_context(nc.Block())
        view = lambda t: t.rearrange("p (b n) -> p b n", b=B)

        @block.sync
        def _(sp):
            sp.dma_start(pw[:], pool_w).then_inc(params, 16)
            sp.dma_start(fw[:], fuse_w).then_inc(params, 16)
            sp.dma_start(gp[:], gnp).then_inc(params, 16)
            sp.dma_start(gf[:], gnf).then_inc(params, 16)
            with sp.Fori(0, NG // 2) as i:
                for h in range(2):
                    sp.wait_ge(fused[h], i + 1)
                    sp.dma_start(yin[h][:], y_dram[bass.ds(i * 2 + h, 1), :, :, :, :]
                                 .rearrange("g b h p n -> (g p) (b h) n")).then_inc(y_loaded[h], 16)

        @block.tensor
        def _(pe):
            for h in range(2):
                pe.sem_inc(fused[h], 1)
            pe.wait_ge(params, 64)
            pe.wait_ge(xm_ready, 1)
            for half in range(2):
                last = nc.tensor.matmul(ps_s[:, half, 0:B], pw[:, 128 * half:128 * half + 128], xmean[:, :],
                                        start=True, stop=True)
            last.then_inc(y5_ready, 1)
            pe.wait_ge(me_ready, 1)
            nc.tensor.matmul(ps_s[:, 0, 0:2 * B * NFC], blk16[:, :], flat(me[:]), start=True, stop=True)\
                .then_inc(gm_ready, 1)
            pe.wait_ge(z5_ready, 1)
            for half in range(2):
                last = nc.tensor.matmul(ps_s[:, 1, 0:B], fw[:, 2 * NBR + half, :], z5[:, half, :],
                                        start=(half == 0), stop=(half == 1))
            last.then_inc(b5_summed, 1)
            with pe.Fori(0, NG // 2) as i:
                for h in range(2):
                    pe.wait_ge(z_ready[h], i + 1)
                    pe.wait_ge(fu_ready[h], i + 1)
                    for n in range(2 * NBR):
                        last = nc.tensor.matmul(ps_f[h][:, :], fw[:, n, :], yin[h][:, n, :],
                                                start=(n == 0), stop=(n == 2 * NBR - 1))
                    last.then_inc(fused[h], 1)
            pe.wait_ge(fme_ready, 1)
            nc.tensor.matmul(ps_s[:, 0, 0:2 * B], blk8[:, :], flat(fme[:]), start=True, stop=True).then_inc(fgm_ready, 1)

        @block.scalar
        def _(act):
            for h in range(2):
                act.sem_inc(fu_ready[h], 1)
            act.wait_ge(var_ready, 1)
            nc.scalar.activation(sd[:], var[:], ACT.Sqrt, bias=eps5[:, 0:1]).then_inc(sd_ready, 1)
            act.wait_ge(ab_ready, 1)
            act.wait_ge(b5_ready, 1)
            act.sem_inc(gate, 1)
            with act.Fori(0, B) as b:
                with act.Fori(0, GI // 2) as i:
                    k = b * (GI // 2) + i
                    for h in range(2):
                        act.wait_ge(y_loaded[h], k * 16 + 16)
                        act.sem_inc(gate, 1)
                        for n in range(2 * NBR):
                            last = nc.scalar.activation(yin[h][:, n, :], yin[h][:, n, :], ACT.Relu,
                                                        bias=ybb[:, bass.ds(b * NFC + n, 1)],
                                                        scale=ya[:, bass.ds(b * NFC + n, 1)])
                        last.then_inc(z_ready[h], 1)
                    for h in range(2):
                        act.wait_ge(fused[h], k + 2)
                        act.sem_inc(gate, 1)
                        nc.scalar.activation(fu[:, bass.ds(b * HW + i * (2 * CH) + h * CH, CH)], ps_f[h][:, :],
                                             ACT.Identity, bias=bias5[:, bass.ds(b, 1)]).then_inc(fu_ready[h], 1)
            act.wait_ge(fvar_ready, 1)
            nc.scalar.activation(fsd[:], fvar[:], ACT.Sqrt, bias=eps5[:, 0:1]).then_inc(fsd_ready, 1)

        @block.vector
        def _(dve):
            st = Steps(dve, step)
            nc.vector.tensor_scalar(xmean[:], xsum[:], 1.0 / HW, None, ALU.mult).then_inc(xm_ready, 1)
            for b in range(B):
                for n in range(2 * NBR):
                    last = nc.vector.bn_aggr(mv[:, b, n, :], ystats[:, n, b * GI * 6:(b + 1) * GI * 6])
            st.then(last)
            m0, m1 = view(me[:, 0, :])[:, :, 0:2 * NBR], view(me[:, 1, :])[:, :, 0:2 * NBR]
            nc.vector.tensor_copy(m0, mv[:, :, :, 0])
            st.then(nc.vector.tensor_tensor(m1, mv[:, :, :, 0], mv[:, :, :, 0], ALU.mult))
            nc.vector.tensor_tensor(m1, m1, mv[:, :, :, 1], ALU.add)
            dve.wait_ge(y5_ready, 1)
            st.then(nc.vector.tensor_copy(y5[:], ps_s[:, :, 0:B].rearrange("p h b -> p b h")))
            nc.vector.tensor_copy(view(me[:, 0, :])[:, :, 2 * NBR:], y5[:])
            nc.vector.tensor_tensor(view(me[:, 1, :])[:, :, 2 * NBR:], y5[:], y5[:], ALU.mult).then_inc(me_ready, 1)
            dve.wait_ge(gm_ready, 1)
            st.then(nc.vector.tensor_copy(flat(gm[:]), ps_s[:, 0, 0:2 * B * NFC]))
            dve.wait_ge(params, 64)
            group_affine(dve, sd_ready, st, sq[:], var[:], sd[:], ya[:], ybb[:], gm, flat(gp[:, 0, :, :]),
                         flat(gp[:, 1, :, :]), var_ready, nc)
            dve.sem_inc(ab_ready, 1)
            z5v = z5[:].rearrange("p h b -> p b h")
            st.then(nc.vector.tensor_tensor(z5v, y5[:], view(ya[:])[:, :, 2 * NBR:], ALU.mult))
            st.then(nc.vector.tensor_tensor(z5v, z5v, view(ybb[:])[:, :, 2 * NBR:], ALU.add))
            nc.vector.tensor_scalar(z5[:], z5[:], 0.0, None, ALU.max).then_inc(z5_ready, 1)
            dve.wait_ge(b5_summed, 1)
            nc.vector.tensor_copy(bias5[:], ps_s[:, 1, 0:B]).then_inc(b5_ready, 1)
            with dve.Fori(0, NG // 2) as i:
                for h in range(2):
                    dve.wait_ge(fu_ready[h], i + 2)
                    dve.sem_inc(gate, 1)
                    nc.vector.bn_stats(fstats[:, bass.ds(i * 12 + h * 6, 6)],
                                       fu[:, bass.ds(i * (2 * CH) + h * CH, CH)]).then_inc(fu_measured, 1)
            dve.wait_ge(fu_measured, NG)
            for b in range(B):
                last = nc.vector.bn_aggr(fmv[:, b, :], fstats[:, b * GI * 6:(b + 1) * GI * 6])
            st.then(last)
            nc.vector.tensor_copy(fme[:, 0, :], fmv[:, :, 0])
            st.then(nc.vector.tensor_tensor(fme[:, 1, :], fmv[:, :, 0], fmv[:, :, 0], ALU.mult))
            nc.vector.tensor_tensor(fme[:, 1, :], fme[:, 1, :], fmv[:, :, 1], ALU.add).then_inc(fme_ready, 1)
            dve.wait_ge(fgm_ready, 1)
            st.then(nc.vector.tensor_copy(flat(fgm[:]), ps_s[:, 0, 0:2 * B]))
            group_affine(dve, fsd_ready, st, fsq[:], fvar[:], fsd[:], fa[:], fb[:], fgm, gf[:, 0, :], gf[:, 1, :],
                         fvar_ready, nc)


def stage_sum(nc, x, fu, fa, fb, accum):
    ctx = ExitStack()
    with ctx:
        sb = lambda name, shape, dt=F32: ctx.enter_context(nc.sbuf_tensor(name, shape, dt))
        sem = lambda name: ctx.enter_context(nc.semaphore(name))
        xg = [sb(f"t_xg{h}", [C, CH]) for h in range(2)]
        rb = [sb(f"t_rb{h}", [C, CH]) for h in range(2)]
        pair = lambda name: [sem(f"{name}{h}") for h in range(2)]
        x_loaded = pair("tx_loaded")
        relu_ready = pair("relu_ready")
        t_added = pair("t_added")
        gate = sem("t_gate")
        block = ctx.enter_context(nc.Block())
        NH = GI // 2

        @block.sync
        def _(sp):
            with sp.Fori(0, B) as b:
                with sp.Fori(0, NH) as i:
                    for h in range(2):
                        sp.wait_ge(t_added[h], b * NH + i + 1)
                        sp.dma_start(xg[h][:, :], x[bass.ds(b, 1), :, bass.ds(i * (2 * CH) + h * CH, CH)]
                                     .rearrange("b c n -> (b c) n")).then_inc(x_loaded[h], 16)

        @block.scalar
        def _(act):
            with act.Fori(0, B) as b:
                with act.Fori(0, NH) as i:
                    for h in range(2):
                        act.wait_ge(t_added[h], b * NH + i + 1)
                        act.sem_inc(gate, 1)
                        nc.scalar.activation(rb[h][:, :], fu[:, bass.ds(b * HW + i * (2 * CH) + h * CH, CH)], ACT.Relu,
                                             bias=fb[:, bass.ds(b, 1)], scale=fa[:, bass.ds(b, 1)])\
                            .then_inc(relu_ready[h], 1)

        @block.vector
        def _(dve):
            for h in range(2):
                dve.sem_inc(t_added[h], 1)
            with dve.Fori(0, B) as b:
                with dve.Fori(0, NH) as i:
                    for h in range(2):
                        k = b * NH + i
                        dve.wait_ge(x_loaded[h], k * 16 + 16)
                        dve.wait_ge(relu_ready[h], k + 1)
                        parity = lambda t: t[:, :].rearrange("p (n a) -> p a n", a=2)
                        nc.vector.tensor_tensor(
                            accum[:, bass.ds(b * 2, 2), bass.ds(i * CH + h * (CH // 2), CH // 2)],
                            parity(rb[h]), parity(xg[h]), ALU.add).then_inc(t_added[h], 1)


def stage_tokens(nc, ident, eps5, accum, uT, dft, dft_edge, spec_dram):
    ctx = ExitStack()
    with ctx:
        sb = lambda name, shape, dt=F32: ctx.enter_context(nc.sbuf_tensor(name, shape, dt))
        sem = lambda name: ctx.enter_context(nc.semaphore(name))
        tch = [sb(f"tch{h}", [C, 16 * NB]) for h in range(2)]
        un = [sb(f"un{h}", [128, 4, C]) for h in range(2)]
        stats = [sb(f"t_stats{h}", [128, 4, 6]) for h in range(2)]
        mv = [sb(f"t_mv{h}", [128, 4, 2]) for h in range(2)]
        sd = [sb(f"t_sd{h}", [128, 4]) for h in range(2)]
        rs = [sb(f"t_rs{h}", [128, 4]) for h in range(2)]
        fwd = sb("fwd", [128, 4 * 2 * NF])
        fwd_edge = sb("fwd_edge", [128, 2 * NF])
        spec = sb("spec", [C, NF, B, 2, 2, EX])
        ps_x = [ctx.enter_context(nc.psum_tensor(f"ps_tx{h}", [128, 4, C], F32)) for h in range(2)]
        ps_n = ctx.enter_context(nc.psum_tensor("ps_tn", [C, CH], F32))
        ps_d = [ctx.enter_context(nc.psum_tensor(f"ps_td{h}", [C, 2, CH], F32)) for h in range(2)]
        ps_e = ctx.enter_context(nc.psum_tensor("ps_te", [C, 2 * NF], F32))
        pair = lambda name: [sem(f"{name}{h}") for h in range(2)]
        params = sem("t_params")
        t_copied = pair("t_copied")
        t_turned = pair("t_turned")
        var_ready = pair("tvar_ready")
        sd_ready = pair("tsd_ready")
        u_ready = pair("u_ready")
        u_turned = sem("u_turned")
        uT_ready = sem("uT_ready")
        transformed = pair("transformed")
        spec_ready = pair("spec_ready")
        spec_stored = sem("spec_stored")
        edge_zeroed = sem("edge_zeroed")
        step = sem("t_step")
        gate = sem("t_gate")
        block = ctx.enter_context(nc.Block())
        HB = NG // 2
        blocks = lambda bp: accum[:, bass.ds(bp, 1), :].rearrange("c o (n s) -> c (o n) s", s=BS)

        @block.sync
        def _(sp):
            sp.dma_start(fwd[:], dft).then_inc(params, 16)
            sp.dma_start(fwd_edge[:], dft_edge).then_inc(params, 16)
            for h in range(2):
                sp.wait_ge(spec_ready[h], HB + 1)
            sp.dma_start(spec_dram.rearrange("f d n -> d f n"), spec[:].rearrange("d f b q r s -> d f (b q r s)"))\
                .then_inc(spec_stored, 16)
            sp.wait_ge(spec_stored, 16)

        @block.gpsimd
        def _(pool):
            pool.memset(uT[:, :, 0:1], 0.0).then_inc(edge_zeroed, 1)
            with pool.Fori(0, 2 * B) as bp:
                with pool.Fori(0, 2) as i:
                    for h in range(2):
                        pool.wait_ge(t_turned[h], bp * 2 + i + 1)
                        pool.sem_inc(gate, 1)
                        nc.gpsimd.tensor_copy(tch[h][:, :].rearrange("c (s n) -> c n s", n=NB),
                                              blocks(bp)[:, :, bass.ds(i * 32 + h * 16, 16)]).then_inc(t_copied[h], 1)

        @block.scalar
        def _(act):
            act.sem_inc(uT_ready, 1)
            for h in range(2):
                act.sem_inc(spec_ready[h], 1)
            act.wait_ge(edge_zeroed, 1)
            with act.Fori(0, B) as b:
                with act.Fori(0, 2) as p:
                    with act.Fori(0, 2) as i:
                        k = b * 4 + p * 2 + i
                        for h in range(2):
                            act.wait_ge(var_ready[h], k + 1)
                            nc.scalar.activation(sd[h][:, :], mv[h][:, :, 1], ACT.Sqrt, bias=eps5[:, 0:1])\
                                .then_inc(sd_ready[h], 1)
                        for h in range(2):
                            act.wait_ge(u_turned, k * 2 + (h + 2))
                            act.sem_inc(gate, 1)
                            nc.scalar.activation(
                                uT[:, bass.ds(b * 2 + p, 1), 1:1 + HALF].rearrange("c o (n s) -> c (o n) s", s=BS)
                                [:, :, bass.ds(i * 32 + h * 16, 16)],
                                ps_n[:, :].rearrange("c (s n) -> c n s", n=NB), ACT.Copy).then_inc(uT_ready, 1)
                            act.wait_ge(transformed[h], k + 2)
                            act.sem_inc(gate, 1)
                            half = lambda lo, n: spec[:, :, bass.ds(b, 1), bass.ds(p, 1), :, bass.ds(lo, n)]\
                                .rearrange("d f b q r s -> d s r (f b q)")
                            for q in range(2):
                                last = nc.scalar.activation(
                                    half(i * -32 + (48 - 16 * h + 8 * q), 8),
                                    ps_d[h][:, q, :].rearrange("d (s r f) -> d s r f", r=2, f=NF), ACT.Copy)
                            if h == 1:
                                last = nc.scalar.activation(
                                    spec[:, :, bass.ds(b, 1), bass.ds(p, 1), :, BS:EX]
                                    .rearrange("d f b q r s -> d (r s) (f b q)"),
                                    ps_e[:, :].rearrange("d (r f) -> d r f", r=2), ACT.Copy)
                            last.then_inc(spec_ready[h], 1)
            act.wait_ge(uT_ready, NG + 1)

        @block.tensor
        def _(pe):
            pe.sem_inc(u_turned, 1)
            for h in range(2):
                pe.sem_inc(t_turned[h], 1)
                pe.sem_inc(transformed[h], 1)
            pe.wait_ge(params, 32)
            with pe.Fori(0, HB) as k:
                for h in range(2):
                    pe.wait_ge(t_copied[h], k + 1)
                    pe.wait_ge(u_ready[h], k + 1)
                    for j in range(4):
                        last = nc.tensor.transpose(ps_x[h][:, j, :], tch[h][:, 128 * j:128 * j + 128], ident[:, :])
                    last.then_inc(t_turned[h], 1)
                for h in range(2):
                    pe.wait_ge(u_ready[h], k + 2)
                    pe.wait_ge(uT_ready, k * 2 + (h + 1))
                    for j in range(4):
                        last = nc.tensor.transpose(ps_n[:, 128 * j:128 * j + 128], un[h][:, j, :], ident[:, :])
                    last.then_inc(u_turned, 1)
                    pe.wait_ge(spec_ready[h], k + 1)
                    for j in range(4):
                        o = ps_d[h][:, (3 - j) // 2, 256 * ((3 - j) % 2):256 * ((3 - j) % 2) + 256]
                        last = nc.tensor.matmul(o, un[h][:, j, :], fwd[:, :], start=True, stop=True)
                    if h == 1:
                        last = nc.tensor.matmul(ps_e[:, :], un[h][:, 3, :], fwd_edge[:, :], start=True, stop=True)
                    last.then_inc(transformed[h], 1)

        @block.vector
        def _(dve):
            for h in range(2):
                dve.sem_inc(u_ready[h], 1)
            with dve.Fori(0, HB) as k:
                st = Steps(dve, step, k * 4)
                for h in range(2):
                    dve.wait_ge(t_turned[h], k + 2)
                    for j in range(4):
                        last = nc.vector.bn_stats(stats[h][:, j, :], ps_x[h][:, j, :])
                    st.then(last)
                    dve.sem_inc(gate, 1)
                    for j in range(4):
                        last = nc.vector.bn_aggr(mv[h][:, j, :], stats[h][:, j, :])
                    last.then_inc(var_ready[h], 1)
                for h in range(2):
                    dve.wait_ge(sd_ready[h], k + 1)
                    st.then(nc.vector.reciprocal(rs[h][:, :], sd[h][:, :]))
                    dve.wait_ge(transformed[h], k + 1)
                    for j in range(4):
                        last = nc.vector.tensor_scalar(un[h][:, j, :], ps_x[h][:, j, :], mv[h][:, j, 0:1],
                                                       rs[h][:, j:j + 1], ALU.subtract, ALU.mult)
                    last.then_inc(u_ready[h], 1)


def segments(r):
    return ((0, 256, 0), (256, 512, 1)) if r == 0 else ((0, 512, min(r + 1, SEG - 1)),)


def stage_mixtures(nc, phi, dft_taps, m_phi, m_u, sigma, logw, gumbel, accum, uT, mh, ml, hot, kern_dram):
    ctx = ExitStack()
    with ctx:
        sb = lambda name, shape, dt=F32: ctx.enter_context(nc.sbuf_tensor(name, shape, dt))
        sem = lambda name: ctx.enter_context(nc.semaphore(name))
        lw = sb("lw", [128, SEG])
        gb = sb("gb", [128, SEG])
        sm = sb("sm", [128, 4])
        ys = sb("ys", [128, SEG])
        wi = sb("wi", [128, SEG])
        sg = sb("sigma_b", [128, KF])
        ws = sb("ws", [128, KF, SEG])
        mu = sb("mu", [C, SEG, 3, C])
        mus = sb("mus", [C, 3, SEG, C])
        mr = [sb(f"mr{h}", [C, 2, SEG, C]) for h in range(2)]
        mt = sb("mt", [C, 2, SEG, C])
        ms = sb("ms", [C, 2, C])
        windows = sb("windows", [NB, 2 * KF, 2 * BS])
        taps_dft = sb("taps_dft", [NB, 4 * NF])
        kern = sb("kern", [128, 2 * KF, 2 * BS])
        ps_m = [ctx.enter_context(nc.psum_tensor(f"ps_m{q}", [C, CH], F32)) for q in range(2)]
        ps_k = [ctx.enter_context(nc.psum_tensor(f"ps_k{q}", [128, CH], F32)) for q in range(2)]
        pair = lambda name: [sem(f"{name}{h}") for h in range(2)]
        params = sem("s_params")
        phi_loaded = sem("phi_loaded")
        step = sem("s_step")
        z_ready = sem("s_z_ready")
        e_ready = sem("s_e_ready")
        sig_rooted = sem("sig_rooted")
        mus_ready = sem("mus_ready")
        m_loaded = pair("m_loaded")
        m_used = pair("m_used")
        m_rounded = sem("m_rounded")
        ms_ready = sem("ms_ready")
        mixed = sem("mixed")
        added = sem("added")
        k_done = sem("k_done")
        k_copied = sem("k_copied")
        k_stored = sem("k_stored")
        gate = sem("s_gate")
        block = ctx.enter_context(nc.Block())
        regions = [(b, p, r) for b in range(B) for p in range(2) for r in range(4)]
        NR = len(regions)
        PADC = HALF + BS
        NK = 2 * KF * 2 * BS // CH

        @block.sync
        def _(sp):
            sp.dma_start(taps_dft[:], dft_taps).then_inc(phi_loaded, 16)
            sp.dma_start(windows[:], bass.AP(tensor=phi.tensor, offset=0, ap=[[BS, NB], [PADC, 2 * KF], [1, 2 * BS]]))\
                .then_inc(phi_loaded, 16)
            one = lambda t, n: t.rearrange("(a k) -> a k", a=1).to_broadcast([128, n])
            sp.dma_start(lw[:], one(logw, SEG)).then_inc(params, 16)
            sp.dma_start(gb[:], one(gumbel, SEG)).then_inc(params, 16)
            sp.dma_start(sg[:], one(sigma, KF)).then_inc(params, 16)
            sp.dma_start(mu[:], m_u).then_inc(params, 16)
            with sp.Fori(0, KF // 2) as i:
                for h in range(2):
                    sp.wait_ge(m_used[h], i + 1)
                    sp.dma_start(mr[h][:], m_phi[bass.ds(i * 2 + h, 1), :, :, :, :].rearrange("k d s i e -> (k d) s i e"))\
                        .then_inc(m_loaded[h], 16)
            sp.wait_ge(k_copied, NK)
            sp.dma_start(kern_dram, kern[:].rearrange("p k n -> p (k n)")).then_inc(k_stored, 16)
            sp.wait_ge(k_stored, 16)

        @block.scalar
        def _(act):
            act.wait_ge(params, 64)
            act.wait_ge(z_ready, 1)
            nc.scalar.activation(ys[:], lw[:], ACT.Exp, bias=sm[:, 1:2]).then_inc(e_ready, 1)
            nc.scalar.activation(sg[:], sg[:], ACT.Sqrt).then_inc(sig_rooted, 1)
            act.wait_ge(sig_rooted, 1)
            nc.scalar.activation(sg[:], sg[:], ACT.Sqrt).then_inc(sig_rooted, 1)
            for n in range(NK):
                act.wait_ge(k_done, n + 1)
                nc.scalar.activation(flat(kern[:])[:, n * CH:(n + 1) * CH], ps_k[n % 2][:, :], ACT.Copy).then_inc(k_copied, 1)
            act.sem_inc(m_rounded, 1)
            with act.Fori(0, KF) as k:
                act.wait_ge(ms_ready, k + 1)
                act.sem_inc(gate, 1)
                nc.scalar.activation(mh[:, :, bass.ds(k, 1), :].rearrange("d p k e -> d p (k e)"), ms[:, :, :], ACT.Copy)\
                    .then_inc(m_rounded, 1)

        @block.vector
        def _(dve):
            dve.sem_inc(added, 2)
            for h in range(2):
                dve.sem_inc(m_used[h], 1)
            st = Steps(dve, step)
            dve.wait_ge(params, 64)
            st.then(nc.vector.tensor_tensor(lw[:], lw[:], gb[:], ALU.add))
            st.then(nc.vector.tensor_reduce(sm[:, 0:1], lw[:], AX.X, ALU.max))
            nc.vector.tensor_scalar(sm[:, 1:2], sm[:, 0:1], -1.0, None, ALU.mult).then_inc(z_ready, 1)
            dve.wait_ge(e_ready, 1)
            st.then(nc.vector.tensor_reduce(sm[:, 2:3], ys[:], AX.X, ALU.add))
            st.then(nc.vector.reciprocal(sm[:, 3:4], sm[:, 2:3]))
            st.then(nc.vector.tensor_scalar(ys[:], ys[:], sm[:, 3:4], None, ALU.mult))
            st.then(nc.vector.tensor_reduce(sm[:, 0:1], ys[:], AX.X, ALU.max))
            st.then(nc.vector.tensor_scalar(hot[:], ys[:], sm[:, 0:1], None, ALU.is_ge))
            st.then(nc.vector.tensor_scalar(sm[:, 2:3], sm[:, 3:4], 0.0, 1.0, ALU.mult, ALU.add))
            for i in range(SEG):
                st.then(nc.vector.tensor_tensor(hot[:, i:i + 1], hot[:, i:i + 1], sm[:, 2:3], ALU.mult))
                st.then(nc.vector.tensor_tensor(sm[:, 2:3], sm[:, 2:3], hot[:, i:i + 1], ALU.subtract))
            st.then(nc.vector.tensor_tensor(wi[:], hot[:], ys[:], ALU.subtract))
            st.then(nc.vector.tensor_tensor(wi[:], wi[:], ys[:], ALU.add))
            dve.wait_ge(sig_rooted, 2)
            for i in range(SEG):
                last = nc.vector.tensor_scalar(ws[:, :, i], sg[:, :], wi[:, i:i + 1], None, ALU.mult)
            st.then(last)
            st.then(nc.vector.tensor_scalar(mus[:, :, SEG - 1, :], mu[:, 0, :, :], wi[:, 0:1], None, ALU.mult))
            for i in range(1, SEG):
                ins = nc.vector.scalar_tensor_tensor(mus[:, :, SEG - 1 - i, :], mu[:, i, :, :], wi[:, i:i + 1],
                                                     mus[:, :, SEG - i, :], ALU.mult, ALU.add)
                if i < SEG - 1:
                    st.then(ins)
                else:
                    ins.then_inc(mus_ready, 1)
            for n, (b, p, r) in enumerate(regions):
                dve.wait_ge(mixed, n + 1)
                acc = accum[:, 2 * b + p, CH * r:CH * r + CH]
                nc.vector.tensor_tensor(acc, acc, ps_m[n % 2][:, :], ALU.add).then_inc(added, 1)
            base = st.n
            PER = 2 * (1 + SEG - 1)
            with dve.Fori(0, KF // 2) as i:
                st = Steps(dve, step, i * PER + base)
                for h in range(2):
                    k = i * 2 + h
                    dve.wait_ge(m_loaded[h], i * 16 + 16)
                    nc.vector.tensor_tensor(mt[:, 0, :, :], mr[h][:, 0, :, :], mr[h][:, 1, :, :], ALU.add)
                    st.then(nc.vector.tensor_tensor(mt[:, 1, :, :], mr[h][:, 0, :, :], mr[h][:, 1, :, :], ALU.subtract))
                    dve.sem_inc(m_used[h], 1)
                    dve.wait_ge(m_rounded, k + 1)
                    for s in range(SEG):
                        w = ws[:].rearrange("p k s -> p (k s)")[:, bass.ds(i * (2 * SEG) + (h * SEG + s), 1)]
                        if s == 0:
                            ins = nc.vector.tensor_scalar(ms[:, :, :], mt[:, :, 0, :], w, None, ALU.mult)
                        else:
                            ins = nc.vector.scalar_tensor_tensor(ms[:, :, :], mt[:, :, s, :], w, ms[:, :, :],
                                                                 ALU.mult, ALU.add)
                        if s < SEG - 1:
                            st.then(ins)
                    ins.then_inc(ms_ready, 1)
                    dve.wait_ge(m_rounded, k + 2)
                    one = lambda t: t[:, :, bass.ds(k, 1), :].rearrange("d p k e -> d p (k e)")
                    nc.vector.tensor_tensor(one(ml), ms[:, :, :], one(mh).bitcast(F32), ALU.subtract)
                assert st.n == PER

        @block.tensor
        def _(pe):
            pe.wait_ge(phi_loaded, 32)
            for n in range(NK):
                if n >= 2:
                    pe.wait_ge(k_copied, n - 1)
                nc.tensor.matmul(ps_k[n % 2][:, :], taps_dft[:, :], flat(windows[:])[:, n * CH:(n + 1) * CH],
                                 start=True, stop=True).then_inc(k_done, 1)
            pe.wait_ge(mus_ready, 1)
            for n, (b, p, r) in enumerate(regions):
                pe.wait_ge(added, n + 1)
                for s, (lo, hi, seg) in enumerate(segments(r)):
                    for lag in range(3):
                        q, shift = (p - lag) % 2, (p - lag) // 2
                        c0 = 1 + CH * r + lo + shift
                        last = nc.tensor.matmul(ps_m[n % 2][:, lo:hi], mus[:, lag, seg, :], uT[:, 2 * b + q, c0:c0 + hi - lo],
                                                start=(s == 0 and lag == 0), stop=(lag == 2), skip_group_check=True)
                last.then_inc(mixed, 1)


def stage_spectral(nc, spec_dram, kern_dram, y2_dram, mh, ml):
    ctx = ExitStack()
    with ctx:
        sb = lambda name, shape, dt=F32: ctx.enter_context(nc.sbuf_tensor(name, shape, dt))
        sem = lambda name: ctx.enter_context(nc.semaphore(name))
        ROW = B * 2 * 2 * EX
        u0 = [sb(f"u0{h}", [C, B, 2, 2, EX]) for h in range(2)]
        up = sb("up", [C, B, 3, 2, BS])
        uh = [sb(f"uh{h}", [C, B, 3, 2 * BS], F32R) for h in range(2)]
        ul = [sb(f"ul{h}", [C, B, 3, 2 * BS], F32R) for h in range(2)]
        t0 = sb("toeplitz0", [128, 2 * KF, 128])
        th = [sb(f"th{h}", [128, 2 * KF, 128], F32R) for h in range(2)]
        tl = [sb(f"tl{h}", [128, 2 * KF, 128], F32R) for h in range(2)]
        ph = [sb(f"ph{h}", [128, KC, 2, B, C], F32R) for h in range(2)]
        pl = [sb(f"pl{h}", [128, KC, 2, B, C], F32R) for h in range(2)]
        yo = [sb(f"yo{h}", [128, CH]) for h in range(2)]
        BANKS = 4
        ps_p = [ctx.enter_context(nc.psum_tensor(f"ps_p{q}", [128, KC, C], F32)) for q in range(BANKS)]
        ps_y = [ctx.enter_context(nc.psum_tensor(f"ps_yf{q}", [128, CH], F32)) for q in range(2)]
        pair = lambda name: [sem(f"{name}{h}") for h in range(2)]
        u_loaded = pair("sp_u_loaded")
        up_ready = sem("up_ready")
        up_used = sem("up_used")
        t_loaded = sem("sp_t_loaded")
        t_split = sem("t_split")
        pool_step = sem("pool_step")
        split = pair("split")
        p_mixed = sem("p_mixed")
        p_high = sem("p_high")
        p_low = sem("p_low")
        convolved = sem("sp_convolved")
        y_copied = sem("y_copied")
        y_stored = pair("sp_y_stored")
        gate = sem("sp_gate")
        block = ctx.enter_context(nc.Block())
        NC = 2 * KF // KC
        TILES = 2 * B
        tiles = [(q, b) for q in range(2) for b in range(B)]
        SRC = {(0, 0): 0, (0, 1): 1, (1, 0): 2, (1, 1): 0}

        @block.sync
        def _(sp):
            for h in range(2):
                sp.sem_inc(y_stored[h], 16)
            with sp.Fori(0, NF // 2) as i:
                for h in range(2):
                    f = i * 2 + h
                    sp.wait_ge(t_split, f + 1)
                    sp.dma_start(u0[h][:].rearrange("d b q r s -> d (b q r s)"),
                                 spec_dram[bass.ds(f, 1), :, :].rearrange("f d n -> (f d) n")).then_inc(u_loaded[h], 16)
                    for g in range(2):
                        for c in range(2):
                            src = bass.AP(tensor=kern_dram.tensor, offset=(2 * g + c) * NF * 2 * KF * 2 * BS + 1,
                                          ap=[[2 * KF * 2 * BS, NF], [1, BS], [2 * BS, 2 * KF], [1, BS]])
                            sp.dma_start(t0[BS * g:BS * g + BS, :, BS * c:BS * c + BS],
                                         src[bass.ds(f, 1), :, :, :].rearrange("f s k r -> (f s) k r")).then_inc(t_loaded, 16)

        @block.gpsimd
        def _(pool):
            pool.sem_inc(t_split, 1)
            with pool.Fori(0, NF // 2) as i:
                for h in range(2):
                    pool.wait_ge(convolved, i * (2 * NC) + (h + 1) * NC)
                    pool.wait_ge(u_loaded[h], i * 16 + 16)
                    pool.sem_inc(gate, 1)
                    nc.gpsimd.tensor_copy(up[:, :, 0:2, :, :], u0[h][:, :, :, :, 0:BS])
                    nc.gpsimd.tensor_copy(up[:, :, 2, :, :], u0[h][:, :, 1, :, 1:EX]).then_inc(pool_step, 1)
                    pool.wait_ge(pool_step, i * 6 + (h * 3 + 1))
                    pool.sem_inc(gate, 1)
                    upf = up[:].rearrange("d b q r s -> d (b q r s)")
                    nc.gpsimd.tensor_copy(flat(uh[h][:]), upf).then_inc(pool_step, 1)
                    pool.wait_ge(pool_step, i * 6 + (h * 3 + 2))
                    nc.gpsimd.tensor_tensor(flat(ul[h][:]), upf, flat(uh[h][:]).bitcast(F32), ALU.subtract)
                    pool.wait_ge(t_loaded, (i * 2 + h) * 64 + 64)
                    pool.sem_inc(gate, 1)
                    nc.gpsimd.tensor_copy(flat(th[h][:]), flat(t0[:])).then_inc(pool_step, 1)
                    pool.wait_ge(pool_step, i * 6 + (h * 3 + 3))
                    nc.gpsimd.tensor_tensor(flat(tl[h][:]), flat(t0[:]), flat(th[h][:]).bitcast(F32), ALU.subtract)\
                        .then_inc(split[h], 1)
                    pool.wait_ge(split[h], i + 1)
                    pool.sem_inc(t_split, 1)

        def dest(t, q, b):
            return t[:, :, q, b, :]

        @block.scalar
        def _(act):
            act.sem_inc(y_copied, 2)
            with act.Fori(0, NF // 2) as i:
                for h in range(2):
                    f = i * 2 + h
                    for kc in range(NC):
                        c = f * NC + kc
                        act.wait_ge(convolved, c + (2 * NC - 1))
                        act.sem_inc(gate, 1)
                        for n, (q, b) in enumerate(tiles):
                            act.wait_ge(p_mixed, c * TILES + n + 1)
                            nc.scalar.activation(dest(ph[kc % 2], q, b), ps_p[n % BANKS][:, :, :], ACT.Copy)\
                                .then_inc(p_high, 1)
                    act.wait_ge(convolved, f * NC + 3 * NC)
                    act.wait_ge(y_stored[h], i * 16 + 16)
                    act.sem_inc(gate, 1)
                    nc.scalar.activation(yo[h][:, :], ps_y[h][:, :], ACT.Copy).then_inc(y_copied, 1)
                    act.wait_ge(y_copied, f + 3)
                    act.dma_start(y2_dram[bass.ds(f, 1), :, :].rearrange("f p n -> (f p) n"), yo[h][:, :])\
                        .then_inc(y_stored[h], 16)
            for h in range(2):
                act.wait_ge(y_stored[h], 16 * (NF // 2 + 1))

        @block.vector
        def _(dve):
            dve.sem_inc(p_low, BANKS)
            with dve.Fori(0, NF) as f:
                for kc in range(NC):
                    for n, (q, b) in enumerate(tiles):
                        dve.wait_ge(p_high, (f * NC + kc) * TILES + n + 1)
                        nc.vector.tensor_tensor(dest(pl[kc % 2], q, b), ps_p[n % BANKS][:, :, :],
                                                dest(ph[kc % 2], q, b).bitcast(F32), ALU.subtract).then_inc(p_low, 1)

        @block.tensor
        def _(pe):
            pe.sem_inc(convolved, 2 * NC)

            def product(out, wh, wl, xh, xl, first, last):
                nc.tensor.matmul(out, wh, xh, start=first, stop=False)
                nc.tensor.matmul(out, wh, xl, start=False, stop=False)
                return nc.tensor.matmul(out, wl, xh, start=False, stop=last)

            with pe.Fori(0, NF // 2) as i:

                def mix(h, kc):
                    c = (i * 2 + h) * NC + kc
                    for n, (q, b) in enumerate(tiles):
                        pe.wait_ge(p_low, c * TILES + n + 1)
                        s = SRC[kc % 2, q]
                        m = [t[:, kc % 2, KC * (kc // 2):KC * (kc // 2) + KC, :].rearrange("d k e -> d (k e)") for t in (mh, ml)]
                        product(flat(ps_p[n % BANKS][:]), uh[h][:, b, s, :], ul[h][:, b, s, :], *m, True, True)\
                            .then_inc(p_mixed, 1)

                def convolve(h, kc):
                    c = (i * 2 + h) * NC + kc
                    pe.wait_ge(p_low, (c + 1) * TILES + BANKS)
                    if kc == 0:
                        pe.wait_ge(y_copied, i * 2 + h + 1)
                    for k in range(KC):
                        x = [t[kc % 2][:, k, :, :, :].rearrange("p q b e -> p (q b e)") for t in (ph, pl)]
                        w = [t[h][:, 2 * (KC * (kc // 2) + k) + kc % 2, :] for t in (th, tl)]
                        last = product(ps_y[h][:, :], *w, *x, kc == 0 and k == 0, kc == NC - 1 and k == KC - 1)
                    last.then_inc(convolved, 1)

                chunks = [(h, kc) for h in range(2) for kc in range(NC)]
                for n, (h, kc) in enumerate(chunks):
                    if kc == 0:
                        pe.wait_ge(split[h], i + 1)
                    mix(h, kc)
                    if n:
                        convolve(*chunks[n - 1])
                convolve(*chunks[-1])


def stage_output(nc, y2_dram, idft, hot, accum, out):
    ctx = ExitStack()
    with ctx:
        sb = lambda name, shape, dt=F32: ctx.enter_context(nc.sbuf_tensor(name, shape, dt))
        sem = lambda name: ctx.enter_context(nc.semaphore(name))
        inv = sb("inv", [2 * NF, NB])
        reach = sb("reach", [2 * NF, NB])
        RC = 16
        yd = [sb(f"yd{h}", [2 * NF, RC, CH]) for h in range(2)]
        ob = [sb(f"ob{h}", [C, CH]) for h in range(2)]
        ps_i = [ctx.enter_context(nc.psum_tensor(f"ps_i{q}", [C, RC, NB], F32)) for q in range(2)]
        pair = lambda name: [sem(f"{name}{h}") for h in range(2)]
        inv_loaded = sem("inv_loaded")
        inv_ready = sem("inv_ready")
        step = sem("out_step")
        y_loaded = pair("oy_loaded")
        inverted = sem("inverted")
        added = sem("out_added")
        o_ready = pair("o_ready")
        o_stored = pair("o_stored")
        block = ctx.enter_context(nc.Block())
        parts = BS // RC
        NT = parts * 2 * B

        @block.sync
        def _(sp):
            sp.dma_start(inv[:], idft).then_inc(inv_loaded, 16)
            for c in range(parts):
                if c >= 2:
                    sp.wait_ge(inverted, (c - 1) * 2 * B)
                sp.dma_start(yd[c % 2][:], y2_dram.rearrange("f (g r) n -> (f g) r n", g=2)[:, RC * c:RC * c + RC, :])\
                    .then_inc(y_loaded[c % 2], 16)
            for n in range(NG):
                b, g = divmod(n, GI)
                sp.wait_ge(o_ready[n % 2], n // 2 + 1)
                sp.dma_start(out[b, :, g * CH:(g + 1) * CH], ob[n % 2][:, :]).then_inc(o_stored[n % 2], 16)
            for h in range(2):
                sp.wait_ge(o_stored[h], 16 * (NG // 2))

        @block.vector
        def _(dve):
            dve.sem_inc(added, 2)
            st = Steps(dve, step)
            dve.wait_ge(inv_loaded, 16)
            h4 = hot[0:2 * NF, :]
            st.then(nc.vector.tensor_scalar(reach[:], inv[:], h4[:, 0:1], None, ALU.mult))
            for i in range(1, SEG):
                n = NB >> i
                ins = nc.vector.scalar_tensor_tensor(reach[:, 0:n], inv[:, 0:n], h4[:, i:i + 1], reach[:, 0:n],
                                                     ALU.mult, ALU.add)
                if i < SEG - 1:
                    st.then(ins)
                else:
                    ins.then_inc(inv_ready, 1)
            n = 0
            for c in range(parts):
                for p in range(2):
                    for b in range(B):
                        dve.wait_ge(inverted, n + 1)
                        acc = accum[:, 2 * b + p, :].rearrange("e (n s) -> e n s", s=BS)[:, :, RC * c:RC * c + RC]
                        nc.vector.tensor_tensor(acc, acc, ps_i[n % 2][:].rearrange("e s n -> e n s"), ALU.add)\
                            .then_inc(added, 1)
                        n += 1
            dve.wait_ge(added, NT + 2)
            for n in range(NG):
                b, g = divmod(n, GI)
                if n >= 2:
                    dve.wait_ge(o_stored[n % 2], 16 * (n // 2))
                nc.vector.tensor_copy(ob[n % 2][:, :].rearrange("p (n a) -> p a n", a=2),
                                      accum[:, 2 * b:2 * b + 2, g * (CH // 2):(g + 1) * (CH // 2)]).then_inc(o_ready[n % 2], 1)

        @block.tensor
        def _(pe):
            pe.wait_ge(inv_ready, 1)
            n = 0
            for c in range(parts):
                pe.wait_ge(y_loaded[c % 2], 16 * (c // 2 + 1))
                for p in range(2):
                    for b in range(B):
                        pe.wait_ge(added, n + 1)
                        for r in range(RC):
                            lhs = yd[c % 2][:, r, (p * B + b) * C:(p * B + b) * C + C]
                            last = nc.tensor.matmul(ps_i[n % 2][:, r, :], lhs, reach[:, :], start=True, stop=True)
                        last.then_inc(inverted, 1)
                        n += 1


def program(nc, d):
    ctx = ExitStack()
    with ctx:
        sb = lambda name, shape, dt=F32: ctx.enter_context(nc.sbuf_tensor(name, shape, dt))
        table = nc.dram_tensor("table", (B * TROWS, 4 * C), F32, kind="Internal").ap()
        xn_dram = nc.dram_tensor("xn_dram", (C, XR, HP), F32, kind="Internal").ap()
        spec_dram = nc.dram_tensor("spec_dram", (NF, C, B * 2 * 2 * EX), F32, kind="Internal").ap()
        kern_dram = nc.dram_tensor("kern_dram", (4 * NF, 2 * KF * 2 * BS), F32, kind="Internal").ap()
        y2_dram = nc.dram_tensor("y2_dram", (NF, 128, CH), F32, kind="Internal").ap()
        y_dram = nc.dram_tensor("y_dram", (NG, NBR, 2, 128, CH), F32, kind="Internal").ap()
        ident = sb("ident", [128, 128])
        blk16 = sb("blk16", [128, 128])
        blk8 = sb("blk8", [128, 128])
        eps6 = sb("eps6", [128, 1])
        eps5 = sb("eps5", [128, 1])
        xsum = sb("xsum", [C, B])
        ystats = sb("ystats", [128, 2 * NBR, NG * 6])
        fa = sb("fa", [C, B])
        fb = sb("fb", [C, B])
        const_loaded = ctx.enter_context(nc.semaphore("const_loaded"))
        with nc.Block() as block:
            @block.sync
            def _(sp):
                for t, name in ((ident, "ident"), (blk16, "blk16"), (blk8, "blk8")):
                    sp.dma_start(t[:], d[name]).then_inc(const_loaded, 16)
                sp.wait_ge(const_loaded, 48)

            @block.gpsimd
            def _(pool):
                pool.memset(eps6[:], 1e-6)
                pool.memset(eps5[:], 1e-5)

        stage_normalise(nc, d["x"], table, ident, eps6, xsum, xn_dram)
        stage_branches(nc, xn_dram, table, d["w_om"], d["base_om"], d["bias_om"], d["row_off"], d["img_off"], d["regw"],
                       ident, y_dram, ystats)
        accum = sb("accum", [C, 2 * B, HALF])
        hot = sb("hot", [128, SEG])
        mh = sb("mh", [C, 2, KF, C], F32R)
        ml = sb("ml", [C, 2, KF, C], F32R)
        with nc.sbuf_tensor("uT", [C, 2 * B, HALF + 1], F32) as uT:
            with nc.sbuf_tensor("fu", [C, B * HW], F32) as fu:
                stage_fuse(nc, y_dram, ystats, xsum, d["pool_w"], d["fuse_w"], d["gnp"], d["gnf"], blk16, blk8, eps5,
                           fu, fa, fb)
                stage_sum(nc, d["x"], fu, fa, fb, accum)
            stage_tokens(nc, ident, eps5, accum, uT, d["dft"], d["dft_edge"], spec_dram)
            stage_mixtures(nc, d["phi"], d["dft_taps"], d["m_phi"], d["m_u"], d["sigma"], d["logw"], d["gumbel"], accum,
                           uT, mh, ml, hot, kern_dram)
        stage_spectral(nc, spec_dram, kern_dram, y2_dram, mh, ml)
        stage_output(nc, y2_dram, d["idft"], hot, accum, d["out"])


def kernel(**inputs):
    import numpy as np
    import concourse.bacc as bacc
    from concourse.bass_utils import run_bass_kernel_spmd as run

    g = {n: np.asarray(v) for n, v in inputs.items()}
    P = "L0_conv_"
    f = np.float32
    a = {}
    a["x"] = g["x"].reshape(B, C, HW)
    w_om = np.zeros((C, 7, 7, 3, TAPS), f)
    bias_om = np.zeros((3, TAPS), f)
    base = np.zeros((128, 3, TAPS), f)
    regw = np.zeros((C, TAPS, O), f)
    p = np.arange(128)
    t0 = 0
    for name, k in (("b4", 7), ("b3", 3), ("b1", 1), ("b2", 1)):
        n, lo = k * k, (7 - k) // 2
        offw = g[P + name + "_offw"].reshape(n, 2, C, k, k)
        w_om[:, lo:lo + k, lo:lo + k, 0:2, t0:t0 + n] = offw.transpose(2, 3, 4, 1, 0)
        w_om[:, lo:lo + k, lo:lo + k, 2, t0:t0 + n] = g[P + name + "_modw"].transpose(1, 2, 3, 0)
        bias_om[0:2, t0:t0 + n] = g[P + name + "_offb"].reshape(n, 2).T
        bias_om[2, t0:t0 + n] = g[P + name + "_modb"]
        ky, kx = np.divmod(np.arange(n), k)
        base[:, 0, t0:t0 + n] = (p[:, None] // W) + ky - k // 2 + 2
        base[:, 1, t0:t0 + n] = (p[:, None] % W) + kx - k // 2 + 2
        regw[:, t0:t0 + n, :] = g[P + name + "_regw"].reshape(O, C, n).transpose(1, 2, 0)
        t0 += n
    a["w_om"] = w_om.reshape(C, 49, 3, TAPS)
    a["bias_om"], a["base_om"], a["regw"] = bias_om, base, regw
    m = np.arange((NG + 1) * 4)
    a["row_off"] = np.broadcast_to((2 * (m % (4 * GI))).astype(f), (128, m.size))
    a["img_off"] = np.broadcast_to((np.minimum(m // (4 * GI), B - 1) * TROWS).astype(f), (128, m.size))
    order = ("b4", "b3", "b1", "b2", "pool")
    gnp = np.stack([np.concatenate([g[P + n + s].reshape(2, 128) for n in order]) for s in ("_gng", "_gnb")])
    a["gnp"] = np.repeat(gnp.transpose(2, 0, 1)[:, :, None, :], B, axis=2)
    a["gnf"] = np.repeat(np.stack([g[P + "fuse_gng"], g[P + "fuse_gnb"]], 1)[:, :, None], B, axis=2)
    fw = g[P + "fuse_w"].reshape(C, 5, 2, 128)[:, [3, 2, 0, 1, 4]]
    a["fuse_w"] = fw.reshape(C, NFC, 128).transpose(2, 1, 0)
    a["pool_w"] = g[P + "pool_w"].reshape(O, C).T
    a["ident"] = np.eye(128, dtype=f)
    grp = lambda n: (p[:, None] // n == p[None, :] // n).astype(f) / f(n)
    a["blk16"], a["blk8"] = grp(O // 16), grp(C // 16)
    Q = "L0_ffn_"
    phi = np.zeros((KF, 2, BS + HALF), f)
    phi[:, :, BS:] = g[Q + "phi"].reshape(HALF, 2, KF).transpose(2, 1, 0)
    a["phi"] = phi
    a["m_phi"] = np.stack([g[Q + "M_phi_plus"], g[Q + "M_phi_minus"]]).transpose(2, 3, 0, 1, 4)
    a["m_u"] = g[Q + "M_u"].transpose(2, 0, 1, 3)
    w = 2 * np.pi / (2 * NB)
    blk, frq = np.arange(NB)[:, None], np.arange(NF)[None, :]

    def transform(n):
        re, im = np.cos(w * n * frq), -np.sin(w * n * frq)
        im[:, 0] = np.where(n[:, 0] % 2, -1.0, 1.0)
        return re, im

    re, im = transform(blk)
    dft = np.zeros((4, NB, 4, 2, NF))
    for s in range(4):
        dft[s, :, 3 - s, 0], dft[s, :, 3 - s, 1] = re, im
    a["dft"] = dft.reshape(128, 4 * 2 * NF).astype(f)
    edge = np.zeros((4, NB, 2, NF))
    edge[3, :, 0], edge[3, :, 1] = transform(blk + 1)
    a["dft_edge"] = edge.reshape(128, 2 * NF).astype(f)
    quarters = np.stack([re, im, -im, re], 1)
    quarters[:, 1, 0] = quarters[:, 2, 0] = 0.0
    quarters[:, 3, 0] = im[:, 0]
    a["dft_taps"] = quarters.reshape(NB, 4 * NF).astype(f)
    idft = np.stack([2 * np.cos(w * blk * frq), -2 * np.sin(w * blk * frq)], 2)
    idft[:, 0, 0], idft[:, 0, 1] = 1.0, im[:, 0]
    a["idft"] = (idft / (2 * NB)).reshape(NB, 2 * NF).T.astype(f)
    a["sigma"], a["logw"], a["gumbel"] = g[Q + "sigma"], g[Q + "log_weights"], g[Q + "gumbel"]
    a = {n: np.ascontiguousarray(v) for n, v in a.items()}

    nc = bacc.Bacc("TRN2", target_bir_lowering=False, num_devices=1)
    d = {n: nc.dram_tensor(f"in_{n}", v.shape, mybir.dt.from_np(v.dtype), kind="ExternalInput").ap() for n, v in a.items()}
    d["out"] = nc.dram_tensor("out", (B, C, HW), F32, kind="ExternalOutput").ap()
    program(nc, d)
    r = run(nc, [{f"in_{n}": v for n, v in a.items()}], core_ids=[0])
    return r.results[0]["out"].reshape(B, C, H, W)
```

```python
import concourse.bass as bass
from concourse import mybir
from contextlib import ExitStack

B, C, H, W = 2, 128, 64, 64
HW = H * W
O = 256
TAPS = 49 + 9 + 1 + 1
BRANCHES = ((0, 49), (49, 9), (58, 1), (59, 1))
NBR = len(BRANCHES)
PAD = 3
HP = H + 2 * PAD
TS = H + 3
TROWS = TS * TS
CH = 512
GI = HW // CH
XR = 2 * HP + 28
HR = CH // W + 2 * PAD
NG = B * GI
RING = 6
KF = 16
HALF = HW // 2
SEG = 4
BS = 64
NB = HALF // BS
NF = NB
EX = BS + 1
KC = 4
NFC = 2 * (NBR + 1)
F32 = mybir.dt.float32
F32R = mybir.dt.float32r
I32 = mybir.dt.int32
ALU = mybir.AluOpType
ACT = mybir.ActivationFunctionType
AX = mybir.AxisListType


class Steps:

    def __init__(self, eng, sem, base=0):
        self.eng, self.sem, self.base, self.n = eng, sem, base, 0

    def then(self, ins):
        self.n += 1
        ins.then_inc(self.sem, 1)
        self.eng.wait_ge(self.sem, self.base + self.n)


def flat(ap):
    n = len(ap.shape) - 1
    names = " ".join("abcdef"[:n])
    return ap.rearrange(f"p {names} -> p ({names})")


def stage_normalise(nc, x, table, ident, eps6, xsum, xn_dram, w_om, wom):
    ctx = ExitStack()
    with ctx:
        sb = lambda name, shape, dt=F32: ctx.enter_context(nc.sbuf_tensor(name, shape, dt))
        sem = lambda name: ctx.enter_context(nc.semaphore(name))
        LNB = 4
        xg = [sb(f"xg{h}", [C, CH]) for h in range(LNB)]
        xn = [sb(f"xn{h}", [128, 4, C]) for h in range(LNB)]
        stats = [sb(f"ln_stats{h}", [128, 4, 6]) for h in range(LNB)]
        mv = [sb(f"ln_mv{h}", [128, 4, 2]) for h in range(LNB)]
        sd = [sb(f"ln_sd{h}", [128, 4]) for h in range(LNB)]
        rs = [sb(f"ln_rs{h}", [128, 4]) for h in range(LNB)]
        zero = sb("zero", [TS, 2 * 4 * C])
        xnpad = sb("xnpad", [C, XR, HP])
        ps_x = [ctx.enter_context(nc.psum_tensor(f"ps_x{h}", [128, 4, C], F32)) for h in range(LNB)]
        ps_n = [ctx.enter_context(nc.psum_tensor(f"ps_n{h}", [128, CH], F32)) for h in range(LNB)]

        zero_set = sem("zero_set")
        border_written = sem("border_written")
        pad_zeroed = sem("pad_zeroed")
        x_loaded = [sem(f"x_loaded{h}") for h in range(LNB)]
        x_turned = sem("x_turned")
        var_ready = sem("var_ready")
        sd_ready = sem("sd_ready")
        dve_step = sem("ln_dve_step")
        xn_ready = sem("xn_ready")
        xn_turned = sem("xn_turned")
        xn_copied = sem("xn_copied")
        table_written = [sem(f"table_written{h}") for h in range(LNB)]
        wom_loaded = sem("wom_loaded")
        xn_stored = sem("xn_stored")
        gate = sem("ln_gate")
        WR = 8 * 16
        tab = table.rearrange("(b y x) s -> b y x s", b=B, y=TS)
        tab2 = table.rearrange("(y x) s -> y x s", x=TS)
        block = ctx.enter_context(nc.Block())

        NK = NG // LNB
        IK = GI // LNB

        @block.gpsimd
        def _(pool):
            for h in range(LNB):
                pool.dma_start(xg[h][:, :], x[0, :, h * CH:h * CH + CH]).then_inc(x_loaded[h], 16)
            pool.memset(zero[:], 0.0).then_inc(zero_set, 1)
            pool.memset(xnpad[:], 0.0).then_inc(pad_zeroed, 1)
            with pool.Fori(1, NK) as k:
                for h in range(LNB):
                    pool.wait_ge(x_turned, k * LNB + h + 1)
                    pool.sem_inc(gate, 1)
                    pool.dma_start(xg[h][:, :], x[bass.ds(k // IK, 1), :, bass.ds((k % IK) * (LNB * CH) + h * CH, CH)]
                                   .rearrange("b c n -> (b c) n")).then_inc(x_loaded[h], 16)

        @block.sync
        def _(sp):
            sp.wait_ge(zero_set, 1)
            for b in range(B):
                for y in (0, TS - 2):
                    sp.dma_start(tab[b, y:y + 2, :, :].rearrange("y x s -> (y x s)").rearrange("(p n) -> p n", p=TS),
                                 zero[:, :]).then_inc(border_written, 16)
                for c in (0, TS - 2):
                    sp.dma_start(tab[b, 2:TS - 2, c:c + 2, :].rearrange("y x s -> y (x s)"), zero[0:TS - 4, :])\
                        .then_inc(border_written, 16)
            for h in range(LNB):
                sp.sem_inc(table_written[h], WR)
            sp.wait_ge(border_written, 16 * 4 * B)
            sp.dma_start(wom[:], w_om).then_inc(wom_loaded, 16)
            with sp.Fori(0, B) as b:
                with sp.Fori(0, IK) as i:
                    for h in range(LNB):
                        sp.wait_ge(xn_ready, (b * IK + i) * LNB + h + 1 + LNB)
                        for half in range(2):
                            src = xn[h][64 * half:64 * half + 64, :, :]
                            for slot, (dy, dx) in enumerate(((0, 0), (0, 1), (1, 0), (1, 1))):
                                y0 = b * TS + i * (8 * LNB) + (h * 8 + half + 2 - dy)
                                dst = tab2[bass.ds(y0, 4, step=2), 2 - dx:2 - dx + W, slot * C:(slot + 1) * C]
                                sp.dma_start(dst.rearrange("t x c -> x t c"), src).then_inc(table_written[h], 16)
            for h in range(LNB):
                sp.wait_ge(table_written[h], WR * (NK + 1))
            sp.wait_ge(wom_loaded, 16)

        @block.tensor
        def _(pe):
            pe.sem_inc(x_turned, LNB)
            pe.sem_inc(xn_turned, LNB)
            with pe.Fori(0, NK) as k:
                for h in range(LNB):
                    pe.wait_ge(x_loaded[h], 16 * k + 16)
                    pe.wait_ge(xn_ready, k * LNB + h + 1)
                    for j in range(4):
                        last = nc.tensor.transpose(ps_x[h][:, j, :], xg[h][:, 128 * j:128 * j + 128], ident[:, :])
                    last.then_inc(x_turned, 1)
                for h in range(LNB):
                    pe.wait_ge(xn_ready, k * LNB + h + 1 + LNB)
                    pe.wait_ge(xn_copied, k * LNB + h + 1)
                    for j in range(4):
                        last = nc.tensor.transpose(ps_n[h][:, 128 * j:128 * j + 128], xn[h][:, j, :], ident[:, :])
                    last.then_inc(xn_turned, 1)

        @block.vector
        def _(dve):
            dve.sem_inc(xn_ready, LNB)
            with dve.Fori(0, NK) as k:
                st = Steps(dve, dve_step, k * (2 * LNB))
                for h in range(LNB):
                    dve.wait_ge(x_turned, k * LNB + h + 1 + LNB)
                    for j in range(4):
                        last = nc.vector.bn_stats(stats[h][:, j, :], ps_x[h][:, j, :])
                    st.then(last)
                    dve.sem_inc(gate, 1)
                    for j in range(4):
                        last = nc.vector.bn_aggr(mv[h][:, j, :], stats[h][:, j, :])
                    last.then_inc(var_ready, 1)
                for h in range(LNB):
                    dve.wait_ge(sd_ready, k * LNB + h + 1)
                    st.then(nc.vector.reciprocal(rs[h][:, :], sd[h][:, :]))
                    dve.wait_ge(table_written[h], k * WR + WR)
                    dve.wait_ge(xn_turned, k * LNB + h + 1)
                    for j in range(4):
                        last = nc.vector.tensor_scalar(xn[h][:, j, :], ps_x[h][:, j, :], mv[h][:, j, 0:1],
                                                       rs[h][:, j:j + 1], ALU.subtract, ALU.mult)
                    last.then_inc(xn_ready, 1)
            dve.wait_ge(xn_copied, NG + LNB)
            for b in range(B):
                nc.vector.tensor_reduce(xsum[:, b:b + 1], xnpad[:, b * HP + PAD:b * HP + PAD + H, PAD:PAD + W],
                                        AX.XY, ALU.add)

        @block.scalar
        def _(act):
            act.sem_inc(xn_copied, LNB)
            act.wait_ge(pad_zeroed, 1)
            act.sem_inc(gate, 1)
            with act.Fori(0, B) as b:
                with act.Fori(0, IK) as i:
                    k = b * IK + i
                    for h in range(LNB):
                        act.wait_ge(var_ready, k * LNB + h + 1)
                        nc.scalar.activation(sd[h][:, :], mv[h][:, :, 1], ACT.Sqrt, bias=eps6[:, 0:1])\
                            .then_inc(sd_ready, 1)
                    for h in range(LNB):
                        act.wait_ge(xn_turned, k * LNB + h + 1 + LNB)
                        act.sem_inc(gate, 1)
                        nc.scalar.activation(
                            xnpad[:, bass.ds(b * HP + i * (8 * LNB) + h * 8 + PAD, 8), PAD:PAD + W],
                            ps_n[h][:, :].rearrange("p (y x) -> p y x", x=W), ACT.Copy).then_inc(xn_copied, 1)
            act.wait_ge(xn_copied, NG + LNB)
            act.dma_start(xn_dram, xnpad[:]).then_inc(xn_stored, 16)
            act.wait_ge(xn_stored, 16)


def stage_branches(nc, xn_dram, table, wom, base_om, bias_om, row_off, img_off, regw, ident, y_dram, ystats):
    ctx = ExitStack()
    with ctx:
        sb = lambda name, shape, dt=F32: ctx.enter_context(nc.sbuf_tensor(name, shape, dt))
        sem = lambda name: ctx.enter_context(nc.semaphore(name))
        pair = lambda name: [sem(f"{name}{h}") for h in range(2)]
        base = sb("base", [128, 3, TAPS])
        rowt = sb("rowt", [128, (NG + 1) * 4])
        imgt = sb("imgt", [128, (NG + 1) * 4])
        win = sb("win", [C, 7, HR, W])
        P = sb("P", [128, 3, TAPS])
        sg = sb("sg", [128, TAPS])
        pi = sb("pi", [128, 2, TAPS], I32)
        fl = sb("fl", [128, 2, TAPS])
        gt = sb("gt", [128, 2, TAPS])
        fr = sb("fr", [128, 2, TAPS])
        a = sb("a", [128, 2, TAPS])
        rowf = a[:, 0, :]
        idx_next = sb("idx_next", [128, TAPS, 4], I32)
        wts_next = sb("wts_next", [128, TAPS, 4, 2, 2])
        R = sb("R", [C, TAPS, O])
        idx = sb("idx", [128, TAPS, 4], I32)
        wts = sb("wts", [128, TAPS * 16])
        G = [sb(f"G{s}", [128, 4, 4 * C]) for s in range(RING)]
        acc = [sb(f"acc{h}", [128, 4, C]) for h in range(3)]
        sT = [sb(f"sT{h}", [C, CH]) for h in range(2)]
        yb = [sb(f"yb{h}", [128, 2, CH]) for h in range(3)]
        YB = (0, 1, 0, 2)
        ps_y = [ctx.enter_context(nc.psum_tensor(f"ps_y{h}", [128, 2, CH], F32)) for h in range(2)]
        ps_t = [ctx.enter_context(nc.psum_tensor(f"ps_t{h}", [C, CH], F32)) for h in range(2)]
        ps_o = [ctx.enter_context(nc.psum_tensor(f"ps_o{h}", [128, 3, 128], F32)) for h in range(2)]

        params = sem("om_params")
        base_ready = sem("base_ready")
        win_loaded = sem("win_loaded")
        om_done = sem("om_done")
        om_read = sem("om_read")
        mod_ready = sem("mod_ready")
        sig_ready = sem("sig_ready")
        sig_used = sem("sig_used")
        step = sem("om_step")
        offsets_ready = sem("offsets_ready")
        handed = pair("handed")
        r_loaded = sem("r_loaded")
        gathered = [sem(f"gathered{s}") for s in range(RING)]
        first_corner = sem("first_corner")
        corner = sem("corner")
        blended = sem("blended")
        turned = sem("turned")
        copied = sem("copied")
        summed = sem("summed")
        evacuated = sem("evacuated")
        measured = sem("measured")
        stored = [sem(f"y_stored{h}") for h in range(3)]
        gate = sem("c_gate")
        SPLIT = TAPS // 2
        parts = ((0, SPLIT), (SPLIT, TAPS))
        TILE_STEPS = 11
        WINDOW_STEP = 4 * TILE_STEPS + 4
        block = ctx.enter_context(nc.Block())
        ends = [t0 + n for t0, n in BRANCHES]
        centre = 24
        conv_taps = sorted(range(49), key=lambda t: (t != centre, t))

        def columns(t):
            ky, kx = divmod(t, 7)
            if t == centre:
                return TAPS
            return 58 if 2 <= ky <= 4 and 2 <= kx <= 4 else 49

        @block.sync
        def _(sp):
            sp.dma_start(base[:], base_om).then_inc(params, 16)
            sp.dma_start(P[:], bias_om.rearrange("(a k) t -> a k t", a=1).to_broadcast([128, 3, TAPS]))\
                .then_inc(params, 16)
            sp.dma_start(rowt[:], row_off).then_inc(params, 16)
            sp.dma_start(imgt[:], img_off).then_inc(params, 16)
            for h in range(3):
                sp.sem_inc(stored[h], 16)

            def load_window(n, kx):
                row = n * (CH // W) + (n >> 3) * (2 * PAD)
                rows = xn_dram[:, 0:HR, kx:kx + W] if isinstance(n, int) and n == 0 else \
                    xn_dram[:, bass.ds(row, HR), kx:kx + W]
                sp.dma_start(win[:, kx, :, :], rows).then_inc(win_loaded, 16)

            def hand(u):
                lo, hi = parts[u]
                sp.dma_start(idx[:, lo:hi, :], idx_next[:, lo:hi, :]).then_inc(handed[u], 16)
                sp.dma_start(wts[:, 16 * lo:16 * hi], flat(wts_next[:])[:, 16 * lo:16 * hi]).then_inc(handed[u], 16)

            def store(g, br):
                sp.wait_ge(evacuated, g * NBR + (br + 3))
                sp.dma_start(y_dram[bass.ds(g, 1), br, :, :, :].rearrange("g h p n -> (g p) h n"),
                             yb[YB[br]][:, :, :]).then_inc(stored[YB[br]], 16)

            for kx in range(7):
                load_window(0, kx)
            sp.dma_start(R[:], regw).then_inc(r_loaded, 16)
            sp.wait_ge(offsets_ready, 1)
            for u in range(2):
                hand(u)
            for kx in range(7):
                load_window(1, kx)
            with sp.Fori(0, NG) as g:
                sp.wait_ge(offsets_ready, g + 2)
                for u in range(2):
                    sp.wait_ge(blended, g * TAPS + parts[u][1] + RING)
                    hand(u)
                    for kx in range(6) if u == 0 else (6,):
                        if u == 0:
                            sp.wait_ge(blended, g * TAPS + (WINDOW_STEP + 2 * kx + RING))
                        load_window(g + 2, kx)
                        if kx == 3:
                            store(g, 0)
                for br in range(1, NBR):
                    store(g, br)
            for h in range(3):
                sp.wait_ge(stored[h], 16 + 16 * YB.count(h) * NG)
            for h in range(2):
                sp.wait_ge(handed[h], 32 * (NG + 1))
            sp.wait_ge(win_loaded, 7 * 16 * (NG + 2))

        @block.gpsimd
        def _(pool):
            with pool.Fori(0, NG) as g:
                for k in range(TAPS):
                    if k in (0, SPLIT):
                        pool.wait_ge(handed[k // SPLIT], g * 32 + 32)
                        pool.sem_inc(gate, 1)
                    pool.wait_ge(blended, g * TAPS + k + 1)
                    pool.sem_inc(gate, 1)
                    for j in range(4):
                        pool.indirect_dma_start(G[k % RING][:, j, :], None, table,
                                                bass.IndirectOffsetOnAxis(ap=idx[:, k, j:j + 1], axis=0))\
                            .then_inc(gathered[k % RING], 16)

        def groups(eng, body, rows, weights, after):
            for j in range(4):
                rows(0, j)
                weights(0, j)
            eng.sem_inc(gate, 1)
            with eng.Fori(0, NG) as g:
                eng.wait_ge(handed[0], g * 32 + 32)
                eng.sem_inc(gate, 1)
                for lo, hi, tr, tw in ((0, 2, 0, None), (2, 3, None, 0), (3, 4, 1, None), (4, 5, None, 1), (5, 6, 2, None),
                                       (6, 7, None, 2), (7, 8, 3, 3), (8, 9, None, None)):
                    if lo == 5:
                        eng.wait_ge(handed[1], g * 32 + 32)
                        eng.sem_inc(gate, 1)
                    with eng.Fori(lo, hi) as q:
                        body(g, q)
                    if tr is not None:
                        rows(g + 1, tr)
                    if tw is not None:
                        weights(g + 1, tw)
                    eng.sem_inc(gate, 1)
                after(g, (0,))
                with eng.Fori(9, 10) as q:
                    body(g, q)
                after(g, (1, 2, 3))

        @block.scalar
        def _(act):
            act.sem_inc(evacuated, 2)

            def rows(n, j):
                m = n * 4 + j
                act.wait_ge(mod_ready, m + 1)
                act.wait_ge(sig_used, m + 1)
                nc.scalar.activation(sg[:, :], P[:, 2, :], ACT.Sigmoid).then_inc(sig_ready, 1)

            def weights(n, j):
                pass

            def corner0(g, q, i):
                n = g * TAPS + q * RING + i
                act.wait_ge(gathered[i], (g * (TAPS // RING) + q) * 64 + 64)
                act.wait_ge(turned, n + 1)
                act.sem_inc(gate, 1)
                for j in range(4):
                    last = nc.scalar.activation(acc[i % 3][:, j, :], G[i][:, j, 0:C], ACT.Copy,
                                                scale=wts[:, bass.ds(q * (16 * RING) + (i * 16 + j * 4), 1)])
                last.then_inc(first_corner, 1)

            def copy_out(g, q, i):
                n = g * TAPS + q * RING + i
                act.wait_ge(turned, n + 4)
                act.wait_ge(summed, n + 1)
                nc.scalar.activation(sT[i % 2][:, :], ps_t[i % 2][:, :], ACT.Copy).then_inc(copied, 1)

            def body(g, q):
                corner0(g, q, 0)
                for i in range(1, RING):
                    corner0(g, q, i)
                    copy_out(g, q, i - 1)
                copy_out(g, q, RING - 1)

            def after(g, brs):
                for br in brs:
                    act.wait_ge(summed, g * TAPS + ends[br] + 2)
                    n = YB.count(YB[br])
                    act.wait_ge(stored[YB[br]], g * (16 * n) + 16 * (YB[:br].count(YB[br]) + 1))
                    act.wait_ge(measured, g * NBR + br + 1)
                    for half in range(2):
                        last = nc.scalar.activation(yb[YB[br]][:, half, :], ps_y[br % 2][:, half, :], ACT.Copy)
                    last.then_inc(evacuated, 1)

            groups(act, body, rows, weights, after)

        @block.vector
        def _(dve):
            dve.sem_inc(blended, RING)
            dve.sem_inc(measured, 2)
            dve.sem_inc(sig_used, 1)
            dve.wait_ge(params, 64)
            nc.vector.tensor_tensor(base[:], base[:], P[:], ALU.add).then_inc(base_ready, 1)
            dve.wait_ge(base_ready, 1)
            ROW_STEPS, WEIGHT_STEPS = 10, 4
            PER = ROW_STEPS + WEIGHT_STEPS

            def rows(n, j):
                m = n * 4 + j
                st = Steps(dve, step, m * PER)
                dve.wait_ge(om_done, m + 1)
                st.then(nc.vector.tensor_tensor(P[:], ps_o[j % 2][:, :, 0:TAPS], base[:], ALU.add))
                dve.sem_inc(om_read, 1)
                dve.sem_inc(mod_ready, 1)
                col = lambda t: t[:, m:m + 1] if isinstance(m, int) else t[:, bass.ds(m, 1)]
                st.then(nc.vector.tensor_scalar(P[:, 0, :], P[:, 0, :], col(rowt), 0.0, ALU.add, ALU.max))
                st.then(nc.vector.tensor_scalar(P[:, 0:2, :], P[:, 0:2, :], 0.0, float(H + 2), ALU.max, ALU.min))
                st.then(nc.vector.tensor_copy(pi[:], P[:, 0:2, :]))
                st.then(nc.vector.tensor_copy(fl[:], pi[:]))
                st.then(nc.vector.tensor_tensor(gt[:], fl[:], P[:, 0:2, :], ALU.is_gt))
                st.then(nc.vector.tensor_tensor(fl[:], fl[:], gt[:], ALU.subtract))
                st.then(nc.vector.tensor_tensor(fr[:], P[:, 0:2, :], fl[:], ALU.subtract))
                st.then(nc.vector.scalar_tensor_tensor(rowf, fl[:, 0, :], float(TS), fl[:, 1, :], ALU.mult, ALU.add))
                if j == 0 and not isinstance(n, int):
                    for u in range(2):
                        dve.wait_ge(handed[u], n * 32)
                st.then(nc.vector.tensor_scalar(idx_next[:, :, j], rowf, col(imgt), None, ALU.add))
                assert st.n == ROW_STEPS

            def weights(n, j):
                m = n * 4 + j
                st = Steps(dve, step, m * PER + ROW_STEPS)
                dve.wait_ge(sig_ready, m + 1)
                st.then(nc.vector.scalar_tensor_tensor(a[:, 1, :], sg[:], 2.0, fr[:, 0, :], ALU.mult, ALU.mult))
                st.then(nc.vector.scalar_tensor_tensor(a[:, 0, :], sg[:], 2.0, a[:, 1, :], ALU.mult, ALU.subtract))
                dve.sem_inc(sig_used, 1)
                for r in range(2):
                    last = nc.vector.tensor_tensor(wts_next[:, :, j, r, 1], a[:, r, :], fr[:, 1, :], ALU.mult)
                st.then(last)
                for r in range(2):
                    last = nc.vector.tensor_tensor(wts_next[:, :, j, r, 0], a[:, r, :], wts_next[:, :, j, r, 1],
                                                   ALU.subtract)
                st.then(last)
                assert st.n == WEIGHT_STEPS
                if j == 3:
                    dve.sem_inc(offsets_ready, 1)

            def body(g, q):
                for i in range(RING):
                    n = g * TAPS + q * RING + i
                    dve.wait_ge(first_corner, n + 1)
                    for c in range(1, 4):
                        if c > 1:
                            dve.wait_ge(corner, n * 2 + c - 1)
                        for j in range(4):
                            last = nc.vector.scalar_tensor_tensor(
                                acc[i % 3][:, j, :], G[i][:, j, c * C:(c + 1) * C],
                                wts[:, bass.ds(q * (16 * RING) + (i * 16 + j * 4 + c), 1)], acc[i % 3][:, j, :],
                                ALU.mult, ALU.add)
                        last.then_inc(corner if c < 3 else blended, 1)

            def after(g, brs):
                for br in brs:
                    dve.wait_ge(evacuated, g * NBR + br + 3)
                    dve.sem_inc(gate, 1)
                    for half in range(2):
                        last = nc.vector.bn_stats(ystats[:, 2 * br + half, bass.ds(g * 6, 6)],
                                                  yb[YB[br]][:, half, :])
                    last.then_inc(measured, 1)

            groups(dve, body, rows, weights, after)
            dve.wait_ge(measured, NBR * NG + 2)

        @block.tensor
        def _(pe):
            pe.sem_inc(turned, 3)
            pe.sem_inc(summed, 2)
            pe.sem_inc(om_read, 2)

            def convolve(n, j, lo, hi):
                m = n * 4 + j
                if lo == 0:
                    if j == 0:
                        pe.wait_ge(win_loaded, n * 112 + 112)
                    pe.wait_ge(om_read, m + 1)
                for t in conv_taps[lo:hi]:
                    ky, kx = divmod(t, 7)
                    last = nc.tensor.matmul(ps_o[j % 2][:, :, 0:columns(t)],
                                            win[:, kx, 2 * j + ky:2 * j + ky + 2, :].rearrange("c y x -> c (y x)"),
                                            wom[:, t, :, 0:columns(t)], start=(t == centre), stop=(t == conv_taps[-1]),
                                            skip_group_check=True)
                if hi == 49:
                    last.then_inc(om_done, 1)

            for j in range(4):
                convolve(0, j, 0, 49)
            pe.wait_ge(r_loaded, 16)
            with pe.Fori(0, NG) as g:

                def turn(k):
                    pe.wait_ge(blended, g * TAPS + k + 1 + RING)
                    for j in range(4):
                        last = nc.tensor.transpose(ps_t[k % 2][:, 128 * j:128 * j + 128], acc[k % 3][:, j, :], ident[:, :])
                    last.then_inc(turned, 1)

                def contract(k):
                    br = [k < e for e in ends].index(True)
                    t0 = BRANCHES[br][0]
                    pe.wait_ge(copied, g * TAPS + k + 1)
                    if k == t0:
                        pe.wait_ge(evacuated, g * NBR + br + 1)
                    for half in range(2):
                        last = nc.tensor.matmul(ps_y[br % 2][:, half, :], R[:, k, 128 * half:128 * half + 128],
                                                sT[k % 2][:, :], start=(k == t0), stop=(k == ends[br] - 1))
                    last.then_inc(summed, 1)

                for k in range(TAPS):
                    turn(k)
                    if k:
                        contract(k - 1)
                    j, i = divmod(k, TILE_STEPS)
                    if j < 4 and i:
                        share = lambda i: 49 * i // (TILE_STEPS - 1)
                        convolve(g + 1, j, share(i - 1), share(i))
                contract(TAPS - 1)


def group_affine(dve, act_sem, st, sq, var, sd, a, b, gm, gamma, beta, ready, nc):
    st.then(nc.vector.tensor_tensor(sq, gm[:, 0, :], gm[:, 0, :], ALU.mult))
    st.then(nc.vector.tensor_tensor(var, gm[:, 1, :], sq, ALU.subtract))
    st.then(nc.vector.tensor_scalar(var, var, 0.0, None, ALU.max))
    dve.sem_inc(ready, 1)
    dve.wait_ge(act_sem, 1)
    st.then(nc.vector.reciprocal(sd, sd))
    st.then(nc.vector.tensor_tensor(a, gamma, sd, ALU.mult))
    st.then(nc.vector.tensor_tensor(b, gm[:, 0, :], a, ALU.mult))
    st.then(nc.vector.tensor_tensor(b, beta, b, ALU.subtract))


def stage_fuse(nc, y_dram, ystats, xsum, pool_w, fuse_w, gnp, gnf, blk16, blk8, eps5, fu, fa, fb):
    ctx = ExitStack()
    with ctx:
        sb = lambda name, shape, dt=F32: ctx.enter_context(nc.sbuf_tensor(name, shape, dt))
        sem = lambda name: ctx.enter_context(nc.semaphore(name))
        pw = sb("pw", [C, O])
        fw = sb("fw", [128, NFC, C])
        gp = sb("gp", [128, 2, B, NFC])
        gf = sb("gf", [C, 2, B])
        mv = sb("mv", [128, B, 2 * NBR, 2])
        me = sb("me", [128, 2, B * NFC])
        gm = sb("gm", [128, 2, B * NFC])
        sq = sb("sq", [128, B * NFC])
        var = sb("var", [128, B * NFC])
        sd = sb("sd", [128, B * NFC])
        ya = sb("ya", [128, B * NFC])
        ybb = sb("ybb", [128, B * NFC])
        xmean = sb("xmean", [C, B])
        y5 = sb("y5", [128, B, 2])
        z5 = sb("z5", [128, 2, B])
        bias5 = sb("bias5", [C, B])
        YR = 4
        yin = [sb(f"yin{h}", [128, 2 * NBR, CH]) for h in range(YR)]
        fstats = sb("fstats", [C, NG * 6])
        fmv = sb("fmv", [C, B, 2])
        fme = sb("fme", [C, 2, B])
        fgm = sb("fgm", [C, 2, B])
        fsq = sb("fsq", [C, B])
        fvar = sb("fvar", [C, B])
        fsd = sb("fsd", [C, B])
        ps_s = ctx.enter_context(nc.psum_tensor("ps_s", [128, 2, 64], F32))
        ps_f = [ctx.enter_context(nc.psum_tensor(f"ps_f{h}", [C, CH], F32)) for h in range(YR)]
        params = sem("f_params")
        step = sem("f_step")
        xm_ready = sem("xm_ready")
        y5_ready = sem("y5_ready")
        me_ready = sem("me_ready")
        gm_ready = sem("gm_ready")
        var_ready = sem("f_var_ready")
        sd_ready = sem("f_sd_ready")
        ab_ready = sem("ab_ready")
        z5_ready = sem("z5_ready")
        b5_summed = sem("b5_summed")
        b5_ready = sem("b5_ready")
        y_loaded = [sem(f"y_loaded{h}") for h in range(YR)]
        z_ready = sem("z_ready")
        fused = sem("fused")
        fu_ready = sem("fu_ready")
        fu_measured = sem("fu_measured")
        fme_ready = sem("fme_ready")
        fgm_ready = sem("fgm_ready")
        fvar_ready = sem("fvar_ready")
        fsd_ready = sem("fsd_ready")
        gate = sem("f_gate")
        block = ctx.enter_context(nc.Block())
        view = lambda t: t.rearrange("p (b n) -> p b n", b=B)

        @block.sync
        def _(sp):
            sp.dma_start(pw[:], pool_w).then_inc(params, 16)
            sp.dma_start(fw[:], fuse_w).then_inc(params, 16)
            sp.dma_start(gp[:], gnp).then_inc(params, 16)
            sp.dma_start(gf[:], gnf).then_inc(params, 16)
            with sp.Fori(0, NG // YR) as i:
                for h in range(YR):
                    sp.wait_ge(fused, i * YR + h + 1)
                    sp.dma_start(yin[h][:], y_dram[bass.ds(i * YR + h, 1), :, :, :, :]
                                 .rearrange("g b h p n -> (g p) (b h) n")).then_inc(y_loaded[h], 16)

        @block.tensor
        def _(pe):
            pe.sem_inc(fused, YR)
            pe.wait_ge(params, 64)
            pe.wait_ge(xm_ready, 1)
            for half in range(2):
                last = nc.tensor.matmul(ps_s[:, half, 0:B], pw[:, 128 * half:128 * half + 128], xmean[:, :],
                                        start=True, stop=True)
            last.then_inc(y5_ready, 1)
            pe.wait_ge(me_ready, 1)
            nc.tensor.matmul(ps_s[:, 0, 0:2 * B * NFC], blk16[:, :], flat(me[:]), start=True, stop=True)\
                .then_inc(gm_ready, 1)
            pe.wait_ge(z5_ready, 1)
            for half in range(2):
                last = nc.tensor.matmul(ps_s[:, 1, 0:B], fw[:, 2 * NBR + half, :], z5[:, half, :],
                                        start=(half == 0), stop=(half == 1))
            last.then_inc(b5_summed, 1)
            with pe.Fori(0, NG // YR) as i:
                for h in range(YR):
                    pe.wait_ge(z_ready, i * YR + h + 1)
                    pe.wait_ge(fu_ready, i * YR + h + 1)
                    for n in range(2 * NBR):
                        last = nc.tensor.matmul(ps_f[h][:, :], fw[:, n, :], yin[h][:, n, :],
                                                start=(n == 0), stop=(n == 2 * NBR - 1))
                    last.then_inc(fused, 1)
            pe.wait_ge(fme_ready, 1)
            nc.tensor.matmul(ps_s[:, 0, 0:2 * B], blk8[:, :], flat(fme[:]), start=True, stop=True).then_inc(fgm_ready, 1)

        @block.scalar
        def _(act):
            act.sem_inc(fu_ready, YR)
            act.wait_ge(var_ready, 1)
            nc.scalar.activation(sd[:], var[:], ACT.Sqrt, bias=eps5[:, 0:1]).then_inc(sd_ready, 1)
            act.wait_ge(ab_ready, 1)
            act.wait_ge(b5_ready, 1)
            act.sem_inc(gate, 1)
            with act.Fori(0, B) as b:
                with act.Fori(0, GI // YR) as i:
                    k = b * (GI // YR) + i

                    def copy_out(h):
                        act.wait_ge(fused, k * YR + h + 1 + YR)
                        act.sem_inc(gate, 1)
                        nc.scalar.activation(fu[:, bass.ds(b * HW + i * (YR * CH) + h * CH, CH)], ps_f[h][:, :],
                                             ACT.Identity, bias=bias5[:, bass.ds(b, 1)]).then_inc(fu_ready, 1)

                    for h in range(YR):
                        act.wait_ge(y_loaded[h], k * 16 + 16)
                        act.sem_inc(gate, 1)
                        for n in range(2 * NBR):
                            last = nc.scalar.activation(yin[h][:, n, :], yin[h][:, n, :], ACT.Relu,
                                                        bias=ybb[:, bass.ds(b * NFC + n, 1)],
                                                        scale=ya[:, bass.ds(b * NFC + n, 1)])
                        last.then_inc(z_ready, 1)
                        if h:
                            copy_out(h - 1)
                    copy_out(YR - 1)
            act.wait_ge(fvar_ready, 1)
            nc.scalar.activation(fsd[:], fvar[:], ACT.Sqrt, bias=eps5[:, 0:1]).then_inc(fsd_ready, 1)

        @block.vector
        def _(dve):
            st = Steps(dve, step)
            nc.vector.tensor_scalar(xmean[:], xsum[:], 1.0 / HW, None, ALU.mult).then_inc(xm_ready, 1)
            for b in range(B):
                for n in range(2 * NBR):
                    last = nc.vector.bn_aggr(mv[:, b, n, :], ystats[:, n, b * GI * 6:(b + 1) * GI * 6])
            st.then(last)
            m0, m1 = view(me[:, 0, :])[:, :, 0:2 * NBR], view(me[:, 1, :])[:, :, 0:2 * NBR]
            nc.vector.tensor_copy(m0, mv[:, :, :, 0])
            st.then(nc.vector.tensor_tensor(m1, mv[:, :, :, 0], mv[:, :, :, 0], ALU.mult))
            nc.vector.tensor_tensor(m1, m1, mv[:, :, :, 1], ALU.add)
            dve.wait_ge(y5_ready, 1)
            st.then(nc.vector.tensor_copy(y5[:], ps_s[:, :, 0:B].rearrange("p h b -> p b h")))
            nc.vector.tensor_copy(view(me[:, 0, :])[:, :, 2 * NBR:], y5[:])
            nc.vector.tensor_tensor(view(me[:, 1, :])[:, :, 2 * NBR:], y5[:], y5[:], ALU.mult).then_inc(me_ready, 1)
            dve.wait_ge(gm_ready, 1)
            st.then(nc.vector.tensor_copy(flat(gm[:]), ps_s[:, 0, 0:2 * B * NFC]))
            dve.wait_ge(params, 64)
            group_affine(dve, sd_ready, st, sq[:], var[:], sd[:], ya[:], ybb[:], gm, flat(gp[:, 0, :, :]),
                         flat(gp[:, 1, :, :]), var_ready, nc)
            dve.sem_inc(ab_ready, 1)
            z5v = z5[:].rearrange("p h b -> p b h")
            st.then(nc.vector.tensor_tensor(z5v, y5[:], view(ya[:])[:, :, 2 * NBR:], ALU.mult))
            st.then(nc.vector.tensor_tensor(z5v, z5v, view(ybb[:])[:, :, 2 * NBR:], ALU.add))
            nc.vector.tensor_scalar(z5[:], z5[:], 0.0, None, ALU.max).then_inc(z5_ready, 1)
            dve.wait_ge(b5_summed, 1)
            nc.vector.tensor_copy(bias5[:], ps_s[:, 1, 0:B]).then_inc(b5_ready, 1)
            with dve.Fori(0, NG // YR) as i:
                for h in range(YR):
                    dve.wait_ge(fu_ready, i * YR + h + 1 + YR)
                    dve.sem_inc(gate, 1)
                    nc.vector.bn_stats(fstats[:, bass.ds(i * (6 * YR) + h * 6, 6)],
                                       fu[:, bass.ds(i * (YR * CH) + h * CH, CH)]).then_inc(fu_measured, 1)
            dve.wait_ge(fu_measured, NG)
            for b in range(B):
                last = nc.vector.bn_aggr(fmv[:, b, :], fstats[:, b * GI * 6:(b + 1) * GI * 6])
            st.then(last)
            nc.vector.tensor_copy(fme[:, 0, :], fmv[:, :, 0])
            st.then(nc.vector.tensor_tensor(fme[:, 1, :], fmv[:, :, 0], fmv[:, :, 0], ALU.mult))
            nc.vector.tensor_tensor(fme[:, 1, :], fme[:, 1, :], fmv[:, :, 1], ALU.add).then_inc(fme_ready, 1)
            dve.wait_ge(fgm_ready, 1)
            st.then(nc.vector.tensor_copy(flat(fgm[:]), ps_s[:, 0, 0:2 * B]))
            group_affine(dve, fsd_ready, st, fsq[:], fvar[:], fsd[:], fa[:], fb[:], fgm, gf[:, 0, :], gf[:, 1, :],
                         fvar_ready, nc)


def stage_sum(nc, x, fu, fa, fb, accum):
    ctx = ExitStack()
    with ctx:
        sb = lambda name, shape, dt=F32: ctx.enter_context(nc.sbuf_tensor(name, shape, dt))
        sem = lambda name: ctx.enter_context(nc.semaphore(name))
        xg = [sb(f"t_xg{h}", [C, CH]) for h in range(2)]
        rb = [sb(f"t_rb{h}", [C, CH]) for h in range(2)]
        pair = lambda name: [sem(f"{name}{h}") for h in range(2)]
        x_loaded = pair("tx_loaded")
        relu_ready = pair("relu_ready")
        t_added = pair("t_added")
        gate = sem("t_gate")
        block = ctx.enter_context(nc.Block())
        NH = GI // 2

        @block.sync
        def _(sp):
            with sp.Fori(0, B) as b:
                with sp.Fori(0, NH) as i:
                    for h in range(2):
                        sp.wait_ge(t_added[h], b * NH + i + 1)
                        sp.dma_start(xg[h][:, :], x[bass.ds(b, 1), :, bass.ds(i * (2 * CH) + h * CH, CH)]
                                     .rearrange("b c n -> (b c) n")).then_inc(x_loaded[h], 16)

        @block.scalar
        def _(act):
            with act.Fori(0, B) as b:
                with act.Fori(0, NH) as i:
                    for h in range(2):
                        act.wait_ge(t_added[h], b * NH + i + 1)
                        act.sem_inc(gate, 1)
                        nc.scalar.activation(rb[h][:, :], fu[:, bass.ds(b * HW + i * (2 * CH) + h * CH, CH)], ACT.Relu,
                                             bias=fb[:, bass.ds(b, 1)], scale=fa[:, bass.ds(b, 1)])\
                            .then_inc(relu_ready[h], 1)

        @block.vector
        def _(dve):
            for h in range(2):
                dve.sem_inc(t_added[h], 1)
            with dve.Fori(0, B) as b:
                with dve.Fori(0, NH) as i:
                    for h in range(2):
                        k = b * NH + i
                        dve.wait_ge(x_loaded[h], k * 16 + 16)
                        dve.wait_ge(relu_ready[h], k + 1)
                        parity = lambda t: t[:, :].rearrange("p (n a) -> p a n", a=2)
                        nc.vector.tensor_tensor(
                            accum[:, bass.ds(b * 2, 2), bass.ds(i * CH + h * (CH // 2), CH // 2)],
                            parity(rb[h]), parity(xg[h]), ALU.add).then_inc(t_added[h], 1)


def stage_tokens(nc, ident, eps5, accum, uT, dft, dft_edge, spec_dram):
    ctx = ExitStack()
    with ctx:
        sb = lambda name, shape, dt=F32: ctx.enter_context(nc.sbuf_tensor(name, shape, dt))
        sem = lambda name: ctx.enter_context(nc.semaphore(name))
        tch = [sb(f"tch{h}", [C, 16 * NB]) for h in range(2)]
        un = [sb(f"un{h}", [128, 4, C]) for h in range(2)]
        stats = [sb(f"t_stats{h}", [128, 4, 6]) for h in range(2)]
        mv = [sb(f"t_mv{h}", [128, 4, 2]) for h in range(2)]
        sd = [sb(f"t_sd{h}", [128, 4]) for h in range(2)]
        rs = [sb(f"t_rs{h}", [128, 4]) for h in range(2)]
        fwd = sb("fwd", [128, 4 * 2 * NF])
        fwd_edge = sb("fwd_edge", [128, 2 * NF])
        spec = sb("spec", [C, NF, B, 2, 2, EX])
        ps_x = [ctx.enter_context(nc.psum_tensor(f"ps_tx{h}", [128, 4, C], F32)) for h in range(2)]
        ps_n = ctx.enter_context(nc.psum_tensor("ps_tn", [C, CH], F32))
        ps_d = [ctx.enter_context(nc.psum_tensor(f"ps_td{h}", [C, 2, CH], F32)) for h in range(2)]
        ps_e = ctx.enter_context(nc.psum_tensor("ps_te", [C, 2 * NF], F32))
        pair = lambda name: [sem(f"{name}{h}") for h in range(2)]
        params = sem("t_params")
        t_copied = pair("t_copied")
        t_turned = pair("t_turned")
        var_ready = pair("tvar_ready")
        sd_ready = pair("tsd_ready")
        u_ready = pair("u_ready")
        u_turned = sem("u_turned")
        uT_ready = sem("uT_ready")
        transformed = pair("transformed")
        spec_ready = pair("spec_ready")
        spec_stored = sem("spec_stored")
        edge_zeroed = sem("edge_zeroed")
        step = sem("t_step")
        gate = sem("t_gate")
        block = ctx.enter_context(nc.Block())
        HB = NG // 2
        blocks = lambda bp: accum[:, bass.ds(bp, 1), :].rearrange("c o (n s) -> c (o n) s", s=BS)

        @block.sync
        def _(sp):
            sp.dma_start(fwd[:], dft).then_inc(params, 16)
            sp.dma_start(fwd_edge[:], dft_edge).then_inc(params, 16)
            one = 2 * 2 * EX
            for b in range(B):
                for h in range(2):
                    sp.wait_ge(spec_ready[h], (b + 1) * (HB // B) + 1)
                sp.dma_start(spec_dram.rearrange("f d n -> d f n")[:, :, b * one:(b + 1) * one],
                             spec[:, :, b, :, :, :].rearrange("d f q r s -> d f (q r s)")).then_inc(spec_stored, 16)
            sp.wait_ge(spec_stored, 16 * B)

        @block.gpsimd
        def _(pool):
            pool.memset(uT[:, :, 0:1], 0.0).then_inc(edge_zeroed, 1)
            with pool.Fori(0, 2 * B) as bp:
                with pool.Fori(0, 2) as i:
                    for h in range(2):
                        pool.wait_ge(t_turned[h], bp * 2 + i + 1)
                        pool.sem_inc(gate, 1)
                        nc.gpsimd.tensor_copy(tch[h][:, :].rearrange("c (s n) -> c n s", n=NB),
                                              blocks(bp)[:, :, bass.ds(i * 32 + h * 16, 16)]).then_inc(t_copied[h], 1)

        @block.scalar
        def _(act):
            act.sem_inc(uT_ready, 1)
            for h in range(2):
                act.sem_inc(spec_ready[h], 1)
            act.wait_ge(edge_zeroed, 1)

            def root(k):
                for h in range(2):
                    act.wait_ge(var_ready[h], k + 1)
                    nc.scalar.activation(sd[h][:, :], mv[h][:, :, 1], ACT.Sqrt, bias=eps5[:, 0:1]).then_inc(sd_ready[h], 1)

            def copy_out(k):
                b, p, i = k // 4, (k // 2) % 2, k % 2
                for h in range(2):
                    act.wait_ge(u_turned, k * 2 + (h + 2))
                    act.sem_inc(gate, 1)
                    nc.scalar.activation(
                        uT[:, bass.ds(b * 2 + p, 1), 1:1 + HALF].rearrange("c o (n s) -> c (o n) s", s=BS)
                        [:, :, bass.ds(i * 32 + h * 16, 16)],
                        ps_n[:, :].rearrange("c (s n) -> c n s", n=NB), ACT.Copy).then_inc(uT_ready, 1)
                    act.wait_ge(transformed[h], k + 2)
                    act.sem_inc(gate, 1)
                    half = lambda lo, n: spec[:, :, bass.ds(b, 1), bass.ds(p, 1), :, bass.ds(lo, n)]\
                        .rearrange("d f b q r s -> d s r (f b q)")
                    for q in range(2):
                        last = nc.scalar.activation(
                            half((1 - i) * 32 + (16 - 16 * h + 8 * q), 8),
                            ps_d[h][:, q, :].rearrange("d (s r f) -> d s r f", r=2, f=NF), ACT.Copy)
                    if h == 1:
                        last = nc.scalar.activation(
                            spec[:, :, bass.ds(b, 1), bass.ds(p, 1), :, BS:EX].rearrange("d f b q r s -> d (r s) (f b q)"),
                            ps_e[:, :].rearrange("d (r f) -> d r f", r=2), ACT.Copy)
                    last.then_inc(spec_ready[h], 1)

            root(0)
            act.sem_inc(gate, 1)
            with act.Fori(0, HB - 1) as k:
                root(k + 1)
                copy_out(k)
            copy_out(HB - 1)
            act.wait_ge(uT_ready, NG + 1)

        @block.tensor
        def _(pe):
            pe.sem_inc(u_turned, 1)
            for h in range(2):
                pe.sem_inc(t_turned[h], 1)
                pe.sem_inc(transformed[h], 1)
            pe.wait_ge(params, 32)

            def turn(k, h):
                pe.wait_ge(t_copied[h], k + 1)
                pe.wait_ge(u_ready[h], k + 1)
                for j in range(4):
                    last = nc.tensor.transpose(ps_x[h][:, j, :], tch[h][:, 128 * j:128 * j + 128], ident[:, :])
                last.then_inc(t_turned[h], 1)

            def transform(before, h):
                pe.wait_ge(u_ready[h], before + 1)
                pe.wait_ge(uT_ready, before * 2 + (h - 1))
                for j in range(4):
                    last = nc.tensor.transpose(ps_n[:, 128 * j:128 * j + 128], un[h][:, j, :], ident[:, :])
                last.then_inc(u_turned, 1)
                pe.wait_ge(spec_ready[h], before)
                for j in range(4):
                    o = ps_d[h][:, (3 - j) // 2, 256 * ((3 - j) % 2):256 * ((3 - j) % 2) + 256]
                    last = nc.tensor.matmul(o, un[h][:, j, :], fwd[:, :], start=True, stop=True)
                if h == 1:
                    last = nc.tensor.matmul(ps_e[:, :], un[h][:, 3, :], fwd_edge[:, :], start=True, stop=True)
                last.then_inc(transformed[h], 1)

            for h in range(2):
                turn(0, h)
            with pe.Fori(1, HB) as k:
                for h in range(2):
                    turn(k, h)
                for h in range(2):
                    transform(k, h)
            for h in range(2):
                transform(HB, h)

        @block.vector
        def _(dve):
            for h in range(2):
                dve.sem_inc(u_ready[h], 1)
            with dve.Fori(0, HB) as k:
                st = Steps(dve, step, k * 4)
                for h in range(2):
                    dve.wait_ge(t_turned[h], k + 2)
                    for j in range(4):
                        last = nc.vector.bn_stats(stats[h][:, j, :], ps_x[h][:, j, :])
                    st.then(last)
                    dve.sem_inc(gate, 1)
                    for j in range(4):
                        last = nc.vector.bn_aggr(mv[h][:, j, :], stats[h][:, j, :])
                    last.then_inc(var_ready[h], 1)
                for h in range(2):
                    dve.wait_ge(sd_ready[h], k + 1)
                    st.then(nc.vector.reciprocal(rs[h][:, :], sd[h][:, :]))
                    dve.wait_ge(transformed[h], k + 1)
                    for j in range(4):
                        last = nc.vector.tensor_scalar(un[h][:, j, :], ps_x[h][:, j, :], mv[h][:, j, 0:1],
                                                       rs[h][:, j:j + 1], ALU.subtract, ALU.mult)
                    last.then_inc(u_ready[h], 1)


def segments(r):
    return ((0, 256, 0), (256, 512, 1)) if r == 0 else ((0, 512, min(r + 1, SEG - 1)),)


def stage_mixtures(nc, phi, dft_taps, m_phi, m_u, sigma, logw, gumbel, accum, uT, mh, ml, hot, kern_dram):
    ctx = ExitStack()
    with ctx:
        sb = lambda name, shape, dt=F32: ctx.enter_context(nc.sbuf_tensor(name, shape, dt))
        sem = lambda name: ctx.enter_context(nc.semaphore(name))
        lw = sb("lw", [128, SEG])
        gb = sb("gb", [128, SEG])
        sm = sb("sm", [128, 4])
        ys = sb("ys", [128, SEG])
        wi = sb("wi", [128, SEG])
        sg = sb("sigma_b", [128, KF])
        mu = sb("mu", [C, SEG, 3, C])
        mus = sb("mus", [C, 3, SEG, C])
        mr = [sb(f"mr{h}", [C, KC, 2, SEG, C]) for h in range(2)]
        mw = [sb(f"mw{h}", [C, KC, 2, C]) for h in range(2)]
        mt = [sb(f"mt{h}", [C, 2, KC, C]) for h in range(2)]
        windows = sb("windows", [NB, 2 * KF, 2 * BS])
        taps_dft = sb("taps_dft", [NB, 4 * NF])
        kern = sb("kern", [128, 2 * KF, 2 * BS])
        ps_m = [ctx.enter_context(nc.psum_tensor(f"ps_m{q}", [C, CH], F32)) for q in range(2)]
        ps_k = [ctx.enter_context(nc.psum_tensor(f"ps_k{q}", [128, CH], F32)) for q in range(2)]
        pair = lambda name: [sem(f"{name}{h}") for h in range(2)]
        params = sem("s_params")
        phi_loaded = sem("phi_loaded")
        step = sem("s_step")
        z_ready = sem("s_z_ready")
        e_ready = sem("s_e_ready")
        sig_rooted = sem("sig_rooted")
        mus_ready = sem("mus_ready")
        m_loaded = pair("m_loaded")
        mt_ready = sem("mt_ready")
        m_rounded = sem("m_rounded")
        m_split = sem("m_split")
        mixed = sem("mixed")
        added = sem("added")
        k_done = sem("k_done")
        k_copied = sem("k_copied")
        k_stored = sem("k_stored")
        block = ctx.enter_context(nc.Block())
        regions = [(b, p, r) for b in range(B) for p in range(2) for r in range(4)]
        NR = len(regions)
        PADC = HALF + BS
        NK = 2 * KF * 2 * BS // CH

        @block.sync
        def _(sp):
            sp.dma_start(taps_dft[:], dft_taps).then_inc(phi_loaded, 16)
            sp.dma_start(windows[:], bass.AP(tensor=phi.tensor, offset=0, ap=[[BS, NB], [PADC, 2 * KF], [1, 2 * BS]]))\
                .then_inc(phi_loaded, 16)
            one = lambda t, n: t.rearrange("(a k) -> a k", a=1).to_broadcast([128, n])
            sp.dma_start(lw[:], one(logw, SEG)).then_inc(params, 16)
            sp.dma_start(gb[:], one(gumbel, SEG)).then_inc(params, 16)
            sp.dma_start(sg[:], one(sigma, KF)).then_inc(params, 16)
            sp.dma_start(mu[:], m_u).then_inc(params, 16)
            for c in range(KF // KC):
                if c >= 2:
                    sp.wait_ge(mt_ready, c - 1)
                sp.dma_start(mr[c % 2][:], m_phi[KC * c:KC * c + KC].rearrange("k d s i e -> d k s i e"))\
                    .then_inc(m_loaded[c % 2], 16)
            sp.wait_ge(k_copied, NK)
            sp.dma_start(kern_dram, kern[:].rearrange("p k n -> p (k n)")).then_inc(k_stored, 16)
            sp.wait_ge(k_stored, 16)

        @block.scalar
        def _(act):
            act.wait_ge(params, 64)
            act.wait_ge(z_ready, 1)
            nc.scalar.activation(ys[:], lw[:], ACT.Exp, bias=sm[:, 1:2]).then_inc(e_ready, 1)
            nc.scalar.activation(sg[:], sg[:], ACT.Sqrt).then_inc(sig_rooted, 1)
            act.wait_ge(sig_rooted, 1)
            nc.scalar.activation(sg[:], sg[:], ACT.Sqrt).then_inc(sig_rooted, 1)
            for n in range(NK):
                act.wait_ge(k_done, n + 1)
                nc.scalar.activation(flat(kern[:])[:, n * CH:(n + 1) * CH], ps_k[n % 2][:, :], ACT.Copy).then_inc(k_copied, 1)
            act.wait_ge(sig_rooted, 2)
            for k in range(KF):
                c, n = divmod(k, KC)
                act.wait_ge(mt_ready, c + 1)
                nc.scalar.activation(mh[:, :, k, :], mt[c % 2][:, :, n, :], ACT.Copy, scale=sg[:, k:k + 1])\
                    .then_inc(m_rounded, 1)

        @block.vector
        def _(dve):
            dve.sem_inc(added, 2)
            st = Steps(dve, step)
            dve.wait_ge(params, 64)
            st.then(nc.vector.tensor_tensor(lw[:], lw[:], gb[:], ALU.add))
            st.then(nc.vector.tensor_reduce(sm[:, 0:1], lw[:], AX.X, ALU.max))
            nc.vector.tensor_scalar(sm[:, 1:2], sm[:, 0:1], -1.0, None, ALU.mult).then_inc(z_ready, 1)
            dve.wait_ge(e_ready, 1)
            st.then(nc.vector.tensor_reduce(sm[:, 2:3], ys[:], AX.X, ALU.add))
            st.then(nc.vector.reciprocal(sm[:, 3:4], sm[:, 2:3]))
            st.then(nc.vector.tensor_scalar(ys[:], ys[:], sm[:, 3:4], None, ALU.mult))
            st.then(nc.vector.tensor_reduce(sm[:, 0:1], ys[:], AX.X, ALU.max))
            st.then(nc.vector.tensor_scalar(hot[:], ys[:], sm[:, 0:1], None, ALU.is_ge))
            st.then(nc.vector.tensor_scalar(sm[:, 2:3], sm[:, 3:4], 0.0, 1.0, ALU.mult, ALU.add))
            for i in range(SEG):
                st.then(nc.vector.tensor_tensor(hot[:, i:i + 1], hot[:, i:i + 1], sm[:, 2:3], ALU.mult))
                st.then(nc.vector.tensor_tensor(sm[:, 2:3], sm[:, 2:3], hot[:, i:i + 1], ALU.subtract))
            st.then(nc.vector.tensor_tensor(wi[:], hot[:], ys[:], ALU.subtract))
            st.then(nc.vector.tensor_tensor(wi[:], wi[:], ys[:], ALU.add))
            st.then(nc.vector.tensor_scalar(mus[:, :, SEG - 1, :], mu[:, 0, :, :], wi[:, 0:1], None, ALU.mult))
            for i in range(1, SEG):
                ins = nc.vector.scalar_tensor_tensor(mus[:, :, SEG - 1 - i, :], mu[:, i, :, :], wi[:, i:i + 1],
                                                     mus[:, :, SEG - i, :], ALU.mult, ALU.add)
                if i < SEG - 1:
                    st.then(ins)
                else:
                    ins.then_inc(mus_ready, 1)
            n = 0

            def add_regions(hi):
                nonlocal n
                while n < hi:
                    b, p, r = regions[n]
                    dve.wait_ge(mixed, n + 1)
                    acc = accum[:, 2 * b + p, CH * r:CH * r + CH]
                    nc.vector.tensor_tensor(acc, acc, ps_m[n % 2][:, :], ALU.add).then_inc(added, 1)
                    n += 1

            dve.wait_ge(sig_rooted, 2)
            for c in range(KF // KC):
                h = c % 2
                dve.wait_ge(m_loaded[h], 16 * (c // 2 + 1))
                for i in range(SEG):
                    if i == 0:
                        st.then(nc.vector.tensor_scalar(mw[h][:], mr[h][:, :, :, 0, :], wi[:, 0:1], None, ALU.mult))
                    else:
                        st.then(nc.vector.scalar_tensor_tensor(mw[h][:], mr[h][:, :, :, i, :], wi[:, i:i + 1], mw[h][:],
                                                               ALU.mult, ALU.add))
                nc.vector.tensor_tensor(mt[h][:, 0, :, :], mw[h][:, :, 0, :], mw[h][:, :, 1, :], ALU.add)
                nc.vector.tensor_tensor(mt[h][:, 1, :, :], mw[h][:, :, 0, :], mw[h][:, :, 1, :], ALU.subtract)\
                    .then_inc(mt_ready, 1)
                add_regions(NR * (c + 1) // (KF // KC))
                for k in range(KC * c, KC * c + KC):
                    dve.wait_ge(m_rounded, k + 1)
                    nc.vector.scalar_tensor_tensor(ml[:, :, k, :], mt[h][:, :, k - KC * c, :], sg[:, k:k + 1],
                                                   mh[:, :, k, :].bitcast(F32), ALU.mult, ALU.subtract).then_inc(m_split, 1)
            dve.wait_ge(m_split, KF)

        @block.tensor
        def _(pe):
            pe.wait_ge(phi_loaded, 32)
            for n in range(NK):
                if n >= 2:
                    pe.wait_ge(k_copied, n - 1)
                nc.tensor.matmul(ps_k[n % 2][:, :], taps_dft[:, :], flat(windows[:])[:, n * CH:(n + 1) * CH],
                                 start=True, stop=True).then_inc(k_done, 1)
            pe.wait_ge(mus_ready, 1)
            for n, (b, p, r) in enumerate(regions):
                pe.wait_ge(added, n + 1)
                for s, (lo, hi, seg) in enumerate(segments(r)):
                    for lag in range(3):
                        q, shift = (p - lag) % 2, (p - lag) // 2
                        c0 = 1 + CH * r + lo + shift
                        last = nc.tensor.matmul(ps_m[n % 2][:, lo:hi], mus[:, lag, seg, :], uT[:, 2 * b + q, c0:c0 + hi - lo],
                                                start=(s == 0 and lag == 0), stop=(lag == 2), skip_group_check=True)
                last.then_inc(mixed, 1)


def stage_spectral(nc, spec_dram, kern_dram, y2_dram, mh, ml):
    ctx = ExitStack()
    with ctx:
        sb = lambda name, shape, dt=F32: ctx.enter_context(nc.sbuf_tensor(name, shape, dt))
        sem = lambda name: ctx.enter_context(nc.semaphore(name))
        u0 = [sb(f"u0{h}", [C, B, 2, 2, EX]) for h in range(2)]
        up = sb("up", [C, B, 3, 2, BS])
        uh = [sb(f"uh{h}", [C, B, 3, 2 * BS], F32R) for h in range(2)]
        ul = [sb(f"ul{h}", [C, B, 3, 2 * BS], F32R) for h in range(2)]
        t0 = sb("toeplitz0", [128, 2 * KF, 128])
        th = [sb(f"th{h}", [128, 2 * KF, 128], F32R) for h in range(2)]
        tl = [sb(f"tl{h}", [128, 2 * KF, 128], F32R) for h in range(2)]
        ph = [sb(f"ph{h}", [128, KC, 2, B, C], F32R) for h in range(2)]
        pl = [sb(f"pl{h}", [128, KC, 2, B, C], F32R) for h in range(2)]
        yo = [sb(f"yo{h}", [128, CH]) for h in range(2)]
        BANKS = 4
        ps_p = [ctx.enter_context(nc.psum_tensor(f"ps_p{q}", [128, KC, C], F32)) for q in range(BANKS)]
        ps_y = [ctx.enter_context(nc.psum_tensor(f"ps_yf{q}", [128, CH], F32)) for q in range(2)]
        pair = lambda name: [sem(f"{name}{h}") for h in range(2)]
        u_loaded = pair("sp_u_loaded")
        t_loaded = sem("sp_t_loaded")
        t_split = sem("t_split")
        pool_step = sem("pool_step")
        split = pair("split")
        p_mixed = sem("p_mixed")
        p_high = sem("p_high")
        p_low = sem("p_low")
        convolved = sem("sp_convolved")
        y_copied = sem("y_copied")
        y_stored = pair("sp_y_stored")
        gate = sem("sp_gate")
        block = ctx.enter_context(nc.Block())
        NC = 2 * KF // KC
        TILES = 2 * B
        tiles = [(q, b) for q in range(2) for b in range(B)]
        SRC = {(0, 0): 0, (0, 1): 1, (1, 0): 2, (1, 1): 0}

        @block.sync
        def _(sp):
            for h in range(2):
                sp.sem_inc(y_stored[h], 16)
            with sp.Fori(0, NF // 2) as i:
                for h in range(2):
                    f = i * 2 + h
                    sp.wait_ge(t_split, f + 1)
                    sp.dma_start(u0[h][:].rearrange("d b q r s -> d (b q r s)"),
                                 spec_dram[bass.ds(f, 1), :, :].rearrange("f d n -> (f d) n")).then_inc(u_loaded[h], 16)
                    for g in range(2):
                        for c in range(2):
                            src = bass.AP(tensor=kern_dram.tensor, offset=(2 * g + c) * NF * 2 * KF * 2 * BS + 1,
                                          ap=[[2 * KF * 2 * BS, NF], [1, BS], [2 * BS, 2 * KF], [1, BS]])
                            sp.dma_start(t0[BS * g:BS * g + BS, :, BS * c:BS * c + BS],
                                         src[bass.ds(f, 1), :, :, :].rearrange("f s k r -> (f s) k r")).then_inc(t_loaded, 16)

        @block.gpsimd
        def _(pool):
            pool.sem_inc(t_split, 1)
            with pool.Fori(0, NF // 2) as i:
                for h in range(2):
                    pool.wait_ge(convolved, i * (2 * NC) + (h + 1) * NC)
                    pool.wait_ge(u_loaded[h], i * 16 + 16)
                    pool.sem_inc(gate, 1)
                    nc.gpsimd.tensor_copy(up[:, :, 0:2, :, :], u0[h][:, :, :, :, 0:BS])
                    nc.gpsimd.tensor_copy(up[:, :, 2, :, :], u0[h][:, :, 1, :, 1:EX]).then_inc(pool_step, 1)
                    pool.wait_ge(pool_step, i * 6 + (h * 3 + 1))
                    pool.sem_inc(gate, 1)
                    upf = up[:].rearrange("d b q r s -> d (b q r s)")
                    nc.gpsimd.tensor_copy(flat(uh[h][:]), upf).then_inc(pool_step, 1)
                    pool.wait_ge(pool_step, i * 6 + (h * 3 + 2))
                    nc.gpsimd.tensor_tensor(flat(ul[h][:]), upf, flat(uh[h][:]).bitcast(F32), ALU.subtract)
                    pool.wait_ge(t_loaded, (i * 2 + h) * 64 + 64)
                    pool.sem_inc(gate, 1)
                    nc.gpsimd.tensor_copy(flat(th[h][:]), flat(t0[:])).then_inc(pool_step, 1)
                    pool.wait_ge(pool_step, i * 6 + (h * 3 + 3))
                    nc.gpsimd.tensor_tensor(flat(tl[h][:]), flat(t0[:]), flat(th[h][:]).bitcast(F32), ALU.subtract)\
                        .then_inc(split[h], 1)
                    pool.wait_ge(split[h], i + 1)
                    pool.sem_inc(t_split, 1)

        def dest(t, q, b):
            return t[:, :, q, b, :]

        @block.scalar
        def _(act):
            act.sem_inc(y_copied, 2)
            with act.Fori(0, NF // 2) as i:
                for h in range(2):
                    f = i * 2 + h
                    for kc in range(NC):
                        c = f * NC + kc
                        act.wait_ge(convolved, c + (2 * NC - 1))
                        act.sem_inc(gate, 1)
                        for n, (q, b) in enumerate(tiles):
                            act.wait_ge(p_mixed, c * TILES + n + 1)
                            nc.scalar.activation(dest(ph[kc % 2], q, b), ps_p[n % BANKS][:, :, :], ACT.Copy)\
                                .then_inc(p_high, 1)
                    act.wait_ge(convolved, f * NC + 3 * NC)
                    act.wait_ge(y_stored[h], i * 16 + 16)
                    act.sem_inc(gate, 1)
                    nc.scalar.activation(yo[h][:, :], ps_y[h][:, :], ACT.Copy).then_inc(y_copied, 1)
                    act.wait_ge(y_copied, f + 3)
                    act.dma_start(y2_dram[bass.ds(f, 1), :, :].rearrange("f p n -> (f p) n"), yo[h][:, :])\
                        .then_inc(y_stored[h], 16)
            for h in range(2):
                act.wait_ge(y_stored[h], 16 * (NF // 2 + 1))

        @block.vector
        def _(dve):
            dve.sem_inc(p_low, BANKS)
            with dve.Fori(0, NF) as f:
                for kc in range(NC):
                    for n, (q, b) in enumerate(tiles):
                        dve.wait_ge(p_high, (f * NC + kc) * TILES + n + 1)
                        nc.vector.tensor_tensor(dest(pl[kc % 2], q, b), ps_p[n % BANKS][:, :, :],
                                                dest(ph[kc % 2], q, b).bitcast(F32), ALU.subtract).then_inc(p_low, 1)

        @block.tensor
        def _(pe):
            pe.sem_inc(convolved, 2 * NC)

            def product(out, wh, wl, xh, xl, first, last):
                nc.tensor.matmul(out, wh, xh, start=first, stop=False)
                nc.tensor.matmul(out, wh, xl, start=False, stop=False)
                return nc.tensor.matmul(out, wl, xh, start=False, stop=last)

            with pe.Fori(0, NF // 2) as i:

                def mix(h, kc):
                    c = (i * 2 + h) * NC + kc
                    for n, (q, b) in enumerate(tiles):
                        pe.wait_ge(p_low, c * TILES + n + 1)
                        s = SRC[kc % 2, q]
                        m = [t[:, kc % 2, KC * (kc // 2):KC * (kc // 2) + KC, :].rearrange("d k e -> d (k e)") for t in (mh, ml)]
                        product(flat(ps_p[n % BANKS][:]), uh[h][:, b, s, :], ul[h][:, b, s, :], *m, True, True)\
                            .then_inc(p_mixed, 1)

                def convolve(h, kc):
                    c = (i * 2 + h) * NC + kc
                    pe.wait_ge(p_low, (c + 1) * TILES + BANKS)
                    if kc == 0:
                        pe.wait_ge(y_copied, i * 2 + h + 1)
                    for k in range(KC):
                        x = [t[kc % 2][:, k, :, :, :].rearrange("p q b e -> p (q b e)") for t in (ph, pl)]
                        w = [t[h][:, 2 * (KC * (kc // 2) + k) + kc % 2, :] for t in (th, tl)]
                        last = product(ps_y[h][:, :], *w, *x, kc == 0 and k == 0, kc == NC - 1 and k == KC - 1)
                    last.then_inc(convolved, 1)

                chunks = [(h, kc) for h in range(2) for kc in range(NC)]
                for n, (h, kc) in enumerate(chunks):
                    if kc == 0:
                        pe.wait_ge(split[h], i + 1)
                    mix(h, kc)
                    if n:
                        convolve(*chunks[n - 1])
                convolve(*chunks[-1])


def stage_output(nc, y2_dram, idft, hot, accum, out):
    ctx = ExitStack()
    with ctx:
        sb = lambda name, shape, dt=F32: ctx.enter_context(nc.sbuf_tensor(name, shape, dt))
        sem = lambda name: ctx.enter_context(nc.semaphore(name))
        inv = sb("inv", [128, NB])
        reach = sb("reach", [128, 2, NB])
        RC = 16
        yd = [sb(f"yd{h}", [128, RC // 2, CH]) for h in range(2)]
        ob = [sb(f"ob{h}", [C, CH]) for h in range(2)]
        ps_i = [ctx.enter_context(nc.psum_tensor(f"ps_i{q}", [C, RC, NB], F32)) for q in range(2)]
        pair = lambda name: [sem(f"{name}{h}") for h in range(2)]
        inv_loaded = sem("inv_loaded")
        inv_ready = sem("inv_ready")
        step = sem("out_step")
        y_loaded = pair("oy_loaded")
        inverted = sem("inverted")
        added = sem("out_added")
        o_ready = pair("o_ready")
        o_stored = pair("o_stored")
        block = ctx.enter_context(nc.Block())
        parts = BS // RC
        NT = parts * 2 * B

        @block.sync
        def _(sp):
            for r in range(2):
                sp.dma_start(inv[64 * r:64 * r + 64, :], idft).then_inc(inv_loaded, 16)
            for c in range(parts):
                if c >= 2:
                    sp.wait_ge(inverted, (c - 1) * 2 * B)
                for r in range(2):
                    src = y2_dram.rearrange("f (g s r) n -> r (f g) s n", g=2, r=2)[r]
                    sp.dma_start(yd[c % 2][64 * r:64 * r + 64, :, :], src[:, RC // 2 * c:RC // 2 * (c + 1), :])\
                        .then_inc(y_loaded[c % 2], 16)
            for n in range(NG):
                b, g = divmod(n, GI)
                sp.wait_ge(o_ready[n % 2], n // 2 + 1)
                sp.dma_start(out[b, :, g * CH:(g + 1) * CH], ob[n % 2][:, :]).then_inc(o_stored[n % 2], 16)
            for h in range(2):
                sp.wait_ge(o_stored[h], 16 * (NG // 2))

        @block.vector
        def _(dve):
            dve.sem_inc(added, 2)
            st = Steps(dve, step)
            dve.wait_ge(inv_loaded, 32)
            st.then(nc.vector.memset(reach[:], 0.0))
            for i in range(SEG):
                n = NB >> i
                for r in range(2):
                    half = slice(64 * r, 64 * r + 64)
                    ins = nc.vector.scalar_tensor_tensor(reach[half, r, 0:n], inv[half, 0:n], hot[half, i:i + 1],
                                                         reach[half, r, 0:n], ALU.mult, ALU.add)
                if i < SEG - 1:
                    st.then(ins)
                else:
                    ins.then_inc(inv_ready, 1)
            n = 0
            for c in range(parts):
                for p in range(2):
                    for b in range(B):
                        dve.wait_ge(inverted, n + 1)
                        acc = accum[:, 2 * b + p, :].rearrange("e (n s) -> e n s", s=BS)[:, :, RC * c:RC * c + RC]
                        nc.vector.tensor_tensor(acc, acc, ps_i[n % 2][:].rearrange("e s n -> e n s"), ALU.add)\
                            .then_inc(added, 1)
                        n += 1
            dve.wait_ge(added, NT + 2)
            for n in range(NG):
                b, g = divmod(n, GI)
                if n >= 2:
                    dve.wait_ge(o_stored[n % 2], 16 * (n // 2))
                nc.vector.tensor_copy(ob[n % 2][:, :].rearrange("p (n a) -> p a n", a=2),
                                      accum[:, 2 * b:2 * b + 2, g * (CH // 2):(g + 1) * (CH // 2)]).then_inc(o_ready[n % 2], 1)

        @block.tensor
        def _(pe):
            pe.wait_ge(inv_ready, 1)
            n = 0
            for c in range(parts):
                pe.wait_ge(y_loaded[c % 2], 32 * (c // 2 + 1))
                for p in range(2):
                    for b in range(B):
                        pe.wait_ge(added, n + 1)
                        for r in range(RC // 2):
                            lhs = yd[c % 2][:, r, (p * B + b) * C:(p * B + b) * C + C]
                            last = nc.tensor.matmul(ps_i[n % 2][:, 2 * r:2 * r + 2, :], lhs, reach[:, :, :],
                                                    start=True, stop=True)
                        last.then_inc(inverted, 1)
                        n += 1


def program(nc, d):
    ctx = ExitStack()
    with ctx:
        sb = lambda name, shape, dt=F32: ctx.enter_context(nc.sbuf_tensor(name, shape, dt))
        table = nc.dram_tensor("table", (B * TROWS, 4 * C), F32, kind="Internal").ap()
        xn_dram = nc.dram_tensor("xn_dram", (C, XR, HP), F32, kind="Internal").ap()
        spec_dram = nc.dram_tensor("spec_dram", (NF, C, B * 2 * 2 * EX), F32, kind="Internal").ap()
        kern_dram = nc.dram_tensor("kern_dram", (4 * NF, 2 * KF * 2 * BS), F32, kind="Internal").ap()
        y2_dram = nc.dram_tensor("y2_dram", (NF, 128, CH), F32, kind="Internal").ap()
        y_dram = nc.dram_tensor("y_dram", (NG, NBR, 2, 128, CH), F32, kind="Internal").ap()
        ident = sb("ident", [128, 128])
        blk16 = sb("blk16", [128, 128])
        blk8 = sb("blk8", [128, 128])
        eps6 = sb("eps6", [128, 1])
        eps5 = sb("eps5", [128, 1])
        xsum = sb("xsum", [C, B])
        ystats = sb("ystats", [128, 2 * NBR, NG * 6])
        fa = sb("fa", [C, B])
        fb = sb("fb", [C, B])
        const_loaded = ctx.enter_context(nc.semaphore("const_loaded"))
        with nc.Block() as block:
            @block.sync
            def _(sp):
                for t, name in ((ident, "ident"), (blk16, "blk16"), (blk8, "blk8")):
                    sp.dma_start(t[:], d[name]).then_inc(const_loaded, 16)
                sp.wait_ge(const_loaded, 48)

            @block.gpsimd
            def _(pool):
                pool.memset(eps6[:], 1e-6)
                pool.memset(eps5[:], 1e-5)

        with nc.sbuf_tensor("wom", [C, 49, 3, TAPS], F32) as wom:
            stage_normalise(nc, d["x"], table, ident, eps6, xsum, xn_dram, d["w_om"], wom)
            stage_branches(nc, xn_dram, table, wom, d["base_om"], d["bias_om"], d["row_off"], d["img_off"], d["regw"],
                           ident, y_dram, ystats)
        accum = sb("accum", [C, 2 * B, HALF])
        hot = sb("hot", [128, SEG])
        mh = sb("mh", [C, 2, KF, C], F32R)
        ml = sb("ml", [C, 2, KF, C], F32R)
        with nc.sbuf_tensor("uT", [C, 2 * B, HALF + 1], F32) as uT:
            with nc.sbuf_tensor("fu", [C, B * HW], F32) as fu:
                stage_fuse(nc, y_dram, ystats, xsum, d["pool_w"], d["fuse_w"], d["gnp"], d["gnf"], blk16, blk8, eps5,
                           fu, fa, fb)
                stage_sum(nc, d["x"], fu, fa, fb, accum)
            stage_tokens(nc, ident, eps5, accum, uT, d["dft"], d["dft_edge"], spec_dram)
            stage_mixtures(nc, d["phi"], d["dft_taps"], d["m_phi"], d["m_u"], d["sigma"], d["logw"], d["gumbel"], accum,
                           uT, mh, ml, hot, kern_dram)
        stage_spectral(nc, spec_dram, kern_dram, y2_dram, mh, ml)
        stage_output(nc, y2_dram, d["idft"], hot, accum, d["out"])


def kernel(**inputs):
    import numpy as np
    import concourse.bacc as bacc
    from concourse.bass_utils import run_bass_kernel_spmd as run

    g = {n: np.asarray(v) for n, v in inputs.items()}
    P = "L0_conv_"
    f = np.float32
    a = {}
    a["x"] = g["x"].reshape(B, C, HW)
    w_om = np.zeros((C, 7, 7, 3, TAPS), f)
    bias_om = np.zeros((3, TAPS), f)
    base = np.zeros((128, 3, TAPS), f)
    regw = np.zeros((C, TAPS, O), f)
    p = np.arange(128)
    t0 = 0
    for name, k in (("b4", 7), ("b3", 3), ("b1", 1), ("b2", 1)):
        n, lo = k * k, (7 - k) // 2
        offw = g[P + name + "_offw"].reshape(n, 2, C, k, k)
        w_om[:, lo:lo + k, lo:lo + k, 0:2, t0:t0 + n] = offw.transpose(2, 3, 4, 1, 0)
        w_om[:, lo:lo + k, lo:lo + k, 2, t0:t0 + n] = g[P + name + "_modw"].transpose(1, 2, 3, 0)
        bias_om[0:2, t0:t0 + n] = g[P + name + "_offb"].reshape(n, 2).T
        bias_om[2, t0:t0 + n] = g[P + name + "_modb"]
        ky, kx = np.divmod(np.arange(n), k)
        base[:, 0, t0:t0 + n] = (p[:, None] // W) + ky - k // 2 + 2
        base[:, 1, t0:t0 + n] = (p[:, None] % W) + kx - k // 2 + 2
        regw[:, t0:t0 + n, :] = g[P + name + "_regw"].reshape(O, C, n).transpose(1, 2, 0)
        t0 += n
    a["w_om"] = w_om.reshape(C, 49, 3, TAPS)
    a["bias_om"], a["base_om"], a["regw"] = bias_om, base, regw
    m = np.arange((NG + 1) * 4)
    a["row_off"] = np.broadcast_to((2 * (m % (4 * GI))).astype(f), (128, m.size))
    a["img_off"] = np.broadcast_to((np.minimum(m // (4 * GI), B - 1) * TROWS).astype(f), (128, m.size))
    order = ("b4", "b3", "b1", "b2", "pool")
    gnp = np.stack([np.concatenate([g[P + n + s].reshape(2, 128) for n in order]) for s in ("_gng", "_gnb")])
    a["gnp"] = np.repeat(gnp.transpose(2, 0, 1)[:, :, None, :], B, axis=2)
    a["gnf"] = np.repeat(np.stack([g[P + "fuse_gng"], g[P + "fuse_gnb"]], 1)[:, :, None], B, axis=2)
    fw = g[P + "fuse_w"].reshape(C, 5, 2, 128)[:, [3, 2, 0, 1, 4]]
    a["fuse_w"] = fw.reshape(C, NFC, 128).transpose(2, 1, 0)
    a["pool_w"] = g[P + "pool_w"].reshape(O, C).T
    a["ident"] = np.eye(128, dtype=f)
    grp = lambda n: (p[:, None] // n == p[None, :] // n).astype(f) / f(n)
    a["blk16"], a["blk8"] = grp(O // 16), grp(C // 16)
    Q = "L0_ffn_"
    phi = np.zeros((KF, 2, BS + HALF), f)
    phi[:, :, BS:] = g[Q + "phi"].reshape(HALF, 2, KF).transpose(2, 1, 0)
    a["phi"] = phi
    a["m_phi"] = np.stack([g[Q + "M_phi_plus"], g[Q + "M_phi_minus"]]).transpose(2, 3, 0, 1, 4)
    a["m_u"] = g[Q + "M_u"].transpose(2, 0, 1, 3)
    w = 2 * np.pi / (2 * NB)
    blk, frq = np.arange(NB)[:, None], np.arange(NF)[None, :]

    def transform(n):
        re, im = np.cos(w * n * frq), -np.sin(w * n * frq)
        im[:, 0] = np.where(n[:, 0] % 2, -1.0, 1.0)
        return re, im

    re, im = transform(blk)
    dft = np.zeros((4, NB, 4, 2, NF))
    for s in range(4):
        dft[s, :, 3 - s, 0], dft[s, :, 3 - s, 1] = re, im
    a["dft"] = dft.reshape(128, 4 * 2 * NF).astype(f)
    edge = np.zeros((4, NB, 2, NF))
    edge[3, :, 0], edge[3, :, 1] = transform(blk + 1)
    a["dft_edge"] = edge.reshape(128, 2 * NF).astype(f)
    quarters = np.stack([re, im, -im, re], 1)
    quarters[:, 1, 0] = quarters[:, 2, 0] = 0.0
    quarters[:, 3, 0] = im[:, 0]
    a["dft_taps"] = quarters.reshape(NB, 4 * NF).astype(f)
    idft = np.stack([2 * np.cos(w * blk * frq), -2 * np.sin(w * blk * frq)], 2)
    idft[:, 0, 0], idft[:, 0, 1] = 1.0, im[:, 0]
    a["idft"] = (idft / (2 * NB)).reshape(NB, 2 * NF).T.astype(f)
    a["sigma"], a["logw"], a["gumbel"] = g[Q + "sigma"], g[Q + "log_weights"], g[Q + "gumbel"]
    a = {n: np.ascontiguousarray(v) for n, v in a.items()}

    nc = bacc.Bacc("TRN2", target_bir_lowering=False, num_devices=1)
    d = {n: nc.dram_tensor(f"in_{n}", v.shape, mybir.dt.from_np(v.dtype), kind="ExternalInput").ap() for n, v in a.items()}
    d["out"] = nc.dram_tensor("out", (B, C, HW), F32, kind="ExternalOutput").ap()
    program(nc, d)
    r = run(nc, [{f"in_{n}": v for n, v in a.items()}], core_ids=[0])
    return r.results[0]["out"].reshape(B, C, H, W)
```
